# Optimizing a Trainium2 kernel written in Bass

```python
import numpy as np
import jax
import jax.numpy as jnp

def _softmax(x, axis=-1):
    return jax.nn.softmax(x, axis=axis)

def _gelu(x):
    return jax.nn.gelu(x, approximate=True)

def _silu(x):
    return jax.nn.silu(x)

def _sigmoid(x):
    return jax.nn.sigmoid(x)

def _layernorm(x, axis=-1, eps=1e-05):
    m = jnp.mean(x, axis=axis, keepdims=True)
    v = jnp.var(x, axis=axis, keepdims=True)
    return (x - m) / jnp.sqrt(v + eps)

def _scatter_add(tgt, idx, src, axis=0):
    return tgt.at[idx].add(src)

def _segment_sum(src, seg, n):
    return jax.ops.segment_sum(src, seg, n)
kernel_name = 'mk_decoder_postln_d1_seqx_r4_543bbf'

def setup_inputs(seed: int=0):
    np.random.seed(seed)
    _w = jnp.asarray

    def _rec_inputs():
        import jax
        import jax.numpy as jnp
        _rk = jax.random.key(seed)
        x = 7.22e-05 + 1 * jax.random.normal(jax.random.fold_in(_rk, 1), (16, 256, 256), jnp.float32)
        _lenS = 256 - jax.random.randint(jax.random.fold_in(_rk, 7), (16,), 0, max(1, 256 // 4) + 1, jnp.int32)
        _lenS2 = 120 - jax.random.randint(jax.random.fold_in(_rk, 8), (16,), 0, max(1, 120 // 4) + 1, jnp.int32)
        _ctx_1024P = jax.random.normal(jax.random.fold_in(_rk, 11), (16, 16, 256), jnp.float32)
        _ctx_1024c = jax.random.dirichlet(jax.random.fold_in(_rk, 511), 0.3 * jnp.ones((16,), jnp.float32), (16, 120))
        _ctx_1024t = jnp.einsum('bsk,bkd->bsd', _ctx_1024c, _ctx_1024P)
        _ctx_1024t = _ctx_1024t * jax.lax.rsqrt(jnp.mean(jnp.square(_ctx_1024t)) + 1e-12) * 0.953939
        ctx_1024 = 4.13588e-05 + 0.999923 * (_ctx_1024t + 0.3 * jax.random.normal(jax.random.fold_in(_rk, 611), (16, 120, 256), jnp.float32))
        return (x, ctx_1024)
    x, ctx_1024 = _rec_inputs()

    def _L0_attn_setup():
        import jax, jax.numpy as jnp
        import numpy as np
        D = 256
        H = 16
        HD = D // H
        K = 4
        I = int(D * 2.7)
        B, T = (2, 512)
        EPS = 1e-06
        GATE_BIAS = 4.0

        def _rmsnorm(x, w):
            return x * jax.lax.rsqrt(jnp.mean(x * x, axis=-1, keepdims=True) + EPS) * w

        def _causal_depthwise_conv(x, conv_w, conv_b):
            xt = jnp.transpose(x, (0, 2, 1))
            y = jax.lax.conv_general_dilated(xt, conv_w[:, None, :], window_strides=(1,), padding=[(K - 1, 0)], feature_group_count=D, dimension_numbers=('NCH', 'OIH', 'NCH'))
            y = jnp.transpose(y, (0, 2, 1)) + conv_b
            return jax.nn.silu(y)

        def _l2norm(x):
            return x * jax.lax.rsqrt(jnp.sum(x * x, axis=-1, keepdims=True) + EPS)

        def _gated_delta_rule(xc, wq, wk, wv, wb, wa):
            b, t = (xc.shape[0], xc.shape[1])
            q = _l2norm((xc @ wq).reshape(b, t, H, HD))
            k = _l2norm((xc @ wk).reshape(b, t, H, HD))
            v = (xc @ wv).reshape(b, t, H, HD)
            beta = jax.nn.sigmoid(xc @ wb)
            alpha = jax.nn.sigmoid(xc @ wa + GATE_BIAS)
            qt = jnp.moveaxis(q, 1, 0)
            kt = jnp.moveaxis(k, 1, 0)
            vt = jnp.moveaxis(v, 1, 0)
            bt = jnp.moveaxis(beta, 1, 0)
            at = jnp.moveaxis(alpha, 1, 0)
            S0 = jnp.zeros((b, H, HD, HD), xc.dtype)

            def step(S, inp):
                q_, k_, v_, b_, a_ = inp
                S = a_[..., None, None] * S
                pred = jnp.einsum('bhkv,bhk->bhv', S, k_)
                S = S + k_[..., :, None] * (b_[..., None] * (v_ - pred))[..., None, :]
                o = jnp.einsum('bhkv,bhk->bhv', S, q_)
                return (S, o)
            _, o = jax.lax.scan(step, S0, (qt, kt, vt, bt, at))
            return jnp.moveaxis(o, 1, 0).reshape(b, t, D)
        key = jax.random.key(seed)
        ks = jax.random.split(key, 16)
        s = D ** (-0.5)
        return {'x': jax.random.normal(ks[0], (B, T, D), jnp.float32), 'norm1_w': jnp.ones((D,), jnp.float32), 'norm2_w': jnp.ones((D,), jnp.float32), 'conv_w': jax.random.normal(ks[1], (D, K), jnp.float32) * 0.2, 'conv_b': jnp.zeros((D,), jnp.float32), 'wq': jax.random.normal(ks[2], (D, D), jnp.float32) * s, 'wk': jax.random.normal(ks[3], (D, D), jnp.float32) * s, 'wv': jax.random.normal(ks[4], (D, D), jnp.float32) * s, 'wb': jax.random.normal(ks[5], (D, H), jnp.float32) * s, 'wa': jax.random.normal(ks[6], (D, H), jnp.float32) * s, 'wo': jax.random.normal(ks[7], (D, D), jnp.float32) * s, 'wg': jax.random.normal(ks[8], (D, I), jnp.float32) * s, 'wu': jax.random.normal(ks[9], (D, I), jnp.float32) * s, 'wd': jax.random.normal(ks[10], (I, D), jnp.float32) * I ** (-0.5)}
    _L0_attn_all = _L0_attn_setup()
    _L0_attn_in = {k: v for k, v in _L0_attn_all.items() if k in ('norm1_w', 'norm2_w', 'conv_w', 'conv_b', 'wq', 'wk', 'wv', 'wb', 'wa', 'wo', 'wg', 'wu', 'wd')}
    del _L0_attn_all

    def _L0_xattn_setup():
        import jax, jax.numpy as jnp
        import numpy as np
        import math
        H = 16
        D_MODEL = 256
        D_K = D_MODEL // H
        key = jax.random.key(seed)
        ks = jax.random.split(key, 11)
        B, S, D = (4, 512, D_MODEL)
        scale = 1.0 / math.sqrt(D)
        inp = {'query': jax.random.normal(ks[0], (B, S, D), jnp.float32), 'key': jax.random.normal(ks[1], (B, S, D), jnp.float32), 'value': jax.random.normal(ks[2], (B, S, D), jnp.float32), 'Wq': jax.random.normal(ks[3], (D, D), jnp.float32) * scale, 'bq': jnp.zeros((D,), jnp.float32), 'Wk': jax.random.normal(ks[4], (D, D), jnp.float32) * scale, 'bk': jnp.zeros((D,), jnp.float32), 'Wv': jax.random.normal(ks[5], (D, D), jnp.float32) * scale, 'bv': jnp.zeros((D,), jnp.float32), 'Wo': jax.random.normal(ks[6], (D, D), jnp.float32) * scale, 'bo': jnp.zeros((D,), jnp.float32)}
        return inp
    _L0_xattn_all = _L0_xattn_setup()
    _L0_xattn_in = {k: v for k, v in _L0_xattn_all.items() if k in ('Wq', 'bq', 'Wk', 'bk', 'Wv', 'bv', 'Wo', 'bo')}
    del _L0_xattn_all

    def _L0_ffn_setup():
        import jax, jax.numpy as jnp
        import numpy as np
        B, S, D, E = (4, 512, 256, 8)
        key = jax.random.key(seed)
        ks = jax.random.split(key, 5)
        s = 0.02
        return {'hidden_states': jax.random.normal(ks[0], (B, S, D), dtype=jnp.float32), 'Wr': jax.random.normal(ks[1], (D, E), dtype=jnp.float32) * s, 'br': jnp.zeros((E,), dtype=jnp.float32), 'W1': jax.random.normal(ks[2], (E, D, 4 * D), dtype=jnp.float32) * s, 'b1': jnp.zeros((E, 4 * D), dtype=jnp.float32), 'W2': jax.random.normal(ks[3], (E, 4 * D, 2 * D), dtype=jnp.float32) * s, 'b2': jnp.zeros((E, 2 * D), dtype=jnp.float32), 'W3': jax.random.normal(ks[4], (E, 2 * D, D), dtype=jnp.float32) * s, 'b3': jnp.zeros((E, D), dtype=jnp.float32)}
    _L0_ffn_all = _L0_ffn_setup()
    _L0_ffn_in = {k: v for k, v in _L0_ffn_all.items() if k in ('Wr', 'br', 'W1', 'b1', 'W2', 'b2', 'W3', 'b3')}
    del _L0_ffn_all
    return {'x': x, 'ctx_1024': ctx_1024, 'L0_attn_norm1_w': _L0_attn_in['norm1_w'], 'L0_attn_norm2_w': _L0_attn_in['norm2_w'], 'L0_attn_conv_w': _L0_attn_in['conv_w'], 'L0_attn_conv_b': _L0_attn_in['conv_b'], 'L0_attn_wq': _L0_attn_in['wq'], 'L0_attn_wk': _L0_attn_in['wk'], 'L0_attn_wv': _L0_attn_in['wv'], 'L0_attn_wb': _L0_attn_in['wb'], 'L0_attn_wa': _L0_attn_in['wa'], 'L0_attn_wo': _L0_attn_in['wo'], 'L0_attn_wg': _L0_attn_in['wg'], 'L0_attn_wu': _L0_attn_in['wu'], 'L0_attn_wd': _L0_attn_in['wd'], 'L0_xattn_Wq': _L0_xattn_in['Wq'], 'L0_xattn_bq': _L0_xattn_in['bq'], 'L0_xattn_Wk': _L0_xattn_in['Wk'], 'L0_xattn_bk': _L0_xattn_in['bk'], 'L0_xattn_Wv': _L0_xattn_in['Wv'], 'L0_xattn_bv': _L0_xattn_in['bv'], 'L0_xattn_Wo': _L0_xattn_in['Wo'], 'L0_xattn_bo': _L0_xattn_in['bo'], 'L0_ffn_Wr': _L0_ffn_in['Wr'], 'L0_ffn_br': _L0_ffn_in['br'], 'L0_ffn_W1': _L0_ffn_in['W1'], 'L0_ffn_b1': _L0_ffn_in['b1'], 'L0_ffn_W2': _L0_ffn_in['W2'], 'L0_ffn_b2': _L0_ffn_in['b2'], 'L0_ffn_W3': _L0_ffn_in['W3'], 'L0_ffn_b3': _L0_ffn_in['b3']}

def reference(x, ctx_1024, L0_attn_norm1_w, L0_attn_norm2_w, L0_attn_conv_w, L0_attn_conv_b, L0_attn_wq, L0_attn_wk, L0_attn_wv, L0_attn_wb, L0_attn_wa, L0_attn_wo, L0_attn_wg, L0_attn_wu, L0_attn_wd, L0_xattn_Wq, L0_xattn_bq, L0_xattn_Wk, L0_xattn_bk, L0_xattn_Wv, L0_xattn_bv, L0_xattn_Wo, L0_xattn_bo, L0_ffn_Wr, L0_ffn_br, L0_ffn_W1, L0_ffn_b1, L0_ffn_W2, L0_ffn_b2, L0_ffn_W3, L0_ffn_b3):
    import jax
    import jax.numpy as jnp

    def _L0_attn_ref(x, norm1_w, norm2_w, conv_w, conv_b, wq, wk, wv, wb, wa, wo, wg, wu, wd):
        import jax, jax.numpy as jnp
        import numpy as np
        D = 256
        H = 16
        HD = D // H
        K = 4
        I = int(D * 2.7)
        B, T = (2, 512)
        EPS = 1e-06
        GATE_BIAS = 4.0

        def _rmsnorm(x, w):
            return x * jax.lax.rsqrt(jnp.mean(x * x, axis=-1, keepdims=True) + EPS) * w

        def _causal_depthwise_conv(x, conv_w, conv_b):
            xt = jnp.transpose(x, (0, 2, 1))
            y = jax.lax.conv_general_dilated(xt, conv_w[:, None, :], window_strides=(1,), padding=[(K - 1, 0)], feature_group_count=D, dimension_numbers=('NCH', 'OIH', 'NCH'))
            y = jnp.transpose(y, (0, 2, 1)) + conv_b
            return jax.nn.silu(y)

        def _l2norm(x):
            return x * jax.lax.rsqrt(jnp.sum(x * x, axis=-1, keepdims=True) + EPS)

        def _gated_delta_rule(xc, wq, wk, wv, wb, wa):
            b, t = (xc.shape[0], xc.shape[1])
            q = _l2norm((xc @ wq).reshape(b, t, H, HD))
            k = _l2norm((xc @ wk).reshape(b, t, H, HD))
            v = (xc @ wv).reshape(b, t, H, HD)
            beta = jax.nn.sigmoid(xc @ wb)
            alpha = jax.nn.sigmoid(xc @ wa + GATE_BIAS)
            qt = jnp.moveaxis(q, 1, 0)
            kt = jnp.moveaxis(k, 1, 0)
            vt = jnp.moveaxis(v, 1, 0)
            bt = jnp.moveaxis(beta, 1, 0)
            at = jnp.moveaxis(alpha, 1, 0)
            S0 = jnp.zeros((b, H, HD, HD), xc.dtype)

            def step(S, inp):
                q_, k_, v_, b_, a_ = inp
                S = a_[..., None, None] * S
                pred = jnp.einsum('bhkv,bhk->bhv', S, k_)
                S = S + k_[..., :, None] * (b_[..., None] * (v_ - pred))[..., None, :]
                o = jnp.einsum('bhkv,bhk->bhv', S, q_)
                return (S, o)
            _, o = jax.lax.scan(step, S0, (qt, kt, vt, bt, at))
            return jnp.moveaxis(o, 1, 0).reshape(b, t, D)
        residual = x
        xn = _rmsnorm(x, norm1_w)
        xc = _causal_depthwise_conv(xn, conv_w, conv_b)
        mixer_out = _gated_delta_rule(xc, wq, wk, wv, wb, wa) @ wo
        h = residual + mixer_out
        hn = _rmsnorm(h, norm2_w)
        ffn = jax.nn.silu(hn @ wg) * (hn @ wu) @ wd
        return h + ffn

    def _L0_xattn_ref(query, key, value, Wq, bq, Wk, bk, Wv, bv, Wo, bo):
        import jax, jax.numpy as jnp
        import numpy as np
        import math
        H = 16
        D_MODEL = 256
        D_K = D_MODEL // H
        B, S, D = query.shape

        def proj(x, W, b):
            return (x @ W + b).reshape(B, -1, H, D_K).transpose(0, 2, 1, 3)
        q = proj(query, Wq, bq)
        k = proj(key, Wk, bk)
        v = proj(value, Wv, bv)
        scores = jnp.einsum('bhqd,bhkd->bhqk', q, k) / math.sqrt(D_K)
        p_attn = jax.nn.softmax(scores, axis=-1)
        x = jnp.einsum('bhqk,bhkd->bhqd', p_attn, v)
        x = x.transpose(0, 2, 1, 3).reshape(B, -1, H * D_K)
        return x @ Wo + bo

    def _L0_ffn_ref(hidden_states, Wr, br, W1, b1, W2, b2, W3, b3):
        import jax, jax.numpy as jnp
        import numpy as np
        B, S, D, E = (4, 512, 256, 8)
        b, s, d = hidden_states.shape
        num_experts = Wr.shape[1]
        x = hidden_states.reshape(-1, d)
        router_logits = x @ Wr + br
        expert_mask = jax.nn.one_hot(jnp.argmax(router_logits, axis=-1), num_experts, dtype=x.dtype)
        out = jnp.zeros_like(x)
        for e in range(num_experts):
            h = jax.nn.gelu(x @ W1[e] + b1[e], approximate=False)
            h = jax.nn.gelu(h @ W2[e] + b2[e], approximate=False)
            y = h @ W3[e] + b3[e]
            out = out + expert_mask[:, e:e + 1] * y
        return out.reshape(b, s, d)
    x = _layernorm(x + _L0_attn_ref(x, L0_attn_norm1_w, L0_attn_norm2_w, L0_attn_conv_w, L0_attn_conv_b, L0_attn_wq, L0_attn_wk, L0_attn_wv, L0_attn_wb, L0_attn_wa, L0_attn_wo, L0_attn_wg, L0_attn_wu, L0_attn_wd), axis=-1)
    x = _layernorm(x + _L0_xattn_ref(x, ctx_1024, ctx_1024, L0_xattn_Wq, L0_xattn_bq, L0_xattn_Wk, L0_xattn_bk, L0_xattn_Wv, L0_xattn_bv, L0_xattn_Wo, L0_xattn_bo), axis=-1)
    x = _layernorm(x + _L0_ffn_ref(x, L0_ffn_Wr, L0_ffn_br, L0_ffn_W1, L0_ffn_b1, L0_ffn_W2, L0_ffn_b2, L0_ffn_W3, L0_ffn_b3), axis=-1)
    return x

_drawn_inputs = setup_inputs


def setup_inputs(seed=0):
    import zlib

    import numpy as np

    out = dict(_drawn_inputs(seed))
    spreads = {'L0_attn_norm1_w': (1.0, 0.2),
     'L0_attn_norm2_w': (1.0, 0.2),
     'L0_attn_conv_b': (0.0, 0.1),
     'L0_xattn_bq': (0.0, 0.278),
     'L0_xattn_bk': (0.0, 0.8),
     'L0_xattn_bv': (0.0, 0.1),
     'L0_xattn_bo': (0.0, 0.1),
     'L0_ffn_br': (0.0, 0.1),
     'L0_ffn_b1': (0.0, 0.8),
     'L0_ffn_b2': (0.0, 0.343),
     'L0_ffn_b3': (0.0, 0.1)}
    factors = {'L0_attn_wb': 5.137, 'L0_attn_wa': 8.0}
    for name, (base, spread) in spreads.items():
        noise = np.random.default_rng([zlib.crc32(name.encode()), seed]).standard_normal(out[name].shape)
        drawn = base * np.exp(spread * noise) if base else spread * noise
        out[name] = jnp.asarray(drawn.astype(out[name].dtype))
    for name, factor in factors.items():
        out[name] = (out[name] * factor).astype(out[name].dtype)
    return out
```

```python
from contextlib import ExitStack

import concourse.bass as bass
from concourse import mybir

F32 = mybir.dt.float32
I32 = mybir.dt.int32
U32 = mybir.dt.uint32
ALU = mybir.AluOpType
ACT = mybir.ActivationFunctionType
AX = mybir.AxisListType.X

P = 128
NB, T, D = 16, 256, 256
G = D // P
J = T // P
H, HD = 16, 16
KC = 4
INNER = int(D * 2.7)
IC = -(-INNER // P)
ILAST = INNER - (IC - 1) * P
CTX = 120
NE, F1, F2 = 8, 4 * D, 2 * D
NTOK = NB * T
TILES = NTOK // P
SLOTS = (NTOK + NE * (P - 1)) // P
XROW = D + 4
WBUFS = 3
WSIZES = (G * F1, F1 // P * F2, F2 // P * D, F1, F2, D)
WPARTS = tuple(sum(WSIZES[:i]) for i in range(len(WSIZES)))
WROW, WDMAS = sum(WSIZES), len(WSIZES)
RMS_EPS, LN_EPS, GATE_BIAS = 1e-6, 1e-5, 4.0


def pipeline(eng, steps, body):
    body((0, 0, 0), None)
    body((1, 1, 0), (0, 0, 0))
    with eng.Fori(0, (steps - 2) // 2) as i:
        body((i * 2 + 2, 0, i + 1), (i * 2 + 1, 1, i))
        body((i * 2 + 3, 1, i + 1), (i * 2 + 2, 0, i + 1))
    last = steps - 1
    if steps % 2:
        body((last, last % 2, last // 2), (last - 1, (last - 1) % 2, (last - 1) // 2))
    body(None, (last, last % 2, last // 2))


def since(n, k):
    return not isinstance(n, int) or n >= k


def column(vec):
    return vec.rearrange("(g p) -> p g", p=P)


def row(vec, parts=P):
    return vec.rearrange("(o n) -> o n", o=1).to_broadcast([parts, vec.shape[0]])


def constants(nc, sb, sem, k):
    k["ident"] = sb("ident", [P, P])
    k["exponent"] = sb("exponent", [P, T])
    k["eps"] = sb("eps", [P, 2, J])
    ident = k["ident"]
    with ExitStack() as ctx:
        empty = ctx.enter_context(nc.sbuf_tensor("empty_rows", [P, XROW], F32))
        zeroed, ident_made, empty_made, empty_out = (sem(n) for n in ("zeroed", "ident_made", "empty_made", "empty_out"))
        block = ctx.enter_context(nc.Block())

        @block.gpsimd
        def _(pool):
            nc.gpsimd.memset(ident[:], 0.0).then_inc(zeroed, 1)
            nc.gpsimd.memset(empty[:], 0.0).then_inc(zeroed, 1)
            nc.gpsimd.memset(k["exponent"][:], -0.5).then_inc(zeroed, 1)
            nc.gpsimd.memset(k["eps"][:, 0], D * RMS_EPS).then_inc(zeroed, 1)
            nc.gpsimd.memset(k["eps"][:, 1], LN_EPS).then_inc(zeroed, 1)
            pool.wait_ge(zeroed, 5)
            nc.gpsimd.affine_select(out=ident[:], in_=ident[:], compare_op=ALU.not_equal, fill=1.0, base=0,
                                    pattern=[[-1, P]], channel_multiplier=1).then_inc(ident_made, 1)
            nc.gpsimd.iota(empty[:, D:D + 1].bitcast(I32), [[0, 1]], base=NTOK, channel_multiplier=0).then_inc(empty_made, 1)
            pool.wait_ge(ident_made, 1)

        @block.sync
        def _(sp):
            sp.wait_ge(empty_made, 1)
            for i in range(SLOTS + 1):
                sp.dma_start(k["routed"][i * P:(i + 1) * P, :], empty[:]).then_inc(empty_out, 16)
            sp.wait_ge(empty_out, 16 * (SLOTS + 1))


def front(nc, sem, w, k):
    ident = k["ident"]
    with ExitStack() as ctx:
        sb = lambda n, s, d=F32: ctx.enter_context(nc.sbuf_tensor("f_" + n, s, d))
        ps = lambda n, s: ctx.enter_context(nc.psum_tensor("f_" + n, s, F32))
        wqkv = sb("wqkv", [P, 3, G, D])
        wba = sb("wba", [P, G, 48])
        n1 = sb("n1", [P, G])
        cw = sb("cw", [P, G, KC])
        cb = sb("cb", [P, G])
        ba_bias = sb("ba_bias", [48, 1])
        xt = sb("xt", [P, 2, J, D])
        sq = sb("sq", [P, 2, J, D])
        ss = sb("ss", [P, 2, J])
        ms = sb("ms", [P, 2, J])
        rstd = sb("rstd", [P, 2, J])
        xn = sb("xn", [P, 2, J, D])
        xT = sb("xT", [P, 2, G, T + KC - 1])
        acc = sb("acc", [P, 2, G, T])
        sg = sb("sg", [P, 2, G, T])
        xc = sb("xc", [P, 2, G, T])
        st = sb("st", [P, 2, 3, G, T])
        bst = sb("bst", [48, 2, T])
        pT = ps("pT", [P, 2, G, T])
        pp = ps("pp", [P, 4, G, T])
        w_in, padded, n1_scaled = sem("f_w_in"), sem("f_padded"), sem("f_n1_scaled")
        x_in = [sem("f_x_in0"), sem("f_x_in1")]
        out = [sem("f_out0"), sem("f_out1")]
        ss_done, ms_done, rstd_done, xn_done, T_done, xT_done, conv_done, sig_done, xc_done, proj_done, evac_done = (
            sem("f_" + n) for n in ("ss_done", "ms_done", "rstd_done", "xn_done", "T_done", "xT_done", "conv_done", "sig_done",
                                    "xc_done", "proj_done", "evac_done"))
        NW = 3 + 2 + 4
        block = ctx.enter_context(nc.Block())

        @block.sync
        def _(sp):
            sp.wait_ge(padded, 3)
            with nc.allow_non_contiguous_dma(reason="small vectors"):
                for i, name in enumerate(("L0_attn_wq", "L0_attn_wk", "L0_attn_wv")):
                    sp.dma_start(wqkv[:, i], w[name].rearrange("(g p) n -> p g n", p=P)).then_inc(w_in, 16)
                sp.dma_start(wba[:, :, 0:H], w["L0_attn_wb"].rearrange("(g p) n -> p g n", p=P)).then_inc(w_in, 16)
                sp.dma_start(wba[:, :, 32:32 + H], w["L0_attn_wa"].rearrange("(g p) n -> p g n", p=P)).then_inc(w_in, 16)
                sp.dma_start(n1[:], column(w["L0_attn_norm1_w"])).then_inc(w_in, 16)
                sp.dma_start(cb[:], column(w["L0_attn_conv_b"])).then_inc(w_in, 16)
                for g in range(G):
                    sp.dma_start(cw[:, g], w["L0_attn_conv_w"][g * P:(g + 1) * P, :]).then_inc(w_in, 16)

            def load(a, b):
                if a:
                    n, s, m = a
                    if since(n, 2):
                        sp.wait_ge(xn_done, (n - 1) * J)
                    sp.dma_start(xt[:, s], w["x"][bass.ds(n, 1)].rearrange("o (j p) f -> p (o j) f", p=P)).then_inc(x_in[s], 16)

            pipeline(sp, NB, load)
            for s in range(2):
                sp.wait_ge(out[s], 16 * 5 * (NB // 2))

        @block.gpsimd
        def _(pool):
            nc.gpsimd.memset(xT[:], 0.0).then_inc(padded, 1)
            nc.gpsimd.memset(wba[:], 0.0).then_inc(padded, 1)
            nc.gpsimd.memset(ba_bias[:], 0.0).then_inc(padded, 1)
            pool.wait_ge(padded, 3)
            nc.gpsimd.memset(ba_bias[32:48, :], GATE_BIAS).then_inc(padded, 1)
            pool.wait_ge(w_in, 16 * NW)

            def silu(a, b):
                if a:
                    n, s, m = a
                    pool.wait_ge(ss_done, (n + 1) * J)
                    nc.gpsimd.tensor_tensor(ms[:, s], ss[:, s], k["eps"][:, 0], ALU.add).then_inc(ms_done, 1)
                    pool.wait_ge(ms_done, n + 1)
                    nc.gpsimd.tensor_tensor(rstd[:, s], ms[:, s], k["exponent"][:, 0:J], ALU.pow).then_inc(rstd_done, 1)
                if b:
                    n, s, m = b
                    if since(n, 2):
                        pool.wait_ge(proj_done, (n - 1) * 4)
                    pool.wait_ge(sig_done, n + 1)
                    nc.gpsimd.tensor_tensor(xc[:, s], acc[:, s], sg[:, s], ALU.mult).then_inc(xc_done, 1)

            pipeline(pool, NB, silu)

        @block.vector
        def _(dve):
            dve.wait_ge(w_in, 16 * NW)
            nc.vector.tensor_scalar(n1[:], n1[:], float(D) ** 0.5, None, ALU.mult).then_inc(n1_scaled, 1)
            dve.wait_ge(padded, 4)

            def step(a, b):
                if a:
                    n, s, m = a
                    dve.wait_ge(rstd_done, n + 1)
                    for j in range(J):
                        nc.vector.tensor_scalar(xn[:, s, j], xt[:, s, j], rstd[:, s, j:j + 1], None, ALU.mult).then_inc(xn_done, 1)
                if b:
                    n, s, m = b
                    dve.wait_ge(xT_done, (n + 1) * G)
                    if since(n, 2):
                        dve.wait_ge(xc_done, n - 1)
                    for c in range(KC):
                        for g in range(G):
                            src = xT[:, s, g, c:c + T]
                            if c == 0:
                                ins = nc.vector.tensor_scalar(acc[:, s, g], src, cw[:, g, 0:1], cb[:, g:g + 1], ALU.mult, ALU.add)
                            else:
                                dve.wait_ge(conv_done, n * (KC * G) + (c - 1) * G + g + 1)
                                ins = nc.vector.scalar_tensor_tensor(acc[:, s, g], src, cw[:, g, c:c + 1], acc[:, s, g], ALU.mult, ALU.add)
                            ins.then_inc(conv_done, 1)

            pipeline(dve, NB, step)

        @block.scalar
        def _(act):
            act.wait_ge(n1_scaled, 1)
            act.wait_ge(padded, 4)

            def step(a, b):
                if a:
                    n, s, m = a
                    act.wait_ge(x_in[s], m * 16 + 16)
                    for j in range(J):
                        nc.scalar.activation(sq[:, s, j], xt[:, s, j], ACT.Square, accum_out=ss[:, s, j:j + 1]).then_inc(ss_done, 1)
                if b:
                    n, s, m = b
                    act.wait_ge(conv_done, (n + 1) * (KC * G))
                    nc.scalar.activation(sg[:, s], acc[:, s], ACT.Sigmoid).then_inc(sig_done, 1)
                if a:
                    n, s, m = a
                    act.wait_ge(T_done, n + 1)
                    for g in range(G):
                        nc.scalar.activation(xT[:, s, g, KC - 1:], pT[:, s, g], ACT.Copy, scale=n1[:, g:g + 1]).then_inc(xT_done, 1)
                if b:
                    n, s, m = b
                    if since(n, 2):
                        act.wait_ge(out[s], m * 80)
                    for i in range(3):
                        act.wait_ge(proj_done, n * 4 + i + 1)
                        nc.scalar.activation(st[:, s, i], pp[:, i], ACT.Copy).then_inc(evac_done, 1)
                        act.wait_ge(evac_done, n * 4 + i + 1)
                        act.dma_start(k["qkv"][i, bass.ds(n, 1)].rearrange("o (g p) t -> p (o g) t", p=P), st[:, s, i]).then_inc(out[s], 16)
                    act.wait_ge(proj_done, n * 4 + 4)
                    nc.scalar.activation(bst[:, s], pp[0:48, 3, 0], ACT.Sigmoid, bias=ba_bias[:, 0:1]).then_inc(evac_done, 1)
                    act.wait_ge(evac_done, n * 4 + 4)
                    for i in range(2):
                        act.dma_start(k["gates"][i, bass.ds(n, 1)].rearrange("o h t -> h (o t)"), bst[32 * i:32 * i + H, s]).then_inc(out[s], 16)

            pipeline(act, NB, step)

        @block.tensor
        def _(pe):
            pe.wait_ge(w_in, 16 * NW)

            def step(a, b):
                if a:
                    n, s, m = a
                    pe.wait_ge(xn_done, (n + 1) * J)
                    if since(n, 2):
                        pe.wait_ge(xT_done, (n - 1) * G)
                    for j in range(J):
                        for g in range(G):
                            ins = nc.tensor.transpose(pT[:, s, g, j * P:(j + 1) * P], xn[:, s, j, g * P:(g + 1) * P], ident[:])
                    ins.then_inc(T_done, 1)
                if b:
                    n, s, m = b
                    pe.wait_ge(xc_done, n + 1)
                    for i in range(4):
                        if since(n, 1):
                            pe.wait_ge(evac_done, (n - 1) * 4 + i + 1)
                        if i < 3:
                            for go in range(G):
                                for g in range(G):
                                    ins = nc.tensor.matmul(pp[:, i, go], wqkv[:, i, g, go * P:(go + 1) * P], xc[:, s, g],
                                                           start=(g == 0), stop=(g == G - 1))
                        else:
                            for g in range(G):
                                ins = nc.tensor.matmul(pp[0:48, i, 0], wba[:, g], xc[:, s, g], start=(g == 0), stop=(g == G - 1))
                        ins.then_inc(proj_done, 1)

            pipeline(pe, NB, step)


def delta_rule(nc, sem, w, k):
    R = 8
    Q = 4
    with ExitStack() as ctx:
        sb = lambda n, s, d=F32: ctx.enter_context(nc.sbuf_tensor("s_" + n, s, d))
        raw = sb("raw", [P, 2, HD, T])
        sq = sb("sq", [P, HD, T])
        ss = sb("ss", [P, T])
        ms = sb("ms", [P, T])
        rn = sb("rn", [P, T])
        kq = [sb("q", [P, 2, T, HD]), sb("k", [P, 2, T, HD])]
        vb = sb("vb", [P, 2, T, HD])
        o = sb("o", [P, 2, HD, T])
        gate = sb("gate", [P, 2, 2, T])
        nab = sb("nab", [P, 2, T])
        S = sb("S", [P, 2, R, HD, HD])
        outer = sb("outer", [P, 2, HD, HD])
        sk = sb("sk", [P, 2, HD, HD])
        pred = sb("pred", [P, 2, HD])
        wv = sb("wv", [P, 2, HD])
        so = sq[:].rearrange("p d t -> p (d t)")[:, 0:2 * Q * HD * HD].rearrange("p (h t v d) -> p h t v d", h=2, t=Q, v=HD)
        gate_in, sq_done, ss_done, ms_done, rn_done, norm_done, nab_done, w_done, outer_done, S_done, sk_done, pred_done = (
            sem("s_" + n) for n in ("gate_in", "sq_done", "ss_done", "ms_done", "rn_done", "norm_done", "nab_done", "w_done",
                                    "outer_done", "S_done", "sk_done", "pred_done"))
        S_read, o_fold, o_done = ([sem(f"s_{n}{h}") for h in range(2)] for n in ("S_read", "o_fold", "o_done"))
        o_out = sem("s_o_out")
        raw_in = [sem("s_raw_in0"), sem("s_raw_in1")]
        ITEMS = [(h, i) for h in range(2) for i in (1, 2, 0)]
        block = ctx.enter_context(nc.Block())
        chains = lambda x, h: x[h * 8:(h + 1) * 8]

        @block.sync
        def _(sp):
            for h in range(2):
                for i in range(2):
                    sp.dma_start(gate[:, h, i], chains(k["gates"][i], h).rearrange("b h t -> (b h) t")).then_inc(gate_in, 16)
            for m, (h, i) in enumerate(ITEMS):
                if m >= 2:
                    sp.wait_ge(norm_done, m - 1)
                sp.dma_start(raw[:, m % 2], chains(k["qkv"][i], h).rearrange("b (h d) t -> (b h) d t", h=H)).then_inc(raw_in[m % 2], 16)
            for h in range(2):
                sp.wait_ge(o_done[h], 1 + T // Q)
                sp.dma_start(chains(k["o"], h).rearrange("b (h d) t -> (b h) d t", h=H), o[:, h]).then_inc(o_out, 16)
            sp.wait_ge(o_out, 32)

        @block.scalar
        def _(act):
            c = 0
            for m, (h, i) in enumerate(ITEMS):
                if i == 2:
                    continue
                act.wait_ge(raw_in[m % 2], 16 * (m // 2 + 1))
                if c >= 1:
                    act.wait_ge(ss_done, c)
                nc.scalar.activation(sq[:], raw[:, m % 2], ACT.Square).then_inc(sq_done, 1)
                c += 1

        @block.vector
        def _(dve):
            nc.vector.memset(S[:, :, R - 1], 0.0).then_inc(S_done, 2)
            dve.wait_ge(gate_in, 64)
            nc.vector.scalar_tensor_tensor(nab[:], gate[:, :, 0], -1.0, gate[:, :, 1], ALU.mult, ALU.mult).then_inc(nab_done, 1)
            c = 0
            for m, (h, i) in enumerate(ITEMS):
                by_token = raw[:, m % 2].rearrange("p d t -> p t d")
                if i == 2:
                    dve.wait_ge(raw_in[m % 2], 16 * (m // 2 + 1))
                    scale, dst = gate[:, h, 0], vb[:, h]
                else:
                    c += 1
                    dve.wait_ge(sq_done, c)
                    if c >= 2:
                        dve.wait_ge(norm_done, m)
                    nc.vector.tensor_reduce(ss[:], sq[:].rearrange("p d t -> p t d"), AX, ALU.add).then_inc(ss_done, 1)
                    dve.wait_ge(ss_done, c)
                    dve.wait_ge(rn_done, c)
                    scale, dst = rn[:], kq[i][:, h]
                nc.vector.tensor_tensor(dst, by_token, scale.rearrange("p (t o) -> p t o", o=1).to_broadcast([P, T, HD]),
                                        ALU.mult).then_inc(norm_done, 1)
            dve.wait_ge(norm_done, len(ITEMS))
            dve.wait_ge(nab_done, 1)
            with dve.Fori(0, T // R) as i:
                for u in range(R):
                    t = i * R + u
                    at = lambda x, h: x[:, h, bass.ds(t, 1)]
                    n = lambda h: t * 2 + h + 1
                    for h in range(2):
                        dve.wait_ge(S_done, n(h))
                        nc.vector.tensor_tensor(sk[:, h], S[:, h, (u - 1) % R], at(kq[1], h).to_broadcast([P, HD, HD]),
                                                ALU.mult).then_inc(sk_done, 1)
                    for h in range(2):
                        dve.wait_ge(sk_done, n(h))
                        nc.vector.tensor_reduce(pred[:, h], sk[:, h], AX, ALU.add).then_inc(pred_done, 1)
                    for h in range(2):
                        dve.wait_ge(pred_done, n(h))
                        nc.vector.scalar_tensor_tensor(wv[:, h], pred[:, h], at(nab, h), at(vb, h).rearrange("p o v -> p (o v)"),
                                                       ALU.mult, ALU.add).then_inc(w_done, 1)
                    for h in range(2):
                        dve.wait_ge(w_done, n(h))
                        nc.vector.tensor_tensor(outer[:, h], wv[:, h].rearrange("p (v o) -> p v o", o=1).to_broadcast([P, HD, HD]),
                                                at(kq[1], h).to_broadcast([P, HD, HD]), ALU.mult).then_inc(outer_done, 1)
                    for h in range(2):
                        dve.wait_ge(outer_done, n(h))
                        if u % Q == 0:
                            dve.wait_ge(S_read[h], i * (R // Q) + u // Q + 1)
                        nc.vector.scalar_tensor_tensor(S[:, h, u], S[:, h, (u - 1) % R], gate[:, h, 1, bass.ds(t, 1)], outer[:, h],
                                                       ALU.mult, ALU.add).then_inc(S_done, 1)

        @block.gpsimd
        def _(pool):
            for h in range(2):
                pool.sem_inc(S_read[h], 2)
                pool.sem_inc(o_done[h], 1)
            for c in range(4):
                pool.wait_ge(ss_done, c + 1)
                nc.gpsimd.tensor_scalar(ms[:], ss[:], RMS_EPS, None, ALU.add).then_inc(ms_done, 1)
                pool.wait_ge(ms_done, c + 1)
                nc.gpsimd.tensor_tensor(rn[:], ms[:], k["exponent"][:], ALU.pow).then_inc(rn_done, 1)
            pool.wait_ge(norm_done, len(ITEMS))
            with pool.Fori(0, T // R) as i:
                for z in range(R // Q):
                    for h in range(2):
                        blk = i * (R // Q) + z
                        pool.wait_ge(S_done, i * (2 * R) + (2 + 2 * (z * Q + Q - 1) + h + 1))
                        pool.wait_ge(o_done[h], blk + 1)
                        q = kq[0][:, h, bass.ds(i * R + z * Q, Q)].rearrange("p t (o d) -> p t o d", o=1).to_broadcast([P, Q, HD, HD])
                        x = so[:, h]
                        nc.gpsimd.tensor_tensor(x, S[:, h, z * Q:(z + 1) * Q], q, ALU.mult).then_inc(S_read[h], 1)
                        pool.wait_ge(S_read[h], blk + 3)
                        for f, half in enumerate((8, 4, 2)):
                            nc.gpsimd.tensor_tensor(x[:, :, :, 0:half], x[:, :, :, 0:half], x[:, :, :, half:2 * half], ALU.add).then_inc(o_fold[h], 1)
                            pool.wait_ge(o_fold[h], blk * 3 + f + 1)
                        nc.gpsimd.tensor_tensor(o[:, h, :, bass.ds(i * R + z * Q, Q)].rearrange("p v t -> p t v"), x[:, :, :, 0], x[:, :, :, 1],
                                                ALU.add).then_inc(o_done[h], 1)


def mixer_ffn(nc, sem, w, k):
    ident = k["ident"]
    with ExitStack() as ctx:
        sb = lambda n, s, d=F32: ctx.enter_context(nc.sbuf_tensor("m_" + n, s, d))
        ps = lambda n, s: ctx.enter_context(nc.psum_tensor("m_" + n, s, F32))
        wo = sb("wo", [P, G, D])
        wg = sb("wg", [P, G, INNER])
        wu = sb("wu", [P, G, INNER])
        wd = sb("wd", [P, IC, D])
        n2 = sb("n2", [P, G])
        oT = sb("oT", [P, 2, G, T])
        xt = sb("xt", [P, 2, J, D])
        h = sb("h", [P, 2, J, D])
        xh = sb("xh", [P, 2, J, D])
        sq = sb("sq", [P, J, D])
        ss = sb("ss", [P, 2, J])
        ms = sb("ms", [P, 2, J])
        rstd = sb("rstd", [P, 2, J])
        hn = sb("hn", [P, 2, J, D])
        hT = sb("hT", [P, 2, G, T])
        gate = sb("gate", [P, 2, T])
        act_gu = sb("gu", [P, 2, IC, T])
        r = sb("r", [P, 2, J, D])
        st6 = sb("st6", [P, 2, J, 6])
        mv = sb("mv", [P, 2, J, 2])
        ve = sb("ve", [P, 2, J])
        rs = sb("rs", [P, 2, J])
        x1 = sb("x1", [P, 2, J, D])
        pm = ps("pm", [P, J, D])
        pT = ps("pT", [P, G, T])
        pgu = ps("pgu", [P, 2, 2, T])
        py = ps("py", [P, 2, J, D])
        w_in, n2_scaled, st_seen = sem("m_w_in"), sem("m_n2_scaled"), sem("m_st_seen")
        o_in, x_in, x1_out = ([sem(f"m_{n}{s}") for s in range(2)] for n in ("o_in", "x_in", "x1_out"))
        names = ("mix_done", "h_done", "xh_done", "ss_done", "ms_done", "rstd_done", "hn_done", "T_done", "hT_done", "gu_done",
                 "gate_done", "prod_done", "down_done", "r_done", "st_done", "mv_done", "ve_done", "rs_done", "x1_done")
        (mix_done, h_done, xh_done, ss_done, ms_done, rstd_done, hn_done, T_done, hT_done, gu_done, gate_done, prod_done,
         down_done, r_done, st_done, mv_done, ve_done, rs_done, x1_done) = (sem("m_" + n) for n in names)
        NW = 6
        width = lambda i: P if i < IC - 1 else ILAST
        block = ctx.enter_context(nc.Block())

        @block.sync
        def _(sp):
            with nc.allow_non_contiguous_dma(reason="small vectors"):
                sp.dma_start(wo[:], w["L0_attn_wo"].rearrange("(g p) n -> p g n", p=P)).then_inc(w_in, 16)
                sp.dma_start(n2[:], column(w["L0_attn_norm2_w"])).then_inc(w_in, 16)
                sp.dma_start(wg[:], w["L0_attn_wg"].rearrange("(g p) n -> p g n", p=P)).then_inc(w_in, 16)
                sp.dma_start(wu[:], w["L0_attn_wu"].rearrange("(g p) n -> p g n", p=P)).then_inc(w_in, 16)
                sp.dma_start(wd[:, 0:IC - 1], w["L0_attn_wd"][0:(IC - 1) * P, :].rearrange("(c p) n -> p c n", p=P)).then_inc(w_in, 16)
                sp.dma_start(wd[0:ILAST, IC - 1], w["L0_attn_wd"][(IC - 1) * P:INNER, :]).then_inc(w_in, 16)

            def load(a, b):
                if a:
                    n, s, m = a
                    if since(n, 2):
                        sp.wait_ge(mix_done, n - 1)
                        sp.wait_ge(h_done, n - 1)
                        sp.wait_ge(xh_done, n - 1)
                    sp.dma_start(oT[:, s], k["o"][bass.ds(n, 1)].rearrange("o (g p) t -> p (o g) t", p=P)).then_inc(o_in[s], 16)
                    sp.dma_start(xt[:, s], w["x"][bass.ds(n, 1)].rearrange("o (j p) f -> p (o j) f", p=P)).then_inc(x_in[s], 16)

            pipeline(sp, NB, load)
            for s in range(2):
                sp.wait_ge(x1_out[s], 16 * (NB // 2))

        @block.gpsimd
        def _(pool):
            def step(a, b):
                if a:
                    n, s, m = a
                    pool.wait_ge(h_done, n + 1)
                    if since(n, 2):
                        pool.wait_ge(r_done, n - 1)
                    nc.gpsimd.tensor_tensor(xh[:, s], xt[:, s], h[:, s], ALU.add).then_inc(xh_done, 1)
                    pool.wait_ge(ss_done, (n + 1) * J)
                    nc.gpsimd.tensor_tensor(ms[:, s], ss[:, s], k["eps"][:, 0], ALU.add).then_inc(ms_done, 1)
                    pool.wait_ge(ms_done, n + 1)
                    nc.gpsimd.tensor_tensor(rstd[:, s], ms[:, s], k["exponent"][:, 0:J], ALU.pow).then_inc(rstd_done, 1)
                if b:
                    n, s, m = b
                    pool.wait_ge(mv_done, (n + 1) * J)
                    nc.gpsimd.tensor_tensor(ve[:, s], mv[:, s, :, 1], k["eps"][:, 1], ALU.add).then_inc(ve_done, 1)
                    pool.wait_ge(ve_done, n + 1)
                    nc.gpsimd.tensor_tensor(rs[:, s], ve[:, s], k["exponent"][:, 0:J], ALU.pow).then_inc(rs_done, 1)
                    pool.wait_ge(x1_done, (n + 1) * J)
                    pool.dma_start(k["x1"][bass.ds(n, 1)].rearrange("o (j p) f -> p (o j) f", p=P), x1[:, s]).then_inc(x1_out[s], 16)

            pipeline(pool, NB, step)

        @block.vector
        def _(dve):
            dve.wait_ge(w_in, 16 * NW)
            nc.vector.tensor_scalar(n2[:], n2[:], float(D) ** 0.5, None, ALU.mult).then_inc(n2_scaled, 1)

            def step(a, b):
                if a:
                    n, s, m = a
                    dve.wait_ge(mix_done, n + 1)
                    dve.wait_ge(x_in[s], m * 16 + 16)
                    if since(n, 2):
                        dve.wait_ge(xh_done, n - 1)
                    nc.vector.tensor_tensor(h[:, s], pm[:], xt[:, s], ALU.add).then_inc(h_done, 1)
                if b:
                    n, s, m = b
                    for i in range(IC - 1):
                        gated(dve, n, s, i)
                if a:
                    n, s, m = a
                    dve.wait_ge(rstd_done, n + 1)
                    if since(n, 2):
                        dve.wait_ge(T_done, n - 1)
                    for j in range(J):
                        nc.vector.tensor_scalar(hn[:, s, j], h[:, s, j], rstd[:, s, j:j + 1], None, ALU.mult).then_inc(hn_done, 1)
                if b:
                    n, s, m = b
                    gated(dve, n, s, IC - 1)
                    dve.wait_ge(down_done, n + 1)
                    dve.wait_ge(xh_done, n + 1)
                    nc.vector.tensor_tensor(r[:, s], py[:, s], xh[:, s], ALU.add).then_inc(r_done, 1)
                    dve.wait_ge(r_done, n + 1)
                    for j in range(J):
                        nc.vector.bn_stats(st6[:, s, j], r[:, s, j]).then_inc(st_done, 1)
                    dve.wait_ge(st_done, (n + 1) * J)
                    dve.sem_inc(st_seen, 1)
                    for j in range(J):
                        nc.vector.bn_aggr(mv[:, s, j], st6[:, s, j]).then_inc(mv_done, 1)
                    dve.wait_ge(rs_done, n + 1)
                    if since(n, 2):
                        dve.wait_ge(x1_out[s], m * 16)
                    for j in range(J):
                        nc.vector.tensor_scalar(x1[:, s, j], r[:, s, j], mv[:, s, j, 0:1], rs[:, s, j:j + 1], ALU.subtract,
                                                ALU.mult).then_inc(x1_done, 1)

            def gated(dve, n, s, i):
                m = width(i)
                dve.wait_ge(gate_done, n * IC + i + 1)
                nc.vector.tensor_tensor(act_gu[0:m, s, i], pgu[0:m, i % 2, 1], gate[0:m, i % 2], ALU.mult).then_inc(prod_done, 1)

            pipeline(dve, NB, step)

        @block.scalar
        def _(act):
            act.wait_ge(n2_scaled, 1)

            def step(a, b):
                if a:
                    n, s, m = a
                    act.wait_ge(h_done, n + 1)
                    if since(n, 1):
                        act.wait_ge(ss_done, n * J)
                    for j in range(J):
                        nc.scalar.activation(sq[:, j], h[:, s, j], ACT.Square, accum_out=ss[:, s, j:j + 1]).then_inc(ss_done, 1)
                if b:
                    for i in range(IC - 1):
                        silu(b, i)
                if a:
                    n, s, m = a
                    act.wait_ge(T_done, n + 1)
                    for g in range(G):
                        nc.scalar.activation(hT[:, s, g], pT[:, g], ACT.Copy, scale=n2[:, g:g + 1]).then_inc(hT_done, 1)
                if b:
                    silu(b, IC - 1)

            def silu(b, i):
                n, s, m = b
                m = width(i)
                act.wait_ge(gu_done, n * IC + i + 1)
                if since(n, 1) or i >= 2:
                    act.wait_ge(prod_done, n * IC + i - 1)
                nc.scalar.activation(gate[0:m, i % 2], pgu[0:m, i % 2, 0], ACT.Silu).then_inc(gate_done, 1)

            pipeline(act, NB, step)

        @block.tensor
        def _(pe):
            pe.wait_ge(w_in, 16 * NW)

            def step(a, b):
                if a:
                    n, s, m = a
                    pe.wait_ge(o_in[s], m * 16 + 16)
                    if since(n, 1):
                        pe.wait_ge(h_done, n)
                    for j in range(J):
                        for g in range(G):
                            ins = nc.tensor.matmul(pm[:, j], oT[:, s, g, j * P:(j + 1) * P], wo[:, g], start=(g == 0), stop=(g == G - 1))
                    ins.then_inc(mix_done, 1)
                if b:
                    for i in range(IC - 1):
                        gate_up(b, i)
                if a:
                    n, s, m = a
                    pe.wait_ge(hn_done, (n + 1) * J)
                    if since(n, 1):
                        pe.wait_ge(hT_done, n * G)
                    for j in range(J):
                        for g in range(G):
                            ins = nc.tensor.transpose(pT[:, g, j * P:(j + 1) * P], hn[:, s, j, g * P:(g + 1) * P], ident[:])
                    ins.then_inc(T_done, 1)
                if b:
                    gate_up(b, IC - 1)
                    n, s, m = b
                    if since(n, 2):
                        pe.wait_ge(r_done, n - 1)
                    for j in range(J):
                        for i in range(IC):
                            pe.wait_ge(prod_done, n * IC + i + 1)
                            c = width(i)
                            ins = nc.tensor.matmul(py[:, s, j], act_gu[0:c, s, i, j * P:(j + 1) * P], wd[0:c, i], start=(i == 0),
                                                   stop=(i == IC - 1))
                    ins.then_inc(down_done, 1)

            def gate_up(b, i):
                n, s, m = b
                c = width(i)
                pe.wait_ge(hT_done, (n + 1) * G)
                if since(n, 1) or i >= 2:
                    pe.wait_ge(prod_done, n * IC + i - 1)
                for which, wt in enumerate((wg, wu)):
                    for g in range(G):
                        ins = nc.tensor.matmul(pgu[0:c, i % 2, which], wt[:, g, i * P:i * P + c], hT[:, s, g], start=(g == 0),
                                               stop=(g == G - 1))
                ins.then_inc(gu_done, 1)

            pipeline(pe, NB, step)


def cross_attention(nc, sem, w, k):
    ident = k["ident"]
    x2_all, chosen = k["x2"], k["chosen"]
    SCALE = HD ** -0.5
    with ExitStack() as ctx:
        sb = lambda n, s, d=F32: ctx.enter_context(nc.sbuf_tensor("a_" + n, s, d))
        ps = lambda n, s: ctx.enter_context(nc.psum_tensor("a_" + n, s, F32))
        wq, wk, wv, wo = (sb("w" + n, [P, G, D]) for n in "qkvo")
        wr = sb("wr", [P, G, NE])
        bq, bk = sb("bq", [P, G]), sb("bk", [P, G])
        bv, bo, br = sb("bv", [P, D]), sb("bo", [P, D]), sb("br", [P, NE])
        number, bit = sb("number", [P, 1], I32), sb("bit", [P, 1], I32)
        parity = sb("parity", [P, 2])
        rank = sb("rank", [P, J, NE])
        ct = sb("ct", [CTX, 2, D])
        cT = sb("cT", [P, G, CTX])
        x1 = sb("x1", [P, 2, J, D])
        xb = sb("xb", [P, 2, J, D])
        x1T = sb("x1T", [P, G, T])
        qT = sb("qT", [P, G, T])
        kE = sb("kE", [P, G, 2, CTX])
        vP = sb("vP", [CTX, 2, H // 2, 2, 2 * HD])
        mx = sb("mx", [P, J, H])
        pr = sb("pr", [P, 2, J, H, CTX])
        sm = sb("sm", [P, J, H])
        rc = sb("rc", [P, J, H])
        prT = sb("prT", [CTX, H, T])
        aT = sb("aT", [P, G, T])
        r = sb("r", [P, J, D])
        st6 = sb("st6", [P, J, 6])
        mv = sb("mv", [P, J, 2])
        ve, rs = sb("ve", [P, J]), sb("rs", [P, J])
        x2 = sb("x2", [P, 2, J, D])
        x2T = sb("x2T", [P, G, T])
        lg = sb("lg", [P, J, NE])
        lmax = sb("lmax", [P, J])
        best = sb("best", [P, J, NE])
        first = sb("first", [P, J])
        pT = ps("pT", [P, G, T])
        pq = ps("pq", [P, G, T])
        pS = ps("pS", [P, 4, 512])
        pP = ps("pP", [P, 4, P])
        po = ps("po", [P, J, D])
        pT4 = pT[:].rearrange("p g (a t) -> p (g a) t", t=P)
        names = ("w_in", "set", "ctxT_done", "ctxT_out", "x1T_done", "x1T_out", "k_done", "k_out", "v_done", "v_out", "q_done", "q_out", "score_done",
                 "max_done", "sub_done", "exp_done", "sum_done", "rec_done", "norm_done", "PT_done", "PT_out", "pv_done", "pv_out",
                 "o_done", "xb_done", "r_done", "st_done", "mv_done", "ve_done", "rs_done", "x2_done", "x2_kept", "x2T_done", "x2T_out",
                 "logit_done", "lg_done", "lmax_done", "best_done", "tied_done", "first_done", "chosen_done")
        (w_in, ready, ctxT_done, ctxT_out, x1T_done, x1T_out, k_done, k_out, v_done, v_out, q_done, q_out, score_done, max_done, sub_done,
         exp_done, sum_done, rec_done, norm_done, PT_done, PT_out, pv_done, pv_out, o_done, xb_done, r_done, st_done, mv_done,
         ve_done, rs_done, x2_done, x2_kept, x2T_done, x2T_out, logit_done, lg_done, lmax_done, best_done, tied_done,
         first_done, chosen_done) = (sem("a_" + n) for n in names)
        x_in, c_in = ([sem(f"a_{n}{s}") for s in range(2)] for n in ("x_in", "c_in"))
        bq_scaled, set_up, st_seen = sem("a_bq_scaled"), sem("a_set_up"), sem("a_st_seen")
        NW = 10
        block = ctx.enter_context(nc.Block())

        @block.sync
        def _(sp):
            with nc.allow_non_contiguous_dma(reason="small vectors"):
                for t, name in ((wk, "Wk"), (wv, "Wv"), (wq, "Wq"), (wo, "Wo")):
                    sp.dma_start(t[:], w["L0_xattn_" + name].rearrange("(g p) n -> p g n", p=P)).then_inc(w_in, 16)
                sp.dma_start(wr[:], w["L0_ffn_Wr"].rearrange("(g p) n -> p g n", p=P)).then_inc(w_in, 16)
                sp.dma_start(bq[:], column(w["L0_xattn_bq"])).then_inc(w_in, 16)
                sp.dma_start(bk[:], column(w["L0_xattn_bk"])).then_inc(w_in, 16)
                sp.dma_start(bv[:], row(w["L0_xattn_bv"])).then_inc(w_in, 16)
                sp.dma_start(bo[:], row(w["L0_xattn_bo"])).then_inc(w_in, 16)
                sp.dma_start(br[:], row(w["L0_ffn_br"])).then_inc(w_in, 16)

            def load(a, b):
                if a:
                    n, s, m = a
                    if since(n, 2):
                        sp.wait_ge(xb_done, n - 1)
                        sp.wait_ge(x1T_done, n - 1)
                        sp.wait_ge(ctxT_done, n - 1)
                    sp.dma_start(ct[:, s], w["ctx_1024"][bass.ds(n, 1)].rearrange("o c f -> c (o f)")).then_inc(c_in[s], 16)
                    sp.dma_start(x1[:, s], k["x1"][bass.ds(n, 1)].rearrange("o (j p) f -> p (o j) f", p=P)).then_inc(x_in[s], 16)

            pipeline(sp, NB, load)

        @block.gpsimd
        def _(pool):
            nc.gpsimd.iota(number[:], [[0, 1]], base=0, channel_multiplier=1).then_inc(ready, 1)
            nc.gpsimd.memset(vP[:], 0.0).then_inc(ready, 1)
            nc.gpsimd.iota(rank[:], [[0, J], [-1, NE]], base=NE, channel_multiplier=0,
                           allow_small_or_imprecise_dtypes=True).then_inc(ready, 1)
            nc.gpsimd.memset(x2_all[:, :, D + 1:], 0.0).then_inc(ready, 1)
            nc.gpsimd.iota(x2_all[:, :, D:D + 1].bitcast(I32), [[P, TILES], [0, 1]], base=0, channel_multiplier=1).then_inc(ready, 1)
            pool.wait_ge(w_in, 16 * NW)

            def step(a, b):
                if a:
                    n, s, m = a
                    pool.wait_ge(x_in[s], m * 16 + 16)
                    if since(n, 2):
                        pool.wait_ge(r_done, n - 1)
                    nc.gpsimd.tensor_tensor(xb[:, s], x1[:, s], bo[:].rearrange("p (o f) -> p o f", o=1).to_broadcast([P, J, D]),
                                            ALU.add).then_inc(xb_done, 1)
                    normalise(n, s, 0)
                if b:
                    n, s, m = b
                    pool.wait_ge(mv_done, (n + 1) * J)
                    nc.gpsimd.tensor_tensor(ve[:], mv[:, :, 1], k["eps"][:, 1], ALU.add).then_inc(ve_done, 1)
                    pool.wait_ge(ve_done, n + 1)
                    nc.gpsimd.tensor_tensor(rs[:], ve[:], k["exponent"][:, 0:J], ALU.pow).then_inc(rs_done, 1)
                if a:
                    normalise(a[0], a[1], 1)

            def normalise(n, s, j):
                pool.wait_ge(rec_done, n * J + j + 1)
                nc.gpsimd.tensor_tensor(pr[:, s, j], pr[:, s, j], rc[:, j].rearrange("p (h o) -> p h o", o=1).to_broadcast([P, H, CTX]),
                                        ALU.mult).then_inc(norm_done, 1)

            pipeline(pool, NB, step)

        @block.vector
        def _(dve):
            dve.wait_ge(w_in, 16 * NW)
            dve.wait_ge(ready, 5)
            nc.vector.tensor_scalar(bq[:], bq[:], SCALE, None, ALU.mult).then_inc(bq_scaled, 1)
            nc.vector.tensor_scalar(bit[:], number[:], HD.bit_length() - 1, 1, ALU.logical_shift_right, ALU.bitwise_and).then_inc(set_up, 1)
            dve.wait_ge(set_up, 1)
            nc.vector.tensor_copy(parity[:, 1:2], bit[:]).then_inc(set_up, 1)
            dve.wait_ge(set_up, 2)
            nc.vector.tensor_scalar(parity[:, 0:1], parity[:, 1:2], -1.0, 1.0, ALU.mult, ALU.add).then_inc(set_up, 1)
            dve.wait_ge(set_up, 3)

            def step(a, b):
                if a:
                    n, s, m = a
                    dve.wait_ge(k_done, n + 1)
                    if since(n, 1):
                        dve.wait_ge(score_done, n * J)
                    for g in range(G):
                        for p in range(2):
                            nc.vector.tensor_scalar(kE[:, g, p], pq[:, g, 0:CTX], bk[:, g:g + 1], parity[:, p:p + 1], ALU.add,
                                                    ALU.mult).then_inc(k_out, 1)
                    dve.wait_ge(v_done, n + 1)
                    if since(n, 2):
                        dve.wait_ge(pv_done, n - 1)
                    for p in range(2):
                        half = slice(p * HD, (p + 1) * HD)
                        nc.vector.tensor_tensor(vP[:, s, :, p, half], pT[0:CTX, 0].rearrange("c (h p d) -> c h p d", p=2, d=HD)[:, :, p],
                                                bv[0:CTX].rearrange("c (h p d) -> c h p d", p=2, d=HD)[:, :, p], ALU.add).then_inc(v_out, 1)
                    shift(n, s, 0)
                    total(n, s, 0)
                    shift(n, s, 1)
                if b:
                    n, s, m = b
                    dve.wait_ge(o_done, n + 1)
                    dve.wait_ge(xb_done, n + 1)
                    nc.vector.tensor_tensor(r[:], po[:], xb[:, s], ALU.add).then_inc(r_done, 1)
                    dve.wait_ge(r_done, n + 1)
                    for j in range(J):
                        nc.vector.bn_stats(st6[:, j], r[:, j]).then_inc(st_done, 1)
                    dve.wait_ge(st_done, (n + 1) * J)
                    dve.sem_inc(st_seen, 1)
                    for j in range(J):
                        nc.vector.bn_aggr(mv[:, j], st6[:, j]).then_inc(mv_done, 1)
                    dve.wait_ge(rs_done, n + 1)
                    if since(n, 2):
                        dve.wait_ge(x2_kept, n - 1)
                    for j in range(J):
                        nc.vector.tensor_scalar(x2[:, s, j], r[:, j], mv[:, j, 0:1], rs[:, j:j + 1], ALU.subtract,
                                                ALU.mult).then_inc(x2_done, 1)
                if a:
                    total(a[0], a[1], 1)
                if b:
                    n, s, m = b
                    dve.wait_ge(logit_done, n + 1)
                    nc.vector.tensor_tensor(lg[:], pq[:, :, 0:NE], br[:].rearrange("p (o e) -> p o e", o=1).to_broadcast([P, J, NE]),
                                            ALU.add).then_inc(lg_done, 1)
                    dve.wait_ge(lg_done, n + 1)
                    nc.vector.tensor_reduce(lmax[:], lg[:], AX, ALU.max).then_inc(lmax_done, 1)
                    dve.wait_ge(lmax_done, n + 1)
                    nc.vector.tensor_tensor(best[:], lg[:], lmax[:].rearrange("p (j o) -> p j o", o=1).to_broadcast([P, J, NE]),
                                            ALU.is_ge).then_inc(best_done, 1)
                    dve.wait_ge(best_done, n + 1)
                    nc.vector.tensor_tensor(best[:], best[:], rank[:], ALU.mult).then_inc(tied_done, 1)
                    dve.wait_ge(tied_done, n + 1)
                    nc.vector.tensor_reduce(first[:], best[:], AX, ALU.max).then_inc(first_done, 1)
                    dve.wait_ge(first_done, n + 1)
                    nc.vector.tensor_tensor(chosen[:, bass.ds(n * J, J)], best[:],
                                            first[:].rearrange("p (j o) -> p j o", o=1).to_broadcast([P, J, NE]),
                                            ALU.is_equal).then_inc(chosen_done, 1)

            def scores(j):
                return pS[:, :, 0:4 * CTX].rearrange("p r (q c) -> p r q c", c=CTX)

            def heads(x):
                return x.rearrange("p (r q) c -> p r q c", r=4)

            def shift(n, s, j):
                dve.wait_ge(score_done, n * J + j + 1)
                nc.vector.tensor_reduce(mx[:, j].rearrange("p (r q) -> p r q", r=4), scores(j), AX, ALU.max).then_inc(max_done, 1)
                dve.wait_ge(max_done, n * J + j + 1)
                if since(n, 2):
                    dve.wait_ge(PT_done, (n - 1) * 8)
                nc.vector.tensor_tensor(heads(pr[:, s, j]), scores(j),
                                        mx[:, j].rearrange("p (r q o) -> p r q o", r=4, o=1).to_broadcast([P, 4, 4, CTX]),
                                        ALU.subtract).then_inc(sub_done, 1)

            def total(n, s, j):
                dve.wait_ge(exp_done, n * J + j + 1)
                nc.vector.tensor_reduce(sm[:, j], pr[:, s, j], AX, ALU.add).then_inc(sum_done, 1)
                dve.wait_ge(sum_done, n * J + j + 1)
                if since(n, 1):
                    dve.wait_ge(norm_done, n * J - J + j + 1)
                nc.vector.reciprocal(rc[:, j], sm[:, j]).then_inc(rec_done, 1)

            pipeline(dve, NB, step)

        @block.scalar
        def _(act):
            act.wait_ge(bq_scaled, 1)

            def step(a, b):
                if a:
                    n, s, m = a
                    act.wait_ge(ctxT_done, n + 1)
                    nc.scalar.activation(cT[:], pq[:, :, 0:CTX], ACT.Copy).then_inc(ctxT_out, 1)
                    act.wait_ge(x1T_done, n + 1)
                    nc.scalar.activation(x1T[:], pT[:], ACT.Copy).then_inc(x1T_out, 1)
                    act.wait_ge(q_done, n + 1)
                    if since(n, 1):
                        act.wait_ge(score_done, n * J)
                    for g in range(G):
                        nc.scalar.activation(qT[:, g], pq[:, g], ACT.Identity, bias=bq[:, g:g + 1], scale=SCALE).then_inc(q_out, 1)
                if b:
                    transposed(b, 0)
                if a:
                    exponential(a, 0)
                if b:
                    transposed(b, 1)
                    n, s, m = b
                    act.wait_ge(pv_done, n + 1)
                    nc.scalar.activation(aT[:], po[:], ACT.Copy).then_inc(pv_out, 1)
                if a:
                    exponential(a, 1)
                if b:
                    n, s, m = b
                    act.wait_ge(x2T_done, n + 1)
                    nc.scalar.activation(x2T[:], pT[:], ACT.Copy).then_inc(x2T_out, 1)
                    nc.scalar.activation(x2_all[:, bass.ds(n * J, J), 0:D], x2[:, s], ACT.Copy).then_inc(x2_kept, 1)

            def transposed(b, j):
                n, s, m = b
                for q in range(4):
                    act.wait_ge(PT_done, n * 8 + j * 4 + q + 1)
                    if since(n, 1):
                        act.wait_ge(pv_done, n)
                    src = (pP, pT4)[q % 2]
                    nc.scalar.activation(prT[:, q * 4:q * 4 + 4, j * P:(j + 1) * P], src[0:CTX], ACT.Copy).then_inc(PT_out, 1)

            def exponential(a, j):
                n, s, m = a
                act.wait_ge(sub_done, n * J + j + 1)
                nc.scalar.activation(pr[:, s, j], pr[:, s, j], ACT.Exp).then_inc(exp_done, 1)

            pipeline(act, NB, step)

        @block.tensor
        def _(pe):
            pe.wait_ge(w_in, 16 * NW)

            def step(a, b):
                if a:
                    n, s, m = a
                    pe.wait_ge(c_in[s], m * 16 + 16)
                    if since(n, 2):
                        pe.wait_ge(lg_done, n - 1)
                    for g in range(G):
                        ins = nc.tensor.transpose(pq[:, g, 0:CTX], ct[:, s, g * P:(g + 1) * P], ident[0:CTX, 0:CTX])
                    ins.then_inc(ctxT_done, 1)
                    pe.wait_ge(x_in[s], m * 16 + 16)
                    if since(n, 2):
                        pe.wait_ge(x2T_out, n - 1)
                    for j in range(J):
                        for g in range(G):
                            ins = nc.tensor.transpose(pT[:, g, j * P:(j + 1) * P], x1[:, s, j, g * P:(g + 1) * P], ident[:])
                    ins.then_inc(x1T_done, 1)
                    pe.wait_ge(ctxT_out, n + 1)
                    for go in range(G):
                        for g in range(G):
                            ins = nc.tensor.matmul(pq[:, go, 0:CTX], wk[:, g, go * P:(go + 1) * P], cT[:, g], start=(g == 0), stop=(g == G - 1))
                    ins.then_inc(k_done, 1)
                    pe.wait_ge(x1T_out, n + 1)
                    for g in range(G):
                        ins = nc.tensor.matmul(pT[0:CTX, 0], cT[:, g], wv[:, g], start=(g == 0), stop=(g == G - 1))
                    ins.then_inc(v_done, 1)
                    pe.wait_ge(k_out, (n + 1) * 4)
                    for go in range(G):
                        for g in range(G):
                            ins = nc.tensor.matmul(pq[:, go], wq[:, g, go * P:(go + 1) * P], x1T[:, g], start=(g == 0), stop=(g == G - 1))
                    ins.then_inc(q_done, 1)
                    pe.wait_ge(q_out, (n + 1) * G)
                    scores(n, 0)
                if b:
                    n, s, m = b
                    if a:
                        pe.wait_ge(v_out, (a[0] + 1) * 2)
                    pe.wait_ge(norm_done, (n + 1) * J)
                    for j in range(J):
                        for q in range(4):
                            if j > 0 or q > 1:
                                pe.wait_ge(PT_out, n * 8 + j * 4 + q - 1)
                            elif since(n, 1):
                                pe.wait_ge(PT_out, n * 8)
                            dst = (pP, pT4)[q % 2]
                            for i in range(4):
                                ins = nc.tensor.transpose(dst[0:CTX, i], pr[:, s, j, q * 4 + i], ident[:])
                            ins.then_inc(PT_done, 1)
                    pe.wait_ge(PT_out, (n + 1) * 8)
                    if since(n, 1):
                        pe.wait_ge(r_done, n)
                    for q in range(4):
                        for g in range(G):
                            for p in range(2):
                                ins = nc.tensor.matmul(po[32 * q:32 * q + 32, g], vP[:, s, g * 4 + q, p], prT[:, q * 4 + g * 2 + p],
                                                       start=(p == 0), stop=(p == 1))
                    ins.then_inc(pv_done, 1)
                if a:
                    scores(a[0], 1)
                if b:
                    n, s, m = b
                    pe.wait_ge(pv_out, n + 1)
                    for j in range(J):
                        for g in range(G):
                            ins = nc.tensor.matmul(po[:, j], aT[:, g, j * P:(j + 1) * P], wo[:, g], start=(g == 0), stop=(g == G - 1))
                    ins.then_inc(o_done, 1)
                    pe.wait_ge(x2_done, (n + 1) * J)
                    for j in range(J):
                        for g in range(G):
                            ins = nc.tensor.transpose(pT[:, g, j * P:(j + 1) * P], x2[:, s, j, g * P:(g + 1) * P], ident[:])
                    ins.then_inc(x2T_done, 1)
                    pe.wait_ge(x2T_out, n + 1)
                    for j in range(J):
                        for g in range(G):
                            ins = nc.tensor.matmul(pq[:, j, 0:NE], x2T[:, g, j * P:(j + 1) * P], wr[:, g], start=(g == 0), stop=(g == G - 1))
                    ins.then_inc(logit_done, 1)

            def scores(n, j):
                if j > 0:
                    pe.wait_ge(sub_done, n * J + j)
                elif since(n, 1):
                    pe.wait_ge(sub_done, n * J)
                for q in range(4):
                    rows = slice(32 * q, 32 * q + 32)
                    for g in range(G):
                        ins = nc.tensor.matmul(pS[:, q, g * 2 * CTX:(g + 1) * 2 * CTX], qT[rows, g, j * P:(j + 1) * P],
                                               kE[rows, g].rearrange("p a c -> p (a c)"), start=True, stop=True)
                ins.then_inc(score_done, 1)

            pipeline(pe, NB, step)


def dispatch(nc, sem, w, k):
    x2, chosen = k["x2"], k["chosen"]
    PAD = TILES // 2
    with ExitStack() as ctx:
        sb = lambda n, s, d=F32: ctx.enter_context(nc.sbuf_tensor("d_" + n, s, d))
        ps = lambda n, s: ctx.enter_context(nc.psum_tensor("d_" + n, s, F32))
        before = sb("before", [P, P])
        ones = sb("ones", [P, P])
        upto = [sb(f"upto{i}", [P, PAD + TILES, NE]) for i in range(2)]
        upto_e = [sb(f"upto_e{i}", [P, NE + NE]) for i in range(2)]
        full = sb("full", [P, NE, TILES])
        needs = sb("needs", [P, NE, TILES])
        used = sb("used", [P, NE])
        start = sb("start", [P, NE])
        place = sb("place", [P, TILES, NE])
        pos = sb("pos", [P, TILES])
        pos_i = sb("pos_i", [P, TILES], U32)
        slot_no = sb("slot_no", [P, SLOTS, NE])
        passed = sb("passed", [P, SLOTS, NE])
        expert = sb("expert", [P, SLOTS])
        turn = sb("turn", [P, 2, SLOTS])
        count = ps("count", [P, 2, TILES, NE])
        made, counted, places, tables, rows_out = (sem("d_" + n) for n in ("made", "counted", "places", "tables", "rows_out"))
        block = ctx.enter_context(nc.Block())

        @block.gpsimd
        def _(pool):
            nc.gpsimd.memset(before[:], 1.0).then_inc(made, 1)
            nc.gpsimd.memset(ones[:], 1.0).then_inc(made, 1)
            for i in range(2):
                nc.gpsimd.memset(upto[i][:], 0.0).then_inc(made, 1)
                nc.gpsimd.memset(upto_e[i][:], 0.0).then_inc(made, 1)
            nc.gpsimd.iota(full[:], [[0, NE], [P, TILES]], base=0, channel_multiplier=0, allow_small_or_imprecise_dtypes=True).then_inc(made, 1)
            nc.gpsimd.iota(slot_no[:], [[1, SLOTS], [0, NE]], base=0, channel_multiplier=0, allow_small_or_imprecise_dtypes=True).then_inc(made, 1)
            pool.wait_ge(made, 8)
            nc.gpsimd.affine_select(out=before[:], in_=before[:], compare_op=ALU.is_gt, fill=0.0, base=0,
                                    pattern=[[1, P]], channel_multiplier=-1).then_inc(made, 1)
            pool.wait_ge(places, 12)
            for t in range(TILES):
                pool.indirect_dma_start(k["routed"], bass.IndirectOffsetOnAxis(ap=pos_i[:, t:t + 1], axis=0), x2[:, t], None).then_inc(rows_out, 16)
            pool.wait_ge(rows_out, 16 * TILES)

        @block.tensor
        def _(pe):
            pe.wait_ge(made, 9)
            every = chosen[:].rearrange("p t e -> p (t e)")
            nc.tensor.matmul(count[:, 0].rearrange("p t e -> p (t e)"), before[:], every, start=True, stop=True).then_inc(counted, 1)
            nc.tensor.matmul(count[:, 1].rearrange("p t e -> p (t e)"), ones[:], every, start=True, stop=True).then_inc(counted, 1)

        @block.vector
        def _(dve):
            of_tile = count[:, 1]
            dve.wait_ge(made, 9)
            dve.wait_ge(counted, 2)
            nc.vector.tensor_copy(upto[0][:, PAD:], of_tile).then_inc(places, 1)
            n, d = 1, 1
            while d < TILES:
                dve.wait_ge(places, n)
                src, dst = upto[(n - 1) % 2], upto[n % 2]
                nc.vector.tensor_tensor(dst[:, PAD:], src[:, PAD:], src[:, PAD - d:PAD + TILES - d], ALU.add).then_inc(places, 1)
                n, d = n + 1, 2 * d
            total = upto[(n - 1) % 2]
            dve.wait_ge(places, n)
            nc.vector.tensor_tensor(place[:], count[:, 0], total[:, PAD:], ALU.add).then_inc(places, 1)
            last = total[:, PAD + TILES - 1].rearrange("p (e o) -> p e o", o=1).to_broadcast([P, NE, TILES])
            nc.vector.tensor_tensor(needs[:], last, full[:], ALU.is_gt).then_inc(tables, 1)
            dve.wait_ge(places, n + 1)
            nc.vector.tensor_tensor(place[:], place[:], of_tile, ALU.subtract).then_inc(places, 1)
            dve.wait_ge(tables, 1)
            nc.vector.tensor_reduce(used[:], needs[:], AX, ALU.add).then_inc(tables, 1)
            dve.wait_ge(tables, 2)
            nc.vector.tensor_copy(upto_e[0][:, NE:], used[:]).then_inc(tables, 1)
            m, d = 3, 1
            while d < NE:
                dve.wait_ge(tables, m)
                src, dst = upto_e[(m - 3) % 2], upto_e[(m - 2) % 2]
                nc.vector.tensor_tensor(dst[:, NE:], src[:, NE:], src[:, NE - d:2 * NE - d], ALU.add).then_inc(tables, 1)
                m, d = m + 1, 2 * d
            end = upto_e[(m - 3) % 2][:, NE:]
            dve.wait_ge(tables, m)
            nc.vector.tensor_tensor(start[:], end, used[:], ALU.subtract).then_inc(tables, 1)
            dve.wait_ge(tables, m + 1)
            nc.vector.tensor_scalar(start[:], start[:], float(P), None, ALU.mult).then_inc(tables, 1)
            dve.wait_ge(tables, m + 2)
            dve.wait_ge(places, n + 2)
            nc.vector.tensor_tensor(place[:], place[:], start[:].rearrange("p (o e) -> p o e", o=1).to_broadcast([P, TILES, NE]),
                                    ALU.add).then_inc(places, 1)
            dve.wait_ge(places, n + 3)
            nc.vector.tensor_tensor(place[:], place[:], chosen[:], ALU.mult).then_inc(places, 1)
            dve.wait_ge(places, n + 4)
            nc.vector.tensor_reduce(pos[:], place[:], AX, ALU.add).then_inc(places, 1)
            dve.wait_ge(places, n + 5)
            nc.vector.tensor_copy(pos_i[:], pos[:]).then_inc(places, 1)
            assert n + 6 == 12
            nc.vector.tensor_tensor(passed[:], slot_no[:], end.rearrange("p (o e) -> p o e", o=1).to_broadcast([P, SLOTS, NE]),
                                    ALU.is_ge).then_inc(tables, 1)
            dve.wait_ge(tables, m + 3)
            nc.vector.tensor_reduce(expert[:], passed[:], AX, ALU.add).then_inc(tables, 1)
            dve.wait_ge(tables, m + 4)
            nc.vector.tensor_scalar(expert[:], expert[:], NE - 1.0, None, ALU.min).then_inc(tables, 1)
            dve.wait_ge(tables, m + 5)
            for i in range(2):
                nc.vector.tensor_scalar(turn[:, i], expert[:], (i + 1.0) * WBUFS, -float(WBUFS), ALU.is_ge, ALU.mult).then_inc(tables, 1)
            dve.wait_ge(tables, m + 7)
            nc.vector.tensor_tensor(turn[:, 0], turn[:, 0], turn[:, 1], ALU.add).then_inc(tables, 1)
            dve.wait_ge(tables, m + 8)
            nc.vector.tensor_tensor(turn[:, 0], turn[:, 0], expert[:], ALU.add).then_inc(tables, 1)
            dve.wait_ge(tables, m + 9)
            nc.vector.tensor_scalar(k["w_at"][:], turn[:, 0], float(WROW), None, ALU.mult).then_inc(tables, 1)
            nc.vector.tensor_scalar(k["w_loads"][:], expert[:], 16.0 * WDMAS, 16.0 * WDMAS, ALU.mult, ALU.add).then_inc(tables, 1)
            nc.vector.tensor_scalar(k["w_free"][:], end, 1.0, None, ALU.add).then_inc(tables, 1)
            dve.wait_ge(tables, m + 12)


def experts(nc, sem, w, k, out):
    ident = k["ident"]
    C1, C2, HALF = F1 // P, F2 // P, F1 // 2
    W1_AT, W2_AT, W3_AT, B1_AT, B2_AT, B3_AT = WPARTS
    with ExitStack() as ctx:
        sb = lambda n, s, d=F32: ctx.enter_context(nc.sbuf_tensor("e_" + n, s, d))
        ps = lambda n, s: ctx.enter_context(nc.psum_tensor("e_" + n, s, F32))
        wt = sb("wt", [P, WBUFS * WROW])
        xt = sb("xt", [P, 2, XROW])
        token = sb("token", [P, 2, 1], U32)
        xb = sb("xb", [P, 2, D])
        xT = sb("xT", [P, G, P])
        h1 = sb("h1", [P, 2, HALF])
        g1 = sb("g1", [P, 2, C1 // 2, P])
        h2 = sb("h2", [P, F2])
        g2 = sb("g2", [P, C2, P])
        r = sb("r", [P, D])
        st6 = sb("st6", [P, 6])
        mv = sb("mv", [P, 2])
        ve, rs = sb("ve", [P, 1]), sb("rs", [P, 1])
        y = sb("y", [P, 2, D])
        pX = ps("pX", [P, G, P])
        ph1 = ps("ph1", [P, 2, HALF])
        pT1 = ps("pT1", [P, 2, C1 // 2, P])
        ph2 = ps("ph2", [P, F2])
        pT2 = ps("pT2", [P, C2, P])
        py = ps("py", [P, D])
        names = ("w_in", "w_ready", "xT_done", "xT_out", "token_kept", "xb_done", "h1_done", "h1_out", "T1_done", "g1_done", "h2_done",
                 "h2_out", "T2_done", "g2_done", "y_done", "r_done", "st_done", "st_seen", "mv_done", "ve_done", "rs_done", "row_done",
                 "row_seen")
        (w_in, w_ready, xT_done, xT_out, token_kept, xb_done, h1_done, h1_out, T1_done, g1_done, h2_done, h2_out, T2_done, g2_done,
         y_done, r_done, st_done, st_seen, mv_done, ve_done, rs_done, row_done, row_seen) = (sem("e_" + n) for n in names)
        x_in, row_out = ([sem(f"e_{n}{s}") for s in range(2)] for n in ("x_in", "row_out"))
        block = ctx.enter_context(nc.Block())

        def entry(eng, table, n, top):
            return eng.value_load(k[table][0:1, bass.ds(n, 1)], min_val=0, max_val=top)

        def weights(eng, n):
            return entry(eng, "w_at", n, (WBUFS - 1) * WROW)

        def loads(eng, n):
            return entry(eng, "w_loads", n, 16 * WDMAS * NE)

        @block.sync
        def _(sp):
            for e in range(NE):
                if e >= WBUFS:
                    sp.wait_ge(r_done, entry(sp, "w_free", e - WBUFS, SLOTS + 1))
                if e >= 1:
                    sp.wait_ge(w_in, 16 * WDMAS * e)
                at = lambda off, n: wt[:, e % WBUFS * WROW + off:e % WBUFS * WROW + off + n]
                for off, name, c, n in ((W1_AT, "W1", G, F1), (W2_AT, "W2", C1, F2), (W3_AT, "W3", C2, D)):
                    sp.dma_start(at(off, c * n).rearrange("p (c n) -> p c n", c=c),
                                 w["L0_ffn_" + name][e].rearrange("(c p) n -> p c n", p=P)).then_inc(w_in, 16)
                for off, name, n in ((B1_AT, "b1", F1), (B2_AT, "b2", F2), (B3_AT, "b3", D)):
                    sp.dma_start(at(off, n), row(w["L0_ffn_" + name][e])).then_inc(w_in, 16)
            sp.wait_ge(w_in, 16 * WDMAS * NE)

        @block.gpsimd
        def _(pool):
            def step(a, b):
                if a:
                    n, s, m = a
                    at = weights(pool, n)
                    pool.wait_ge(w_in, loads(pool, n))
                    pool.wait_ge(x_in[s], m * 16 + 16)
                    if since(n, 2):
                        pool.wait_ge(r_done, n)
                    pool.sem_inc(w_ready, 1)
                    nc.gpsimd.tensor_tensor(xb[:, s], xt[:, s, 0:D], wt[:, bass.ds(at + B3_AT, D)], ALU.add).then_inc(xb_done, 1)
                if b:
                    n, s, m = b
                    pool.wait_ge(mv_done, n + 1)
                    nc.gpsimd.tensor_tensor(ve[:], mv[:, 1:2], k["eps"][:, 1, 0:1], ALU.add).then_inc(ve_done, 1)
                    pool.wait_ge(ve_done, n + 1)
                    nc.gpsimd.tensor_tensor(rs[:], ve[:], k["exponent"][:, 0:1], ALU.pow).then_inc(rs_done, 1)
                    pool.wait_ge(row_done, n + 1)
                    pool.sem_inc(row_seen, 1)
                    pool.indirect_dma_start(out.rearrange("b t f -> (b t) f"), bass.IndirectOffsetOnAxis(ap=token[:, s], axis=0),
                                            y[:, s], None, bounds_check=NTOK - 1, oob_is_err=False).then_inc(row_out[s], 16)

            pipeline(pool, SLOTS, step)
            for s in range(2):
                pool.wait_ge(row_out[s], 16 * len(range(s, SLOTS, 2)))

        @block.vector
        def _(dve):
            dve.sem_inc(r_done, 1)

            def step(a, b):
                if a:
                    n, s, m = a
                    dve.wait_ge(x_in[s], m * 16 + 16)
                    if since(n, 2):
                        dve.wait_ge(row_out[s], m * 16)
                    nc.vector.tensor_copy(token[:, s], xt[:, s, D:D + 1].bitcast(U32)).then_inc(token_kept, 1)
                    dve.wait_ge(xT_done, n + 1)
                    if since(n, 1):
                        dve.wait_ge(h1_done, n * 2)
                    nc.vector.tensor_copy(xT[:], pX[:]).then_inc(xT_out, 1)
                if b:
                    n, s, m = b
                    at = weights(dve, n)
                    dve.wait_ge(h2_done, n + 1)
                    if since(n, 1):
                        dve.wait_ge(T2_done, n)
                    nc.vector.tensor_tensor(h2[:], ph2[:], wt[:, bass.ds(at + B2_AT, F2)], ALU.add).then_inc(h2_out, 1)
                if a:
                    n, s, m = a
                    at = weights(dve, n)
                    for q in range(2):
                        dve.wait_ge(h1_done, n * 2 + q + 1)
                        if since(n, 1):
                            dve.wait_ge(T1_done, n * 2 + q - 1)
                        nc.vector.tensor_tensor(h1[:, q], ph1[:, q], wt[:, bass.ds(at + (B1_AT + q * HALF), HALF)], ALU.add).then_inc(h1_out, 1)
                if b:
                    n, s, m = b
                    dve.wait_ge(y_done, n + 1)
                    dve.wait_ge(xb_done, n + 1)
                    nc.vector.tensor_tensor(r[:], py[:], xb[:, s], ALU.add).then_inc(r_done, 1)
                    dve.wait_ge(r_done, n + 2)
                    nc.vector.bn_stats(st6[:], r[:]).then_inc(st_done, 1)
                    dve.wait_ge(st_done, n + 1)
                    dve.sem_inc(st_seen, 1)
                    nc.vector.bn_aggr(mv[:], st6[:]).then_inc(mv_done, 1)
                    dve.wait_ge(rs_done, n + 1)
                    nc.vector.tensor_scalar(y[:, s], r[:], mv[:, 0:1], rs[:, 0:1], ALU.subtract, ALU.mult).then_inc(row_done, 1)

            pipeline(dve, SLOTS, step)

        @block.scalar
        def _(act):
            def load(n, s):
                act.dma_start(xt[:, s], k["routed"][bass.ds(n * P, P), :]).then_inc(x_in[s], 16)

            load(0, 0)

            def step(a, b):
                if a:
                    n, s, m = a
                    if not (isinstance(n, int) and n == SLOTS - 1):
                        if since(n, 1):
                            act.wait_ge(xT_done, n)
                            act.wait_ge(xb_done, n)
                            act.wait_ge(token_kept, n)
                        load(n + 1, 1 - s)
                if b:
                    n, s, m = b
                    act.wait_ge(T2_done, n + 1)
                    if since(n, 1):
                        act.wait_ge(y_done, n)
                    nc.scalar.activation(g2[:], pT2[:], ACT.Gelu).then_inc(g2_done, 1)
                if a:
                    n, s, m = a
                    for q in range(2):
                        act.wait_ge(T1_done, n * 2 + q + 1)
                        if since(n, 1):
                            act.wait_ge(h2_done, n)
                        nc.scalar.activation(g1[:, q], pT1[:, q], ACT.Gelu).then_inc(g1_done, 1)

            pipeline(act, SLOTS, step)

        @block.tensor
        def _(pe):
            def step(a, b):
                if a:
                    n, s, m = a
                    pe.wait_ge(x_in[s], m * 16 + 16)
                    if since(n, 1):
                        pe.wait_ge(xT_out, n)
                    for g in range(G):
                        ins = nc.tensor.transpose(pX[:, g], xt[:, s, g * P:(g + 1) * P], ident[:])
                    ins.then_inc(xT_done, 1)
                if b:
                    n, s, m = b
                    at_b = weights(pe, n)
                    if since(n, 1):
                        pe.wait_ge(h2_out, n)
                    for c in range(C1):
                        pe.wait_ge(g1_done, n * 2 + c // (C1 // 2) + 1)
                        ins = nc.tensor.matmul(ph2[:], g1[:, c // (C1 // 2), c % (C1 // 2)], wt[:, bass.ds(at_b + (W2_AT + c * F2), F2)],
                                               start=(c == 0), stop=(c == C1 - 1))
                    ins.then_inc(h2_done, 1)
                if a:
                    n, s, m = a
                    at_a = weights(pe, n)
                    pe.wait_ge(w_in, loads(pe, n))
                    pe.wait_ge(xT_out, n + 1)
                    for q in range(2):
                        if since(n, 1):
                            pe.wait_ge(h1_out, n * 2 + q - 1)
                        for g in range(G):
                            ins = nc.tensor.matmul(ph1[:, q], xT[:, g], wt[:, bass.ds(at_a + (W1_AT + g * F1 + q * HALF), HALF)],
                                                   start=(g == 0), stop=(g == G - 1))
                        ins.then_inc(h1_done, 1)
                if b:
                    n, s, m = b
                    pe.wait_ge(h2_out, n + 1)
                    if since(n, 1):
                        pe.wait_ge(g2_done, n)
                    for c in range(C2):
                        ins = nc.tensor.transpose(pT2[:, c], h2[:, c * P:(c + 1) * P], ident[:])
                    ins.then_inc(T2_done, 1)
                if a:
                    transposed(a, 0)
                if b:
                    n, s, m = b
                    pe.wait_ge(g2_done, n + 1)
                    if since(n, 1):
                        pe.wait_ge(r_done, n + 1)
                    for c in range(C2):
                        ins = nc.tensor.matmul(py[:], g2[:, c], wt[:, bass.ds(at_b + (W3_AT + c * D), D)], start=(c == 0), stop=(c == C2 - 1))
                    ins.then_inc(y_done, 1)
                if a:
                    transposed(a, 1)

            def transposed(a, q):
                n, s, m = a
                pe.wait_ge(h1_out, n * 2 + q + 1)
                if since(n, 1):
                    pe.wait_ge(g1_done, n * 2 + q - 1)
                for c in range(C1 // 2):
                    ins = nc.tensor.transpose(pT1[:, q, c], h1[:, q, c * P:(c + 1) * P], ident[:])
                ins.then_inc(T1_done, 1)

            pipeline(pe, SLOTS, step)


INPUTS = ["x", "ctx_1024", "L0_attn_norm1_w", "L0_attn_norm2_w", "L0_attn_conv_w", "L0_attn_conv_b", "L0_attn_wq",
          "L0_attn_wk", "L0_attn_wv", "L0_attn_wb", "L0_attn_wa", "L0_attn_wo", "L0_attn_wg", "L0_attn_wu", "L0_attn_wd",
          "L0_xattn_Wq", "L0_xattn_bq", "L0_xattn_Wk", "L0_xattn_bk", "L0_xattn_Wv", "L0_xattn_bv", "L0_xattn_Wo",
          "L0_xattn_bo", "L0_ffn_Wr", "L0_ffn_br", "L0_ffn_W1", "L0_ffn_b1", "L0_ffn_W2", "L0_ffn_b2", "L0_ffn_W3",
          "L0_ffn_b3"]


def build(nc, w, out):
    k = {
        "qkv": nc.dram_tensor("qkv", (3, NB, D, T), F32, kind="Internal").ap(),
        "gates": nc.dram_tensor("gates", (2, NB, H, T), F32, kind="Internal").ap(),
        "o": nc.dram_tensor("o", (NB, D, T), F32, kind="Internal").ap(),
        "x1": nc.dram_tensor("x1", (NB, T, D), F32, kind="Internal").ap(),
        "routed": nc.dram_tensor("routed", ((SLOTS + 1) * P, XROW), F32, kind="Internal").ap(),
    }
    with ExitStack() as ctx:
        sb = lambda n, s, d=F32: ctx.enter_context(nc.sbuf_tensor(n, s, d))
        sem = lambda n: ctx.enter_context(nc.semaphore(n))
        constants(nc, sb, sem, k)
        front(nc, sem, w, k)
        delta_rule(nc, sem, w, k)
        mixer_ffn(nc, sem, w, k)
        k["x2"] = sb("x2", [P, TILES, XROW])
        k["chosen"] = sb("chosen", [P, TILES, NE])
        cross_attention(nc, sem, w, k)
        k["w_at"] = sb("w_at", [P, SLOTS], I32)
        k["w_loads"] = sb("w_loads", [P, SLOTS], I32)
        k["w_free"] = sb("w_free", [P, NE], I32)
        dispatch(nc, sem, w, k)
        experts(nc, sem, w, k, out)


def kernel(**inputs):
    import numpy as np
    import concourse.bacc as bacc
    from concourse.bass_utils import run_bass_kernel_spmd as run

    nc = bacc.Bacc("TRN2", target_bir_lowering=False, num_devices=1)
    arrays, w = {}, {}
    for name in INPUTS:
        arrays[f"in_{name}"] = np.ascontiguousarray(inputs[name])
        w[name] = nc.dram_tensor(f"in_{name}", arrays[f"in_{name}"].shape, F32, kind="ExternalInput").ap()
    out = nc.dram_tensor("out_0", (NB, T, D), F32, kind="ExternalOutput").ap()
    build(nc, w, out)
    return run(nc, [arrays], core_ids=[0]).results[0]["out_0"]
```

```python
from contextlib import ExitStack
from functools import partial

import concourse.bass as bass
from concourse import mybir

F32 = mybir.dt.float32
I32 = mybir.dt.int32
U32 = mybir.dt.uint32
ALU = mybir.AluOpType
ACT = mybir.ActivationFunctionType
AX = mybir.AxisListType.X

P = 128
NB, T, D = 16, 256, 256
G = D // P
J = T // P
JB, TB = J, P
R, Q = 8, 4
H, HD = 16, 16
KC = 4
INNER = int(D * 2.7)
IC = -(-INNER // P)
ILAST = INNER - (IC - 1) * P
CTX = 120
NE, F1, F2 = 8, 4 * D, 2 * D
NTOK = NB * T
TILES = NTOK // P
SLOTS = (NTOK + NE * (P - 1)) // P
XROW = D + 4
WBUFS = 3
WSIZES = (G * F1, F1 // P * F2, F2 // P * D, F1, F2, D)
WPARTS = tuple(sum(WSIZES[:i]) for i in range(len(WSIZES)))
WROW, WDMAS = sum(WSIZES), len(WSIZES)
RMS_EPS, LN_EPS, GATE_BIAS = 1e-6, 1e-5, 4.0


def pipeline(eng, count, depth, body, base=0, after=0):
    first = depth - 1 + (0 if base >= 2 else 2)

    def at(step):
        items = [base + step - d if 0 <= step - d < count else None for d in range(depth)]
        body(*(None if n is None else (n, n % 2, n // 2) for n in items))

    def looped(i, c):
        c += base
        return i * 2 + c, c % 2, i + c // 2

    loops = (count - first - after) // 2
    for step in range(first):
        at(step)
    with eng.Fori(0, loops) as i:
        for u in range(2):
            body(*(looped(i, first + u - d) for d in range(depth)))
    for step in range(first + 2 * loops, count + depth - 1):
        at(step)


def since(n, k):
    return not isinstance(n, int) or n >= k


def column(vec):
    return vec.rearrange("(g p) -> p g", p=P)


def row(vec, parts=P):
    return vec.rearrange("(o n) -> o n", o=1).to_broadcast([parts, vec.shape[0]])


def scan_state(nc, sb, sem):
    s = {n: sb("s_" + n, shape) for n, shape in (
        ("q", [P, 2, TB, HD]), ("k", [P, 2, TB, HD]), ("vb", [P, 2, TB, HD]), ("o", [P, 2, HD, TB]),
        ("gate", [P, JB, 2, 2, TB]),
        ("nab", [P, 2, TB]),
        ("S", [P, 2, R, HD, HD]),
        ("outer", [P, 2, HD, HD]), ("sk", [P, 2, HD, HD]), ("so", [P, 2, Q, HD, HD]), ("pred", [P, 2, HD]), ("wv", [P, 2, HD]))}
    for n in ("sk_done", "pred_done", "w_done", "outer_done", "S_done", "o_out"):
        s[n] = sem("s_" + n)
    for n in ("S_read", "o_fold", "o_done"):
        s[n] = [sem(f"s_{n}{h}") for h in range(2)]
    return s


def scan_step(nc, dve, s, jb, c, u):
    g = c + jb * (TB // R)
    t = c * R + u
    n = lambda h: g * (2 * R) + (2 * u + h + 1)
    at = lambda x, h: x[:, h, bass.ds(t, 1)]
    before, now = s["S"][:, :, (u - 1) % R], s["S"][:, :, u]
    for h in range(2):
        dve.wait_ge(s["S_done"], n(h))
        nc.vector.tensor_tensor(s["sk"][:, h], before[:, h], at(s["k"], h).to_broadcast([P, HD, HD]), ALU.mult).then_inc(s["sk_done"], 1)
    for h in range(2):
        dve.wait_ge(s["sk_done"], n(h))
        nc.vector.tensor_reduce(s["pred"][:, h], s["sk"][:, h], AX, ALU.add).then_inc(s["pred_done"], 1)
    for h in range(2):
        dve.wait_ge(s["pred_done"], n(h))
        nc.vector.scalar_tensor_tensor(s["wv"][:, h], s["pred"][:, h], at(s["nab"], h), at(s["vb"], h).rearrange("p o v -> p (o v)"),
                                       ALU.mult, ALU.add).then_inc(s["w_done"], 1)
    for h in range(2):
        dve.wait_ge(s["w_done"], n(h))
        nc.vector.tensor_tensor(s["outer"][:, h], s["wv"][:, h].rearrange("p (v o) -> p v o", o=1).to_broadcast([P, HD, HD]),
                                at(s["k"], h).to_broadcast([P, HD, HD]), ALU.mult).then_inc(s["outer_done"], 1)
    for h in range(2):
        dve.wait_ge(s["outer_done"], n(h))
        if u % Q == 0:
            dve.wait_ge(s["S_read"][h], g * (R // Q) + (u // Q + 1))
        nc.vector.scalar_tensor_tensor(now[:, h], before[:, h], s["gate"][:, jb, h, 1, bass.ds(t, 1)], s["outer"][:, h],
                                       ALU.mult, ALU.add).then_inc(s["S_done"], 1)


def scan_steps(nc, dve, s, jb, c):
    for u in range(R):
        scan_step(nc, dve, s, jb, c, u)


def read_out(nc, pool, s, jb, c, parts=range(R // Q)):
    g = c + jb * (TB // R)
    for z in parts:
        for h in range(2):
            done = g * (R // Q) + z
            now = bass.ds(c * R + z * Q, Q)
            pool.wait_ge(s["S_done"], g * (2 * R) + (2 + 2 * (z * Q + Q - 1) + h + 1))
            pool.wait_ge(s["o_done"][h], done + 1)
            x = s["so"][:, h]
            nc.gpsimd.tensor_tensor(x, s["S"][:, h, z * Q:(z + 1) * Q],
                                    s["q"][:, h, now].rearrange("p t (o d) -> p t o d", o=1).to_broadcast([P, Q, HD, HD]),
                                    ALU.mult).then_inc(s["S_read"][h], 1)
            pool.wait_ge(s["S_read"][h], done + 3)
            for f, half in enumerate((8, 4, 2)):
                nc.gpsimd.tensor_tensor(x[:, :, :, 0:half], x[:, :, :, 0:half], x[:, :, :, half:2 * half], ALU.add).then_inc(s["o_fold"][h], 1)
                pool.wait_ge(s["o_fold"][h], done * 3 + (f + 1))
            nc.gpsimd.tensor_tensor(s["o"][:, h, :, now].rearrange("p v t -> p t v"), x[:, :, :, 0], x[:, :, :, 1],
                                    ALU.add).then_inc(s["o_done"][h], 1)


def store_o(sp, s, k, jb):
    for h in range(2):
        sp.wait_ge(s["o_done"][h], 1 + (jb + 1) * (TB // Q))
        sp.dma_start(k["o"][jb, h * (NB // 4):(h + 1) * (NB // 4)].rearrange("m g q (h d) t -> (m g q h) d t", d=HD), s["o"][:, h]).then_inc(s["o_out"], 16)


def front_and_scan(nc, sem, w, k, s):
    ident, empty = k["ident"], k["empty"]
    with ExitStack() as ctx:
        sb = lambda n, shape, d=F32: ctx.enter_context(nc.sbuf_tensor("f_" + n, shape, d))
        ps = lambda n, shape: ctx.enter_context(nc.psum_tensor("f_" + n, shape, F32))
        wqkv = sb("wqkv", [P, 3, G, D])
        wba = sb("wba", [P, G, 48])
        n1 = sb("n1", [P, G])
        cw, cb = sb("cw", [P, G, KC]), sb("cb", [P, G])
        xt = sb("xt", [P, 2, 2, D])
        sq = sb("sq", [P, 2, D])
        ss, ms, rstd = (sb(n, [P, 2, 2]) for n in ("ss", "ms", "rstd"))
        xn = sb("xn", [P, 2, 2, D])
        xT = sb("xT", [P, 2, G, 2, TB + KC - 1])
        tail = sb("tail", [P, NB // 2, G, 2, KC - 1])
        acc = sb("acc", [P, 2, G, 2, TB])
        xc = sb("xc", [P, 2, G, 2, TB])
        st = sb("st", [P, 3, G, 2 * TB])
        bst = sb("bst", [48, 2, TB])
        raw = [sb("raw_q", [P, 2, HD, TB]), sb("raw_k", [P, 2, HD, TB]), s["o"]]
        squares = sb("squares", [P, 2, HD, TB])
        lens, roots, rn = (sb(n, [P, 4, TB]) for n in ("lens", "roots", "rn"))
        alpha_bias, len_eps = sb("alpha_bias", [P, 1]), sb("len_eps", [P, 1])
        wk, wv = sb("wk", [P, G, D]), sb("wv", [P, G, D])
        bk, bkp = sb("bk", [P, G]), sb("bkp", [P, G, 2])
        bv, ones = sb("bv", [1, D]), sb("ones", [1, CTX])
        number, bit, parity = sb("number", [P, 1], I32), sb("bit", [P, 1], I32), sb("parity", [P, 2])
        ct, cT = sb("ct", [CTX, 2, D]), sb("cT", [P, 2, G, CTX])
        kE = sb("kE", [P, 2, G, 2, CTX])
        vP = sb("vP", [CTX, 2, H // 2, 2, 2 * HD])
        pT = ps("pT", [P, G, 2, TB])
        pp = ps("pp", [P, 4, G, 2 * TB])
        pc = ps("pc", [P, G, CTX])
        pk = ps("pk", [P, G, CTX])
        pv = ps("pv", [P, D])
        w_in, zeroed, set_up, n1_scaled, kv_in, parity_done, bkp_done, halo_done, empty_out = (
            sem("f_" + n) for n in ("w_in", "zeroed", "set_up", "n1_scaled", "kv_in", "parity_done", "bkp_done", "halo_done", "empty_out"))
        x_in, ct_in, kv_out = ([sem(f"f_{n}{i}") for i in range(2)] for n in ("x_in", "ct_in", "kv_out"))
        out = [sem(f"f_out_{n}") for n in "qkvg"]
        (ss_done, ms_done, rstd_done, xn_done, T_done, tail_done, xT_done, conv_done, xc_done, proj_done, evac_done) = (
            sem("f_" + n) for n in ("ss_done", "ms_done", "rstd_done", "xn_done", "T_done", "tail_done", "xT_done", "conv_done",
                                    "xc_done", "proj_done", "evac_done"))
        raw_in = [sem(f"f_raw_in_{n}") for n in "qkv"]
        gate_in, gate_done, nab_done, sq_done, fold_done, root_done, rn_done, norm_done = (
            sem("f_" + n) for n in ("gate_in", "gate_done", "nab_done", "sq_done", "fold_done", "root_done", "rn_done",
                                    "norm_done"))
        cT_done, cT_out, k_done, v_done, kE_done, vP_done = (
            sem("f_" + n) for n in ("cT_done", "cT_out", "k_done", "v_done", "kE_done", "vP_done"))
        M = NB // 2
        NW = 3 + 2 + 4
        SETUPS = 13
        TAPS = KC * G
        LENS = [(i, h) for i in (1, 0) for h in range(2)]
        block = ctx.enter_context(nc.Block())

        @block.sync
        def _(sp):
            with nc.allow_non_contiguous_dma(reason="small vectors"):
                sp.dma_start(n1[:], column(w["L0_attn_norm1_w"])).then_inc(w_in, 16)
                sp.dma_start(cb[:], column(w["L0_attn_conv_b"])).then_inc(w_in, 16)
                for g in range(G):
                    sp.dma_start(cw[:, g], w["L0_attn_conv_w"][g * P:(g + 1) * P, :]).then_inc(w_in, 16)
                for i, name in enumerate(("L0_attn_wq", "L0_attn_wk", "L0_attn_wv")):
                    sp.dma_start(wqkv[:, i], w[name].rearrange("(g p) n -> p g n", p=P)).then_inc(w_in, 16)
                sp.wait_ge(set_up, 1)
                sp.dma_start(wba[:, :, 0:H], w["L0_attn_wb"].rearrange("(g p) n -> p g n", p=P)).then_inc(w_in, 16)
                sp.dma_start(wba[:, :, 32:32 + H], w["L0_attn_wa"].rearrange("(g p) n -> p g n", p=P)).then_inc(w_in, 16)

            def load_rows(jb):
                def load(a):
                    n, s, m = a
                    if since(n, 2):
                        sp.wait_ge(xn_done, (n - 1) * 2)
                    sp.dma_start(xt[:, s], w["x"].rearrange("(m q) (j p) f -> j m p q f", q=2, p=P)[jb, bass.ds(n - jb * M, 1)]
                                 .rearrange("m p q f -> p (m q) f")).then_inc(x_in[s], 16)

                pipeline(sp, M, 1, load, base=jb * M)

            def load_raw(jb):
                if jb:
                    sp.wait_ge(norm_done, 6 * jb)
                half = lambda x, h: x[h * (M // 2):(h + 1) * (M // 2)]
                sp.wait_ge(out[3], 64 * M * (jb + 1))
                for h in range(2):
                    for i in range(2):
                        sp.dma_start(s["gate"][:, jb, h, i], half(k["gates"][jb, i], h).rearrange("m g q h t -> (m g q h) t")).then_inc(gate_in, 16)
                for i in (1, 0, 2):
                    sp.wait_ge(out[i], 16 * M * (jb + 1))
                    if i == 2 and jb:
                        store_o(sp, s, k, jb - 1)
                        sp.wait_ge(s["o_out"], 32 * jb)
                    for h in range(2):
                        sp.dma_start(raw[i][:, h], half(k["qkv"][jb, i], h).rearrange("m g q (h d) t -> (m g q h) d t", d=HD)).then_inc(raw_in[i], 16)

            load_rows(0)
            load_raw(0)
            load_rows(1)

            def contexts(a, b, c):
                if a:
                    n, slot, m = a
                    if since(n, 2):
                        sp.wait_ge(cT_done, n - 1)
                    sp.dma_start(ct[:, slot], w["ctx_1024"][bass.ds(n, 1)].rearrange("o c f -> c (o f)")).then_inc(ct_in[slot], 16)
                if c:
                    n, slot, m = c
                    sp.wait_ge(kE_done, (n + 1) * 2 * G)
                    sp.dma_start(k["kE"][bass.ds(n, 1)].rearrange("o p x -> p (o x)"), kE[:, slot].rearrange("p g a c -> p (g a c)")).then_inc(kv_out[slot], 16)
                    sp.wait_ge(vP_done, (n + 1) * 2)
                    sp.dma_start(k["vP"][bass.ds(n, 1)].rearrange("o p x -> p (o x)"), vP[:, slot].rearrange("c h a d -> c (h a d)")).then_inc(kv_out[slot], 16)

            for i in range(SLOTS + 1):
                sp.dma_start(k["routed"][i * P:(i + 1) * P, :], empty[:]).then_inc(empty_out, 16)
            pipeline(sp, NB, 3, contexts)
            load_raw(1)
            for i in range(2):
                sp.wait_ge(kv_out[i], 32 * (NB // 2))
            sp.wait_ge(empty_out, 16 * (SLOTS + 1))

        @block.gpsimd
        def _(pool):
            nc.gpsimd.memset(wba[:], 0.0).then_inc(set_up, 1)
            nc.gpsimd.memset(ident[:], 0.0).then_inc(zeroed, 1)
            nc.gpsimd.memset(empty[:], 0.0).then_inc(zeroed, 1)
            nc.gpsimd.memset(k["exponent"][:], -0.5).then_inc(set_up, 1)
            nc.gpsimd.memset(k["eps"][:, 0], D * RMS_EPS).then_inc(set_up, 1)
            nc.gpsimd.memset(k["eps"][:, 1], LN_EPS).then_inc(set_up, 1)
            nc.gpsimd.memset(xT[:], 0.0).then_inc(set_up, 1)
            nc.gpsimd.memset(alpha_bias[:], GATE_BIAS).then_inc(set_up, 1)
            nc.gpsimd.memset(len_eps[:], RMS_EPS).then_inc(set_up, 1)
            nc.gpsimd.memset(ones[:], 1.0).then_inc(set_up, 1)
            nc.gpsimd.memset(vP[:], 0.0).then_inc(set_up, 1)
            nc.gpsimd.iota(number[:], [[0, 1]], base=0, channel_multiplier=1).then_inc(set_up, 1)
            nc.gpsimd.memset(s["S"][:, :, R - 1], 0.0).then_inc(set_up, 1)
            pool.wait_ge(zeroed, 2)
            nc.gpsimd.affine_select(out=ident[:], in_=ident[:], compare_op=ALU.not_equal, fill=1.0, base=0,
                                    pattern=[[-1, P]], channel_multiplier=1).then_inc(set_up, 1)
            nc.gpsimd.iota(empty[:, D:D + 1].bitcast(I32), [[0, 1]], base=NTOK, channel_multiplier=0).then_inc(set_up, 1)
            pool.wait_ge(set_up, SETUPS)

            def inverse_rms(a):
                if a:
                    n, slot, m = a
                    pool.wait_ge(ss_done, (n + 1) * 2)
                    nc.gpsimd.tensor_tensor(ms[:, slot], ss[:, slot], k["eps"][:, 0], ALU.add).then_inc(ms_done, 1)
                    pool.wait_ge(ms_done, n + 1)
                    nc.gpsimd.tensor_tensor(rstd[:, slot], ms[:, slot], k["exponent"][:], ALU.pow).then_inc(rstd_done, 1)

            pipeline(pool, M, 1, inverse_rms)
            for h in range(2):
                pool.sem_inc(s["S_read"][h], 2)
                pool.sem_inc(s["o_done"][h], 1)
            pool.wait_ge(norm_done, 6)
            for a in range(2):
                inverse_rms((M + a, a, M // 2))
                read_out(nc, pool, s, 0, a)
            with pool.Fori(0, M // 2 - 1) as i:
                for u in range(2):
                    inverse_rms((i * 2 + (M + 2 + u), u, i + (M // 2 + 1)))
                    read_out(nc, pool, s, 0, i * 2 + (2 + u))
            with pool.Fori(M, TB // R) as c:
                read_out(nc, pool, s, 0, c)

        @block.vector
        def _(dve):
            dve.wait_ge(set_up, SETUPS)
            nc.vector.tensor_scalar(bit[:], number[:], HD.bit_length() - 1, 1, ALU.logical_shift_right, ALU.bitwise_and).then_inc(parity_done, 1)
            dve.wait_ge(parity_done, 1)
            nc.vector.tensor_copy(parity[:, 1:2], bit[:]).then_inc(parity_done, 1)
            dve.wait_ge(parity_done, 2)
            nc.vector.tensor_scalar(parity[:, 0:1], parity[:, 1:2], -1.0, 1.0, ALU.mult, ALU.add).then_inc(parity_done, 1)
            dve.wait_ge(w_in, 16 * NW)
            nc.vector.tensor_scalar(n1[:], n1[:], float(D) ** 0.5, None, ALU.mult).then_inc(n1_scaled, 1)

            def step(a, b):
                if a:
                    n, slot, m = a
                    dve.wait_ge(rstd_done, n + 1)
                    if since(n, 2):
                        dve.wait_ge(T_done, n - 1)
                    for q in range(2):
                        nc.vector.tensor_scalar(xn[:, slot, q], xt[:, slot, q], rstd[:, slot, q:q + 1], None, ALU.mult).then_inc(xn_done, 1)
                if b:
                    n, slot, m = b
                    dve.wait_ge(xT_done, (n + 1) * G)
                    if since(n, 2):
                        dve.wait_ge(xc_done, n - 1)
                    for c in range(KC):
                        for g in range(G):
                            src = xT[:, slot, g, :, c:c + TB]
                            if c == 0:
                                ins = nc.vector.tensor_scalar(acc[:, slot, g], src, cw[:, g, 0:1], cb[:, g:g + 1], ALU.mult, ALU.add)
                            else:
                                dve.wait_ge(conv_done, n * TAPS + ((c - 1) * G + g + 1))
                                ins = nc.vector.scalar_tensor_tensor(acc[:, slot, g], src, cw[:, g, c:c + 1], acc[:, slot, g], ALU.mult, ALU.add)
                            ins.then_inc(conv_done, 1)

            def prepare(jb):
                dve.wait_ge(gate_done, 2 * (jb + 1))
                beta, alpha = (s["gate"][:, jb, :, i] for i in range(2))
                if jb:
                    dve.wait_ge(s["S_done"], 2 + 2 * TB)
                nc.vector.scalar_tensor_tensor(s["nab"][:], beta, -1.0, alpha, ALU.mult, ALU.mult).then_inc(nab_done, 1)
                folds = jb * 16
                for c in range(4):
                    x = squares[:, c % 2]
                    dve.wait_ge(sq_done, jb * 4 + c + 1)
                    for half in (8, 4, 2, 1):
                        if half < 8:
                            dve.wait_ge(fold_done, folds)
                        dst = x[:, 0:half] if half > 1 else lens[:, c:c + 1]
                        nc.vector.tensor_tensor(dst, x[:, 0:half], x[:, half:2 * half], ALU.add).then_inc(fold_done, 1)
                        folds += 1
                dve.wait_ge(root_done, jb + 1)
                nc.vector.reciprocal(rn[:], roots[:]).then_inc(rn_done, 1)
                if jb:
                    for h in range(2):
                        dve.wait_ge(s["o_done"][h], 1 + jb * (TB // Q))
                dve.wait_ge(rn_done, jb + 1)
                for i, name in ((1, "k"), (0, "q"), (2, "vb")):
                    dve.wait_ge(raw_in[i], 32 * (jb + 1))
                    for h in range(2):
                        scale = s["gate"][:, jb, h, 0] if i == 2 else rn[:, LENS.index((i, h))]
                        nc.vector.tensor_tensor(s[name][:, h], raw[i][:, h].rearrange("p d t -> p t d"),
                                                scale.rearrange("p (t o) -> p t o", o=1).to_broadcast([P, TB, HD]), ALU.mult).then_inc(norm_done, 1)
                dve.wait_ge(norm_done, 6 * (jb + 1))
                dve.wait_ge(nab_done, jb + 1)

            pipeline(dve, M, 2, step)
            dve.wait_ge(kv_in, 64)
            dve.wait_ge(parity_done, 3)
            for g in range(G):
                nc.vector.tensor_scalar(bkp[:, g], parity[:], bk[:, g:g + 1], None, ALU.mult).then_inc(bkp_done, 1)
            prepare(0)
            dve.sem_inc(s["S_done"], 2)
            scan_steps(nc, dve, s, 0, 0)
            step((M, 0, M // 2), None)
            scan_steps(nc, dve, s, 0, 1)
            step((M + 1, 1, M // 2), (M, 0, M // 2))
            with dve.Fori(0, M // 2 - 1) as i:
                for u in range(2):
                    scan_steps(nc, dve, s, 0, i * 2 + (2 + u))
                    step((i * 2 + (M + 2 + u), u, i + (M // 2 + 1)), (i * 2 + (M + 1 + u), 1 - u, i + (M // 2 + u)))
            scan_steps(nc, dve, s, 0, M)
            step(None, (2 * M - 1, 1, M - 1))
            with dve.Fori(M + 1, TB // R) as c:
                scan_steps(nc, dve, s, 0, c)
            prepare(1)

        @block.scalar
        def _(act):
            with nc.allow_non_contiguous_dma(reason="small vectors"):
                for t, name in ((wk, "Wk"), (wv, "Wv")):
                    act.dma_start(t[:], w["L0_xattn_" + name].rearrange("(g p) n -> p g n", p=P)).then_inc(kv_in, 16)
                act.dma_start(bk[:], column(w["L0_xattn_bk"])).then_inc(kv_in, 16)
                act.dma_start(bv[:], row(w["L0_xattn_bv"], 1)).then_inc(kv_in, 16)
            act.wait_ge(n1_scaled, 1)
            act.wait_ge(set_up, SETUPS)

            def step(jb, a, b, c):
                if a:
                    n, slot, m = a
                    act.wait_ge(x_in[slot], m * 16 + 16)
                    for q in range(2):
                        if since(n, 1):
                            act.wait_ge(ss_done, n * 2 + q - 1)
                        nc.scalar.activation(sq[:, q], xt[:, slot, q], ACT.Square, accum_out=ss[:, slot, q:q + 1]).then_inc(ss_done, 1)
                if c:
                    n, slot, m = c
                    pair = n - jb * M
                    for i in range(3):
                        act.wait_ge(proj_done, n * 4 + (i + 1))
                        if since(n, 1):
                            act.wait_ge(out[i], n * 16)
                        nc.scalar.activation(st[:, i], pp[:, i], ACT.Copy).then_inc(evac_done, 1)
                        act.wait_ge(evac_done, n * 4 + (i + 1))
                        act.dma_start(k["qkv"][jb, i, bass.ds(pair, 1)].rearrange("m g q p t -> p (m g q) t"),
                                      st[:, i].rearrange("p g (q t) -> p (g q) t", q=2)).then_inc(out[i], 16)
                    act.wait_ge(proj_done, n * 4 + 4)
                    if since(n, 1):
                        act.wait_ge(out[3], n * 64)
                    nc.scalar.activation(bst[:].rearrange("p q t -> p (q t)"), pp[0:48, 3, 0], ACT.Copy).then_inc(evac_done, 1)
                    act.wait_ge(evac_done, n * 4 + 4)
                    for i in range(2):
                        for g in range(G):
                            act.dma_start(k["gates"][jb, i, bass.ds(pair, 1), g].rearrange("m q h t -> h (m q) t"),
                                          bst[32 * i + g * H // G:32 * i + (g + 1) * H // G]).then_inc(out[3], 16)
                if b:
                    n, slot, m = b
                    act.wait_ge(conv_done, (n + 1) * TAPS)
                    if since(n, 2):
                        act.wait_ge(proj_done, (n - 1) * 4)
                    nc.scalar.activation(xc[:, slot], acc[:, slot], ACT.Silu).then_inc(xc_done, 1)
                if a:
                    n, slot, m = a
                    act.wait_ge(T_done, n + 1)
                    if since(n, 2):
                        act.wait_ge(conv_done, (n - 1) * TAPS)
                    pair = bass.ds(n - jb * M, 1)
                    if jb:
                        nc.scalar.activation(xT[:, slot, :, :, 0:KC - 1], tail[:, pair].rearrange("p m g q t -> p (m g) q t"), ACT.Copy).then_inc(halo_done, 1)
                    for g in range(G):
                        nc.scalar.activation(xT[:, slot, g, :, KC - 1:], pT[:, g], ACT.Copy, scale=n1[:, g:g + 1]).then_inc(xT_done, 1)
                        if not jb:
                            nc.scalar.activation(tail[:, pair, g].rearrange("p m q t -> p (m q) t"), pT[:, g, :, TB - KC + 1:], ACT.Copy,
                                                 scale=n1[:, g:g + 1]).then_inc(tail_done, 1)

            def lengths(jb):
                act.wait_ge(gate_in, 64 * (jb + 1))
                beta, alpha = (s["gate"][:, jb, :, i] for i in range(2))
                nc.scalar.activation(beta, beta, ACT.Sigmoid).then_inc(gate_done, 1)
                nc.scalar.activation(alpha, alpha, ACT.Sigmoid, bias=alpha_bias[:, 0:1]).then_inc(gate_done, 1)
                for c, (i, h) in enumerate(LENS):
                    act.wait_ge(raw_in[i], 32 * (jb + 1))
                    if jb or c >= 2:
                        act.wait_ge(fold_done, (jb * 4 + c - 1) * 4)
                    nc.scalar.activation(squares[:, c % 2], raw[i][:, h], ACT.Square).then_inc(sq_done, 1)
                act.wait_ge(fold_done, (jb + 1) * 16)
                nc.scalar.activation(roots[:], lens[:], ACT.Sqrt, bias=len_eps[:, 0:1]).then_inc(root_done, 1)

            pipeline(act, M, 3, partial(step, 0))
            lengths(0)
            pipeline(act, M, 3, partial(step, 1), base=M)
            act.wait_ge(bkp_done, G)

            def keys_values(a, b):
                if a:
                    n, slot, m = a
                    act.wait_ge(cT_done, n + 1)
                    if since(n, 2):
                        act.wait_ge(v_done, n - 1)
                    nc.scalar.activation(cT[:, slot], pc[:], ACT.Copy).then_inc(cT_out, 1)
                if b:
                    n, slot, m = b
                    act.wait_ge(k_done, n + 1)
                    if since(n, 2):
                        act.wait_ge(kv_out[slot], m * 32)
                    for g in range(G):
                        for p in range(2):
                            nc.scalar.activation(kE[:, slot, g, p], pk[:, g], ACT.Identity, bias=bkp[:, g, p:p + 1],
                                                 scale=parity[:, p:p + 1]).then_inc(kE_done, 1)
                    act.wait_ge(v_done, n + 1)
                    for p in range(2):
                        nc.scalar.activation(vP[:, slot, :, p, p * HD:(p + 1) * HD],
                                             pv[0:CTX].rearrange("c (h p d) -> c h p d", p=2, d=HD)[:, :, p], ACT.Copy).then_inc(vP_done, 1)

            pipeline(act, NB, 2, keys_values)
            lengths(1)

        @block.tensor
        def _(pe):
            pe.wait_ge(set_up, SETUPS)
            pe.wait_ge(w_in, 16 * NW)

            def step(jb, a, b, c):
                if c:
                    n, slot, m = c
                    pe.wait_ge(xc_done, n + 1)
                    x = lambda g: xc[:, slot, g].rearrange("p q t -> p (q t)")
                    for i in range(4):
                        if since(n, 1):
                            pe.wait_ge(evac_done, n * 4 + (i - 3))
                        if i < 3:
                            for go in range(G):
                                for g in range(G):
                                    ins = nc.tensor.matmul(pp[:, i, go], wqkv[:, i, g, go * P:(go + 1) * P], x(g),
                                                           start=(g == 0), stop=(g == G - 1))
                        else:
                            for g in range(G):
                                ins = nc.tensor.matmul(pp[0:48, i, 0], wba[:, g], x(g), start=(g == 0), stop=(g == G - 1))
                        ins.then_inc(proj_done, 1)
                if a:
                    n, slot, m = a
                    pe.wait_ge(xn_done, (n + 1) * 2)
                    if since(n, 1):
                        pe.wait_ge(xT_done, n * G)
                        if not jb:
                            pe.wait_ge(tail_done, n * G)
                    for q in range(2):
                        for g in range(G):
                            ins = nc.tensor.transpose(pT[:, g, q], xn[:, slot, q, g * P:(g + 1) * P], ident[:])
                    ins.then_inc(T_done, 1)

            pipeline(pe, M, 3, partial(step, 0))
            pe.wait_ge(tail_done, M * G)
            pipeline(pe, M, 3, partial(step, 1), base=M)
            pe.wait_ge(kv_in, 64)

            def keys_values(a, b):
                if a:
                    n, slot, m = a
                    pe.wait_ge(ct_in[slot], m * 16 + 16)
                    if since(n, 1):
                        pe.wait_ge(cT_out, n)
                    for g in range(G):
                        ins = nc.tensor.transpose(pc[:, g], ct[:, slot, g * P:(g + 1) * P], ident[0:CTX, 0:CTX])
                    ins.then_inc(cT_done, 1)
                if b:
                    n, slot, m = b
                    pe.wait_ge(cT_out, n + 1)
                    if since(n, 1):
                        pe.wait_ge(kE_done, n * (2 * G))
                    for go in range(G):
                        for g in range(G):
                            ins = nc.tensor.matmul(pk[:, go], wk[:, g, go * P:(go + 1) * P], cT[:, slot, g], start=(g == 0), stop=(g == G - 1))
                    ins.then_inc(k_done, 1)
                    if since(n, 1):
                        pe.wait_ge(vP_done, n * 2)
                    for g in range(G):
                        nc.tensor.matmul(pv[0:CTX], cT[:, slot, g], wv[:, g], start=(g == 0), stop=False)
                    nc.tensor.matmul(pv[0:CTX], ones[:], bv[:], start=False, stop=True).then_inc(v_done, 1)

            pipeline(pe, NB, 2, keys_values)


def scan_and_post(nc, sem, w, k, s):
    ident, chosen = k["ident"], k["chosen"]
    SCALE = HD ** -0.5
    M, PAIRS, DEPTH = NB // 2, NB // 2 * JB, 4
    HALVES, HG = 4, H // 2
    with ExitStack() as ctx:
        sb = lambda n, shape, d=F32: ctx.enter_context(nc.sbuf_tensor("p_" + n, shape, d))
        ps = lambda n, shape: ctx.enter_context(nc.psum_tensor("p_" + n, shape, F32))
        w_mix, wg, wu, wd = sb("w_mix", [P, G, D]), sb("wg", [P, G, INNER]), sb("wu", [P, G, INNER]), sb("wd", [P, IC, D])
        wq, wo, wr = sb("wq", [P, G, D]), sb("wo", [P, G, D]), sb("wr", [P, G, NE])
        n2, bq = sb("n2", [P, G]), sb("bq", [P, G])
        bo, br = sb("bo", [P, D]), sb("br", [P, NE])
        rank = sb("rank", [P, 2, NE])
        oT, xt, h, xh, hn, r, x1 = (sb(n, [P, 2, D]) for n in ("oT", "xt", "h", "xh", "hn", "r", "x1"))
        hT, x1T, qT, aT, x2T = (sb(n, [P, G, 2 * P]) for n in ("hT", "x1T", "qT", "aT", "x2T"))
        ss, ms, rstd = (sb(n, [P, 2]) for n in ("ss", "ms", "rstd"))
        gate, prod = sb("gate", [P, 2, 2 * P]), sb("prod", [P, IC, 2 * P])
        st6, mv, ve, rs = sb("st6", [P, 2, 6]), sb("mv", [P, 2, 2]), sb("ve", [P, 2]), sb("rs", [P, 2])
        kE, vP = sb("kE", [P, 2, G, 2, CTX]), sb("vP", [CTX, 2, H // 2, 2, 2 * HD])
        pr = sb("pr", [P, 2, H, CTX])
        mx, sm, rc = (sb(n, [P, 2, H]) for n in ("mx", "sm", "rc"))
        prT = sb("prT", [CTX, H, 2 * P])
        xb, r2, x2 = (sb(n, [P, 2, D]) for n in ("xb", "r2", "x2"))
        st62, mv2, ve2, rs2 = sb("st62", [P, 2, 6]), sb("mv2", [P, 2, 2]), sb("ve2", [P, 2]), sb("rs2", [P, 2])
        lg, best = sb("lg", [P, 2, NE]), sb("best", [P, 2, NE])
        lmax, first = sb("lmax", [P, 2]), sb("first", [P, 2])
        pm = ps("pm", [P, 2, D])
        pT = ps("pT", [P, G, 2 * P])
        pU = ps("pU", [P, 2, 512])
        py = ps("py", [P, 2, D])
        pS = ps("pS", [P, 2, 512])
        pq = ps("pq", [P, G, 2 * P])
        gu = pU[:].rearrange("p i (u t) -> p i u t", u=2)
        pP = pU[0:CTX].rearrange("p i (x t) -> p i x t", t=P)
        scores = pS[:, :, 0:4 * CTX].rearrange("p r (x c) -> p r x c", c=CTX)
        w_in, set_up, scaled, o_in, x_in, k_in, v_in, x2_out = (
            sem("p_" + n) for n in ("w_in", "set_up", "scaled", "o_in", "x_in", "k_in", "v_in", "x2_out"))
        (mix_done, h_done, ss_done, ms_done, rstd_done, hn_done, T_done, hT_done, xh_done) = (
            sem("p_" + n) for n in ("mix_done", "h_done", "ss_done", "ms_done", "rstd_done", "hn_done", "T_done", "hT_done", "xh_done"))
        (gu_done, gate_done, prod_done, down_done, r_done, st_done, st_seen, mv_done, ve_done, rs_done, x1_done) = (
            sem("p_" + n) for n in ("gu_done", "gate_done", "prod_done", "down_done", "r_done", "st_done", "st_seen", "mv_done",
                                    "ve_done", "rs_done", "x1_done"))
        (x1T_done, x1T_out, xb_done, q_done, q_out, score_done, max_done, exp_done, rec_done, norm_done) = (
            sem("p_" + n) for n in ("x1T_done", "x1T_out", "xb_done", "q_done", "q_out", "score_done", "max_done", "exp_done",
                                    "rec_done", "norm_done"))
        (PT_done, PT_out, pv_done, pv_out, att_done, r2_done, st2_done, st2_seen, mv2_done, ve2_done, rs2_done, x2_done, x2T_done,
         x2T_out, logit_done, lg_done, lmax_done, best_done, tied_done, first_done, chosen_done) = (
            sem("p_" + n) for n in ("PT_done", "PT_out", "pv_done", "pv_out", "att_done", "r2_done", "st2_done", "st2_seen",
                                    "mv2_done", "ve2_done", "rs2_done", "x2_done", "x2T_done", "x2T_out", "logit_done", "lg_done",
                                    "lmax_done", "best_done", "tied_done", "first_done", "chosen_done"))
        NW = 6 + 6
        width = lambda i: P if i < IC - 1 else ILAST
        block = ctx.enter_context(nc.Block())

        def stages(step, depth):
            if not isinstance(step, int):
                return [step - d for d in range(depth)]
            return [step - d if 0 <= step - d < PAIRS else None for d in range(depth)]

        def steps(eng, body, depth, start=0):
            looped = max(start, depth)
            for step in range(start, looped):
                body(*stages(step, depth))
            with eng.Fori(looped, PAIRS) as step:
                body(*stages(step, depth))
            for step in range(PAIRS, PAIRS + depth - 1):
                body(*stages(step, depth))

        @block.sync
        def _(sp):
            with nc.allow_non_contiguous_dma(reason="small vectors"):
                sp.dma_start(w_mix[:], w["L0_attn_wo"].rearrange("(g p) n -> p g n", p=P)).then_inc(w_in, 16)
                sp.dma_start(n2[:], column(w["L0_attn_norm2_w"])).then_inc(w_in, 16)
                sp.dma_start(wg[:], w["L0_attn_wg"].rearrange("(g p) n -> p g n", p=P)).then_inc(w_in, 16)
                sp.dma_start(wu[:], w["L0_attn_wu"].rearrange("(g p) n -> p g n", p=P)).then_inc(w_in, 16)
                sp.dma_start(wd[:, 0:IC - 1], w["L0_attn_wd"][0:(IC - 1) * P, :].rearrange("(c p) n -> p c n", p=P)).then_inc(w_in, 16)
                sp.dma_start(wd[0:ILAST, IC - 1], w["L0_attn_wd"][(IC - 1) * P:INNER, :]).then_inc(w_in, 16)
                sp.dma_start(wq[:], w["L0_xattn_Wq"].rearrange("(g p) n -> p g n", p=P)).then_inc(w_in, 16)
                sp.dma_start(wo[:], w["L0_xattn_Wo"].rearrange("(g p) n -> p g n", p=P)).then_inc(w_in, 16)
                sp.dma_start(wr[:], w["L0_ffn_Wr"].rearrange("(g p) n -> p g n", p=P)).then_inc(w_in, 16)
                sp.dma_start(bq[:], column(w["L0_xattn_bq"])).then_inc(w_in, 16)
                sp.dma_start(bo[:], row(w["L0_xattn_bo"])).then_inc(w_in, 16)
                sp.dma_start(br[:], row(w["L0_ffn_br"])).then_inc(w_in, 16)

            def values(n, m):
                if since(n, 1):
                    sp.wait_ge(pv_done, n)
                sp.dma_start(vP[:].rearrange("c q h a d -> c q (h a d)"),
                             k["vP"].rearrange("(m q) c x -> m c q x", q=2)[bass.ds(m, 1)].rearrange("m c q x -> c (m q) x")).then_inc(v_in, 16)

            def rows(n, jb, m):
                if since(n, 1):
                    sp.wait_ge(mix_done, n)
                sp.dma_start(oT[:].rearrange("p g (q t) -> p (g q) t", q=2),
                             k["o"][jb, bass.ds(m, 1)].rearrange("m g q p t -> p (m g q) t")).then_inc(o_in, 16)
                if since(n, 1):
                    sp.wait_ge(xh_done, n)
                sp.dma_start(xt[:], w["x"].rearrange("(m q) (j p) f -> j m p q f", q=2, p=P)[jb, bass.ds(m, 1)]
                             .rearrange("m p q f -> p (m q) f")).then_inc(x_in, 16)

            def keys(n, m):
                if since(n, 1):
                    sp.wait_ge(score_done, n * HALVES)
                sp.dma_start(kE[:].rearrange("p q g a c -> p q (g a c)"),
                             k["kE"].rearrange("(m q) p x -> m p q x", q=2)[bass.ds(m, 1)].rearrange("m p q x -> p (m q) x")).then_inc(k_in, 16)

            def load(jb, step):
                a, b, c, d = stages(step, DEPTH)
                if d is not None:
                    values(d, d if not jb else place(d))
                if a is not None:
                    rows(a, jb, a - jb * M)
                if c is not None:
                    keys(c, c if not jb else place(c))

            def place(n):
                return n % M if isinstance(n, int) else n - M

            for step in range(DEPTH):
                load(0, step)
            with sp.Fori(DEPTH, M) as step:
                load(0, step)
            store_o(sp, s, k, 1)
            sp.wait_ge(s["o_out"], 64)
            for step in range(M, M + DEPTH):
                load(1, step)
            with sp.Fori(M + DEPTH, PAIRS) as step:
                load(1, step)
            for step in range(PAIRS, PAIRS + DEPTH - 1):
                load(1, step)

        @block.gpsimd
        def _(pool):
            nc.gpsimd.iota(rank[:], [[0, 2], [-1, NE]], base=NE, channel_multiplier=0,
                           allow_small_or_imprecise_dtypes=True).then_inc(set_up, 1)
            pool.wait_ge(w_in, 16 * NW)

            def biased(n):
                pool.wait_ge(x1_done, (n + 1) * 2)
                if since(n, 1):
                    pool.wait_ge(r2_done, n)
                nc.gpsimd.tensor_tensor(xb[:], x1[:], bo[:].rearrange("p (o f) -> p o f", o=1).to_broadcast([P, 2, D]), ALU.add).then_inc(xb_done, 1)

            def inverse_rms(n):
                pool.wait_ge(ss_done, (n + 1) * 2)
                nc.gpsimd.tensor_tensor(ms[:], ss[:], k["eps"][:, 0], ALU.add).then_inc(ms_done, 1)
                pool.wait_ge(ms_done, n + 1)
                if since(n, 1):
                    pool.wait_ge(hn_done, n * 2)
                nc.gpsimd.tensor_tensor(rstd[:], ms[:], k["exponent"][:], ALU.pow).then_inc(rstd_done, 1)

            def inverse_std(n, var, var_done, ve, ve_done, rs, rs_done):
                pool.wait_ge(var_done, (n + 1) * 2)
                nc.gpsimd.tensor_tensor(ve[:], var[:, :, 1], k["eps"][:, 1], ALU.add).then_inc(ve_done, 1)
                pool.wait_ge(ve_done, n + 1)
                nc.gpsimd.tensor_tensor(rs[:], ve[:], k["exponent"][:], ALU.pow).then_inc(rs_done, 1)

            def doubled(n):
                pool.wait_ge(h_done, n + 1)
                if since(n, 1):
                    pool.wait_ge(r_done, n)
                nc.gpsimd.tensor_tensor(xh[:], xt[:], h[:], ALU.add).then_inc(xh_done, 1)

            def step(a, b, c, d, chunk=None):
                if c is not None:
                    biased(c)
                if chunk is not None:
                    read_out(nc, pool, s, 1, chunk, (0,))
                if d is not None:
                    inverse_std(d, mv2, mv2_done, ve2, ve2_done, rs2, rs2_done)
                if a is not None:
                    inverse_rms(a)
                if chunk is not None:
                    read_out(nc, pool, s, 1, chunk, (1,))
                    read_out(nc, pool, s, 1, chunk + 1, (0,))
                if b is not None:
                    inverse_std(b, mv, mv_done, ve, ve_done, rs, rs_done)
                if a is not None:
                    doubled(a)
                if chunk is not None:
                    read_out(nc, pool, s, 1, chunk + 1, (1,))

            for n in range(DEPTH):
                step(*stages(n, DEPTH), n * 2)
            with pool.Fori(DEPTH, M) as n:
                step(*stages(n, DEPTH), n * 2)
            steps(pool, step, DEPTH, M)

        @block.vector
        def _(dve):
            dve.wait_ge(w_in, 16 * NW)
            dve.wait_ge(set_up, 1)
            nc.vector.tensor_scalar(n2[:], n2[:], float(D) ** 0.5, None, ALU.mult).then_inc(scaled, 1)
            nc.vector.tensor_scalar(bq[:], bq[:], SCALE, None, ALU.mult).then_inc(scaled, 1)

            def residual(n):
                dve.wait_ge(mix_done, n + 1)
                dve.wait_ge(x_in, n * 16 + 16)
                if since(n, 1):
                    dve.wait_ge(hn_done, n * 2)
                    dve.wait_ge(xh_done, n)
                nc.vector.tensor_tensor(h[:], pm[:], xt[:], ALU.add).then_inc(h_done, 1)

            def gated(n, i):
                c = width(i)
                dve.wait_ge(gate_done, n * IC + (i + 1))
                if since(n, 1):
                    dve.wait_ge(down_done, n)
                nc.vector.tensor_tensor(prod[0:c, i], gu[0:c, i % 2, 1], gate[0:c, i % 2], ALU.mult).then_inc(prod_done, 1)

            def statistics(n, r, r_done, st6, st_done, st_seen, mv, mv_done):
                dve.wait_ge(r_done, n + 1)
                for q in range(2):
                    nc.vector.bn_stats(st6[:, q], r[:, q]).then_inc(st_done, 1)
                dve.wait_ge(st_done, (n + 1) * 2)
                dve.sem_inc(st_seen, 1)
                for q in range(2):
                    nc.vector.bn_aggr(mv[:, q], st6[:, q]).then_inc(mv_done, 1)

            def mlp_out(n):
                dve.wait_ge(down_done, n + 1)
                dve.wait_ge(xh_done, n + 1)
                nc.vector.tensor_tensor(r[:], py[:], xh[:], ALU.add).then_inc(r_done, 1)
                statistics(n, r, r_done, st6, st_done, st_seen, mv, mv_done)

            def first_norm(n):
                dve.wait_ge(rs_done, n + 1)
                if since(n, 1):
                    dve.wait_ge(x1T_done, n)
                    dve.wait_ge(xb_done, n)
                for q in range(2):
                    nc.vector.tensor_scalar(x1[:, q], r[:, q], mv[:, q, 0:1], rs[:, q:q + 1], ALU.subtract, ALU.mult).then_inc(x1_done, 1)

            def maximum(n, x):
                dve.wait_ge(score_done, n * HALVES + (x + 1))
                if since(n, 1):
                    dve.wait_ge(exp_done, n * HALVES)
                nc.vector.tensor_reduce(mx[:, x // 2, x % 2 * HG:(x % 2 + 1) * HG].rearrange("p (r x) -> p r x", r=2), scores, AX, ALU.max,
                                        negate=True).then_inc(max_done, 1)

            def inverse_sums(n, q):
                dve.wait_ge(exp_done, n * HALVES + 2 * (q + 1))
                if since(n, 1):
                    dve.wait_ge(norm_done, n * 2)
                nc.vector.reciprocal(rc[:, q], sm[:, q]).then_inc(rec_done, 1)

            def attended(n):
                dve.wait_ge(att_done, n + 1)
                dve.wait_ge(xb_done, n + 1)
                nc.vector.tensor_tensor(r2[:], py[:], xb[:], ALU.add).then_inc(r2_done, 1)
                statistics(n, r2, r2_done, st62, st2_done, st2_seen, mv2, mv2_done)

            def second_norm(n):
                dve.wait_ge(rs2_done, n + 1)
                if since(n, 1):
                    dve.wait_ge(x2T_done, n)
                    dve.wait_ge(x2_out, n * 16)
                for q in range(2):
                    nc.vector.tensor_scalar(x2[:, q], r2[:, q], mv2[:, q, 0:1], rs2[:, q:q + 1], ALU.subtract, ALU.mult).then_inc(x2_done, 1)

            def logits(n):
                dve.wait_ge(logit_done, n + 1)
                nc.vector.tensor_tensor(lg[:], pq[:, :, 0:NE], br[:].rearrange("p (o e) -> p o e", o=1).to_broadcast([P, 2, NE]), ALU.add).then_inc(lg_done, 1)

            def choice(n):
                dve.wait_ge(lg_done, n + 1)
                nc.vector.tensor_reduce(lmax[:], lg[:], AX, ALU.max).then_inc(lmax_done, 1)
                dve.wait_ge(lmax_done, n + 1)
                if since(n, 1):
                    dve.wait_ge(chosen_done, n)
                nc.vector.tensor_tensor(best[:], lg[:], lmax[:].rearrange("p (j o) -> p j o", o=1).to_broadcast([P, 2, NE]), ALU.is_ge).then_inc(best_done, 1)
                dve.wait_ge(best_done, n + 1)
                nc.vector.tensor_tensor(best[:], best[:], rank[:], ALU.mult).then_inc(tied_done, 1)
                dve.wait_ge(tied_done, n + 1)
                nc.vector.tensor_reduce(first[:], best[:], AX, ALU.max).then_inc(first_done, 1)
                dve.wait_ge(first_done, n + 1)
                nc.vector.tensor_tensor(chosen[:, bass.ds(n * 2, 2)], best[:],
                                        first[:].rearrange("p (j o) -> p j o", o=1).to_broadcast([P, 2, NE]), ALU.is_equal).then_inc(chosen_done, 1)

            def step(a, b, c, d, e, scan=lambda u: None):
                scan(0)
                if e is not None:
                    logits(e)
                scan(1)
                if e is not None:
                    choice(e)
                scan(2)
                if c is not None:
                    maximum(c, 0)
                scan(3)
                scan(4)
                if c is not None:
                    maximum(c, 1)
                scan(5)
                if d is not None:
                    attended(d)
                if a is not None:
                    residual(a)
                scan(6)
                if c is not None:
                    inverse_sums(c, 0)
                    maximum(c, 2)
                scan(7)
                if d is not None:
                    second_norm(d)
                scan(8)
                if b is not None:
                    gated(b, 0)
                    gated(b, 1)
                if c is not None:
                    maximum(c, 3)
                scan(9)
                scan(10)
                if c is not None:
                    inverse_sums(c, 1)
                if b is not None:
                    gated(b, 2)
                    gated(b, 3)
                scan(11)
                scan(12)
                if b is not None:
                    gated(b, 4)
                    gated(b, 5)
                scan(13)
                scan(14)
                if b is not None:
                    mlp_out(b)
                scan(15)
                if b is not None:
                    first_norm(b)

            def beside(n):
                step(*stages(n, DEPTH + 1), lambda u: scan_step(nc, dve, s, 1, n * 2 + u // R, u % R))

            for n in range(DEPTH + 1):
                beside(n)
            with dve.Fori(DEPTH + 1, M) as n:
                beside(n)
            steps(dve, step, DEPTH + 1, M)

        @block.scalar
        def _(act):
            act.wait_ge(scaled, 2)

            def probabilities(n, q):
                for x in range(4):
                    act.wait_ge(PT_done, n * 8 + (q * 4 + x + 1))
                    if since(n, 1):
                        act.wait_ge(pv_done, n)
                    nc.scalar.activation(prT[:, x * 4:x * 4 + 4, q * P:(q + 1) * P], pP[:, x % 2], ACT.Copy).then_inc(PT_out, 1)

            def exponential(n, x):
                act.wait_ge(max_done, n * HALVES + (x + 1))
                if since(n, 1):
                    act.wait_ge(PT_done, n * 8)
                    act.wait_ge(rec_done, n * 2)
                for y in range(HG):
                    head = x % 2 * HG + y
                    ins = nc.scalar.activation(pr[:, x // 2, head], scores[:, y // 4, y % 4], ACT.Exp, bias=mx[:, x // 2, head:head + 1],
                                               accum_out=sm[:, x // 2, head:head + 1])
                ins.then_inc(exp_done, 1)

            def normalise(n, q):
                act.wait_ge(rec_done, n * 2 + (q + 1))
                for head in range(H):
                    ins = nc.scalar.activation(pr[:, q, head], pr[:, q, head], ACT.Copy, scale=rc[:, q, head:head + 1])
                ins.then_inc(norm_done, 1)

            def silu(n, i):
                c = width(i)
                act.wait_ge(gu_done, n * IC + (i + 1))
                if since(n, 1) or i >= 2:
                    act.wait_ge(prod_done, n * IC + (i - 1))
                nc.scalar.activation(gate[0:c, i % 2], gu[0:c, i % 2, 0], ACT.Silu).then_inc(gate_done, 1)

            def copied(n, done, out, used, dst, src):
                act.wait_ge(done, n + 1)
                if since(n, 1):
                    act.wait_ge(used[0], n * used[1])
                nc.scalar.activation(dst, src, ACT.Copy).then_inc(out, 1)

            def squares(n):
                act.wait_ge(h_done, n + 1)
                if since(n, 1):
                    act.wait_ge(T_done, n)
                for q in range(2):
                    nc.scalar.activation(hn[:, q], h[:, q], ACT.Square, accum_out=ss[:, q:q + 1]).then_inc(ss_done, 1)

            def normed(n):
                act.wait_ge(rstd_done, n + 1)
                for q in range(2):
                    nc.scalar.activation(hn[:, q], h[:, q], ACT.Copy, scale=rstd[:, q:q + 1]).then_inc(hn_done, 1)

            def step(a, b, c, d):
                if c is not None:
                    copied(c, x1T_done, x1T_out, (q_done, 1), x1T[:], pT[:])
                if d is not None:
                    probabilities(d, 0)
                if c is not None:
                    act.wait_ge(q_done, c + 1)
                    if since(c, 1):
                        act.wait_ge(score_done, c * HALVES)
                    for g in range(G):
                        nc.scalar.activation(qT[:, g], pq[:, g], ACT.Identity, bias=bq[:, g:g + 1], scale=SCALE).then_inc(q_out, 1)
                if d is not None:
                    probabilities(d, 1)
                if c is not None:
                    exponential(c, 0)
                if d is not None:
                    copied(d, pv_done, pv_out, (att_done, 1), aT[:], pq[:])
                if c is not None:
                    exponential(c, 1)
                    normalise(c, 0)
                if a is not None:
                    squares(a)
                if c is not None:
                    exponential(c, 2)
                if b is not None:
                    silu(b, 0)
                    silu(b, 1)
                if a is not None:
                    normed(a)
                if c is not None:
                    exponential(c, 3)
                    normalise(c, 1)
                if b is not None:
                    silu(b, 2)
                    silu(b, 3)
                if d is not None:
                    copied(d, x2T_done, x2T_out, (logit_done, 1), x2T[:], pT[:])
                    act.wait_ge(x2_done, (d + 1) * 2)
                    act.dma_start(k["x2"][bass.ds(d * 2, 2)].rearrange("q p f -> p q f"), x2[:]).then_inc(x2_out, 16)
                if b is not None:
                    silu(b, 4)
                    silu(b, 5)
                if a is not None:
                    act.wait_ge(T_done, a + 1)
                    for g in range(G):
                        nc.scalar.activation(hT[:, g], pT[:, g], ACT.Copy, scale=n2[:, g:g + 1]).then_inc(hT_done, 1)

            steps(act, step, DEPTH)
            act.wait_ge(x2_out, 16 * PAIRS)

        @block.tensor
        def _(pe):
            pe.wait_ge(w_in, 16 * NW)

            def transposed(dst, src, done):
                for q in range(2):
                    for g in range(G):
                        ins = nc.tensor.transpose(dst[:, g, q * P:(q + 1) * P], src[:, q, g * P:(g + 1) * P], ident[:])
                ins.then_inc(done, 1)

            def by_rows(dst, rows, wt, done):
                for q in range(2):
                    for g in range(G):
                        ins = nc.tensor.matmul(dst[:, q], rows[:, g, q * P:(q + 1) * P], wt[:, g], start=(g == 0), stop=(g == G - 1))
                ins.then_inc(done, 1)

            def mix(n):
                pe.wait_ge(o_in, n * 16 + 16)
                if since(n, 1):
                    pe.wait_ge(h_done, n)
                by_rows(pm, oT, w_mix, mix_done)

            def normed_rows(n):
                pe.wait_ge(hn_done, (n + 1) * 2)
                transposed(pT, hn, T_done)

            def gate_up(n, i):
                c = width(i)
                if i >= 2:
                    pe.wait_ge(prod_done, n * IC + (i - 1))
                for which, wt in enumerate((wg, wu)):
                    for g in range(G):
                        ins = nc.tensor.matmul(gu[0:c, i % 2, which], wt[:, g, i * P:i * P + c], hT[:, g], start=(g == 0), stop=(g == G - 1))
                ins.then_inc(gu_done, 1)

            def down(n):
                pe.wait_ge(prod_done, (n + 1) * IC)
                for q in range(2):
                    for i in range(IC):
                        c = width(i)
                        ins = nc.tensor.matmul(py[:, q], prod[0:c, i, q * P:(q + 1) * P], wd[0:c, i], start=(i == 0), stop=(i == IC - 1))
                ins.then_inc(down_done, 1)

            def queries(n):
                pe.wait_ge(x1T_out, n + 1)
                for go in range(G):
                    for g in range(G):
                        ins = nc.tensor.matmul(pq[:, go], wq[:, g, go * P:(go + 1) * P], x1T[:, g], start=(g == 0), stop=(g == G - 1))
                ins.then_inc(q_done, 1)

            def score(n, x):
                q = x // 2
                if x == 0:
                    pe.wait_ge(q_out, (n + 1) * G)
                    pe.wait_ge(k_in, n * 16 + 16)
                if x or since(n, 1):
                    pe.wait_ge(exp_done, n * HALVES + x)
                for i in range(2):
                    group = x % 2 * 2 + i
                    rows = slice(32 * group, 32 * group + 32)
                    for g in range(G):
                        ins = nc.tensor.matmul(pS[:, i, g * 2 * CTX:(g + 1) * 2 * CTX], qT[rows, g, q * P:(q + 1) * P],
                                               kE[rows, q, g].rearrange("p a c -> p (a c)"), start=True, stop=True)
                ins.then_inc(score_done, 1)

            def probabilities(n, q):
                pe.wait_ge(norm_done, n * 2 + (q + 1))
                for x in range(4):
                    if q or x > 1:
                        pe.wait_ge(PT_out, n * 8 + (q * 4 + x - 1))
                    for y in range(4):
                        ins = nc.tensor.transpose(pP[:, x % 2, y], pr[:, q, x * 4 + y], ident[:])
                    ins.then_inc(PT_done, 1)

            def values(n):
                pe.wait_ge(PT_out, (n + 1) * 8)
                pe.wait_ge(v_in, n * 16 + 16)
                for q in range(2):
                    for group in range(4):
                        for g in range(G):
                            for p in range(2):
                                ins = nc.tensor.matmul(pq[32 * group:32 * group + 32, g, q * P:(q + 1) * P], vP[:, q, g * 4 + group, p],
                                                       prT[:, group * 4 + g * 2 + p, q * P:(q + 1) * P], start=(p == 0), stop=(p == 1))
                ins.then_inc(pv_done, 1)

            def attention_out(n, behind):
                pe.wait_ge(pv_out, n + 1)
                if behind is not None:
                    pe.wait_ge(r_done, behind)
                by_rows(py, aT, wo, att_done)

            def routed(n):
                pe.wait_ge(x2T_out, n + 1)
                for q in range(2):
                    for g in range(G):
                        ins = nc.tensor.matmul(pq[:, q, 0:NE], x2T[:, g, q * P:(q + 1) * P], wr[:, g], start=(g == 0), stop=(g == G - 1))
                ins.then_inc(logit_done, 1)

            def step(a, b, c, d):
                if b is not None:
                    pe.wait_ge(hT_done, (b + 1) * G)
                if c is not None:
                    pe.wait_ge(x1_done, (c + 1) * 2)
                    transposed(pT, x1, x1T_done)
                if d is not None:
                    probabilities(d, 0)
                if c is not None:
                    if d is not None and since(d, 1):
                        pe.wait_ge(lg_done, d)
                    queries(c)
                if d is not None:
                    probabilities(d, 1)
                if c is not None:
                    score(c, 0)
                if d is not None:
                    if c is None and since(d, 1):
                        pe.wait_ge(lg_done, d)
                    values(d)
                if c is not None:
                    score(c, 1)
                if d is not None:
                    attention_out(d, min(d + 2, PAIRS) if isinstance(d, int) else d + 2)
                if a is not None:
                    mix(a)
                if b is not None:
                    gate_up(b, 0)
                    gate_up(b, 1)
                if c is not None:
                    score(c, 2)
                    score(c, 3)
                if b is not None:
                    gate_up(b, 2)
                    gate_up(b, 3)
                if d is not None:
                    pe.wait_ge(x2_done, (d + 1) * 2)
                    transposed(pT, x2, x2T_done)
                if b is not None:
                    gate_up(b, 4)
                    gate_up(b, 5)
                if a is not None:
                    if d is not None:
                        pe.wait_ge(x2T_out, d + 1)
                    elif c is not None:
                        pe.wait_ge(x1T_out, c + 1)
                    normed_rows(a)
                if d is not None:
                    routed(d)
                if b is not None:
                    if d is not None:
                        pe.wait_ge(r2_done, d + 1)
                    down(b)

            steps(pe, step, DEPTH)


def dispatch(nc, sem, w, k):
    chosen = k["chosen"]
    PAD = TILES // 2
    with ExitStack() as ctx:
        sb = lambda n, s, d=F32: ctx.enter_context(nc.sbuf_tensor("d_" + n, s, d))
        ps = lambda n, s: ctx.enter_context(nc.psum_tensor("d_" + n, s, F32))
        x2 = sb("x2", [P, TILES, XROW])
        before = sb("before", [P, P])
        ones = sb("ones", [P, P])
        upto = [sb(f"upto{i}", [P, PAD + TILES, NE]) for i in range(2)]
        upto_e = [sb(f"upto_e{i}", [P, NE + NE]) for i in range(2)]
        full = sb("full", [P, NE, TILES])
        needs = sb("needs", [P, NE, TILES])
        used = sb("used", [P, NE])
        start = sb("start", [P, NE])
        place = sb("place", [P, TILES, NE])
        pos = sb("pos", [P, TILES])
        pos_i = sb("pos_i", [P, TILES], U32)
        slot_no = sb("slot_no", [P, SLOTS, NE])
        passed = sb("passed", [P, SLOTS, NE])
        expert = sb("expert", [P, SLOTS])
        turn = sb("turn", [P, 2, SLOTS])
        count = ps("count", [P, 2, TILES, NE])
        made, counted, places, tables, rows_in, rows_out = (sem("d_" + n) for n in ("made", "counted", "places", "tables", "rows_in", "rows_out"))
        LOADS = 4
        block = ctx.enter_context(nc.Block())

        @block.sync
        def _(sp):
            some = TILES // LOADS
            for i in range(LOADS):
                tiles = slice(i * some, (i + 1) * some)
                sp.dma_start(x2[:, tiles, 0:D], k["x2"][tiles].rearrange("t p f -> p t f")).then_inc(rows_in, 16)

        @block.gpsimd
        def _(pool):
            nc.gpsimd.memset(before[:], 1.0).then_inc(made, 1)
            nc.gpsimd.memset(ones[:], 1.0).then_inc(made, 1)
            for i in range(2):
                nc.gpsimd.memset(upto[i][:], 0.0).then_inc(made, 1)
                nc.gpsimd.memset(upto_e[i][:], 0.0).then_inc(made, 1)
            nc.gpsimd.iota(full[:], [[0, NE], [P, TILES]], base=0, channel_multiplier=0, allow_small_or_imprecise_dtypes=True).then_inc(made, 1)
            nc.gpsimd.iota(slot_no[:], [[1, SLOTS], [0, NE]], base=0, channel_multiplier=0, allow_small_or_imprecise_dtypes=True).then_inc(made, 1)
            nc.gpsimd.memset(x2[:, :, D + 1:], 0.0).then_inc(made, 1)
            for jb in range(JB):
                nc.gpsimd.iota(x2[:, jb * NB:(jb + 1) * NB, D:D + 1].bitcast(I32), [[T, NB], [0, 1]], base=jb * TB, channel_multiplier=1).then_inc(made, 1)
            pool.wait_ge(made, 11)
            nc.gpsimd.affine_select(out=before[:], in_=before[:], compare_op=ALU.is_gt, fill=0.0, base=0,
                                    pattern=[[1, P]], channel_multiplier=-1).then_inc(made, 1)
            pool.wait_ge(places, 12)
            pool.wait_ge(rows_in, 16 * LOADS)
            for t in range(TILES):
                pool.indirect_dma_start(k["routed"], bass.IndirectOffsetOnAxis(ap=pos_i[:, t:t + 1], axis=0), x2[:, t], None).then_inc(rows_out, 16)
            pool.wait_ge(rows_out, 16 * TILES)

        @block.tensor
        def _(pe):
            pe.wait_ge(made, 12)
            every = chosen[:].rearrange("p t e -> p (t e)")
            nc.tensor.matmul(count[:, 0].rearrange("p t e -> p (t e)"), before[:], every, start=True, stop=True).then_inc(counted, 1)
            nc.tensor.matmul(count[:, 1].rearrange("p t e -> p (t e)"), ones[:], every, start=True, stop=True).then_inc(counted, 1)

        @block.vector
        def _(dve):
            of_tile = count[:, 1]
            dve.wait_ge(made, 12)
            dve.wait_ge(counted, 2)
            nc.vector.tensor_copy(upto[0][:, PAD:], of_tile).then_inc(places, 1)
            n, d = 1, 1
            while d < TILES:
                dve.wait_ge(places, n)
                src, dst = upto[(n - 1) % 2], upto[n % 2]
                nc.vector.tensor_tensor(dst[:, PAD:], src[:, PAD:], src[:, PAD - d:PAD + TILES - d], ALU.add).then_inc(places, 1)
                n, d = n + 1, 2 * d
            total = upto[(n - 1) % 2]
            dve.wait_ge(places, n)
            nc.vector.tensor_tensor(place[:], count[:, 0], total[:, PAD:], ALU.add).then_inc(places, 1)
            last = total[:, PAD + TILES - 1].rearrange("p (e o) -> p e o", o=1).to_broadcast([P, NE, TILES])
            nc.vector.tensor_tensor(needs[:], last, full[:], ALU.is_gt).then_inc(tables, 1)
            dve.wait_ge(places, n + 1)
            nc.vector.tensor_tensor(place[:], place[:], of_tile, ALU.subtract).then_inc(places, 1)
            dve.wait_ge(tables, 1)
            nc.vector.tensor_reduce(used[:], needs[:], AX, ALU.add).then_inc(tables, 1)
            dve.wait_ge(tables, 2)
            nc.vector.tensor_copy(upto_e[0][:, NE:], used[:]).then_inc(tables, 1)
            m, d = 3, 1
            while d < NE:
                dve.wait_ge(tables, m)
                src, dst = upto_e[(m - 3) % 2], upto_e[(m - 2) % 2]
                nc.vector.tensor_tensor(dst[:, NE:], src[:, NE:], src[:, NE - d:2 * NE - d], ALU.add).then_inc(tables, 1)
                m, d = m + 1, 2 * d
            end = upto_e[(m - 3) % 2][:, NE:]
            dve.wait_ge(tables, m)
            nc.vector.tensor_tensor(start[:], end, used[:], ALU.subtract).then_inc(tables, 1)
            dve.wait_ge(tables, m + 1)
            nc.vector.tensor_scalar(start[:], start[:], float(P), None, ALU.mult).then_inc(tables, 1)
            dve.wait_ge(tables, m + 2)
            dve.wait_ge(places, n + 2)
            nc.vector.tensor_tensor(place[:], place[:], start[:].rearrange("p (o e) -> p o e", o=1).to_broadcast([P, TILES, NE]),
                                    ALU.add).then_inc(places, 1)
            dve.wait_ge(places, n + 3)
            nc.vector.tensor_tensor(place[:], place[:], chosen[:], ALU.mult).then_inc(places, 1)
            dve.wait_ge(places, n + 4)
            nc.vector.tensor_reduce(pos[:], place[:], AX, ALU.add).then_inc(places, 1)
            dve.wait_ge(places, n + 5)
            nc.vector.tensor_copy(pos_i[:], pos[:]).then_inc(places, 1)
            assert n + 6 == 12
            nc.vector.tensor_tensor(passed[:], slot_no[:], end.rearrange("p (o e) -> p o e", o=1).to_broadcast([P, SLOTS, NE]),
                                    ALU.is_ge).then_inc(tables, 1)
            dve.wait_ge(tables, m + 3)
            nc.vector.tensor_reduce(expert[:], passed[:], AX, ALU.add).then_inc(tables, 1)
            dve.wait_ge(tables, m + 4)
            nc.vector.tensor_scalar(expert[:], expert[:], NE - 1.0, None, ALU.min).then_inc(tables, 1)
            dve.wait_ge(tables, m + 5)
            for i in range(2):
                nc.vector.tensor_scalar(turn[:, i], expert[:], (i + 1.0) * WBUFS, -float(WBUFS), ALU.is_ge, ALU.mult).then_inc(tables, 1)
            dve.wait_ge(tables, m + 7)
            nc.vector.tensor_tensor(turn[:, 0], turn[:, 0], turn[:, 1], ALU.add).then_inc(tables, 1)
            dve.wait_ge(tables, m + 8)
            nc.vector.tensor_tensor(turn[:, 0], turn[:, 0], expert[:], ALU.add).then_inc(tables, 1)
            dve.wait_ge(tables, m + 9)
            nc.vector.tensor_scalar(k["w_at"][:], turn[:, 0], float(WROW), None, ALU.mult).then_inc(tables, 1)
            nc.vector.tensor_scalar(k["w_loads"][:], expert[:], 16.0 * WDMAS, 16.0 * WDMAS, ALU.mult, ALU.add).then_inc(tables, 1)
            nc.vector.tensor_scalar(k["w_free"][:], end, 1.0, None, ALU.add).then_inc(tables, 1)
            dve.wait_ge(tables, m + 12)


def experts(nc, sem, w, k, out):
    ident = k["ident"]
    C1, C2, HALF = F1 // P, F2 // P, F1 // 2
    W1_AT, W2_AT, W3_AT, B1_AT, B2_AT, B3_AT = WPARTS
    with ExitStack() as ctx:
        sb = lambda n, s, d=F32: ctx.enter_context(nc.sbuf_tensor("e_" + n, s, d))
        ps = lambda n, s: ctx.enter_context(nc.psum_tensor("e_" + n, s, F32))
        wt = sb("wt", [P, WBUFS * WROW])
        xt = sb("xt", [P, 2, XROW])
        token = sb("token", [P, 2, 1], U32)
        xb = sb("xb", [P, 2, D])
        xT = sb("xT", [P, G, P])
        h1 = sb("h1", [P, 2, HALF])
        g1 = sb("g1", [P, 2, C1 // 2, P])
        h2 = sb("h2", [P, F2])
        g2 = sb("g2", [P, C2, P])
        r = sb("r", [P, D])
        st6 = sb("st6", [P, 6])
        mv = sb("mv", [P, 2])
        ve, rs = sb("ve", [P, 1]), sb("rs", [P, 1])
        y = sb("y", [P, 2, D])
        pX = ps("pX", [P, G, P])
        ph1 = ps("ph1", [P, 2, HALF])
        pT1 = ps("pT1", [P, 2, C1 // 2, P])
        ph2 = ps("ph2", [P, F2])
        pT2 = ps("pT2", [P, C2, P])
        py = ps("py", [P, D])
        names = ("w_in", "w_ready", "xT_done", "xT_out", "token_kept", "xb_done", "h1_done", "h1_out", "T1_done", "g1_done", "h2_done",
                 "h2_out", "T2_done", "g2_done", "y_done", "r_done", "st_done", "st_seen", "mv_done", "ve_done", "rs_done", "row_done",
                 "row_seen")
        (w_in, w_ready, xT_done, xT_out, token_kept, xb_done, h1_done, h1_out, T1_done, g1_done, h2_done, h2_out, T2_done, g2_done,
         y_done, r_done, st_done, st_seen, mv_done, ve_done, rs_done, row_done, row_seen) = (sem("e_" + n) for n in names)
        x_in, row_out = ([sem(f"e_{n}{s}") for s in range(2)] for n in ("x_in", "row_out"))
        block = ctx.enter_context(nc.Block())

        def entry(eng, table, n, top):
            return eng.value_load(k[table][0:1, bass.ds(n, 1)], min_val=0, max_val=top)

        def weights(eng, n):
            return entry(eng, "w_at", n, (WBUFS - 1) * WROW)

        def loads(eng, n):
            return entry(eng, "w_loads", n, 16 * WDMAS * NE)

        @block.sync
        def _(sp):
            for e in range(NE):
                if e >= WBUFS:
                    sp.wait_ge(r_done, entry(sp, "w_free", e - WBUFS, SLOTS + 1))
                if e >= 1:
                    sp.wait_ge(w_in, 16 * WDMAS * e)
                at = lambda off, n: wt[:, e % WBUFS * WROW + off:e % WBUFS * WROW + off + n]
                for off, name, c, n in ((W1_AT, "W1", G, F1), (W2_AT, "W2", C1, F2), (W3_AT, "W3", C2, D)):
                    sp.dma_start(at(off, c * n).rearrange("p (c n) -> p c n", c=c),
                                 w["L0_ffn_" + name][e].rearrange("(c p) n -> p c n", p=P)).then_inc(w_in, 16)
                for off, name, n in ((B1_AT, "b1", F1), (B2_AT, "b2", F2), (B3_AT, "b3", D)):
                    sp.dma_start(at(off, n), row(w["L0_ffn_" + name][e])).then_inc(w_in, 16)
            sp.wait_ge(w_in, 16 * WDMAS * NE)

        @block.gpsimd
        def _(pool):
            def step(a, b):
                if a:
                    n, s, m = a
                    at = weights(pool, n)
                    pool.wait_ge(w_in, loads(pool, n))
                    pool.wait_ge(x_in[s], m * 16 + 16)
                    if since(n, 2):
                        pool.wait_ge(r_done, n)
                    pool.sem_inc(w_ready, 1)
                    nc.gpsimd.tensor_tensor(xb[:, s], xt[:, s, 0:D], wt[:, bass.ds(at + B3_AT, D)], ALU.add).then_inc(xb_done, 1)
                if b:
                    n, s, m = b
                    pool.wait_ge(mv_done, n + 1)
                    nc.gpsimd.tensor_tensor(ve[:], mv[:, 1:2], k["eps"][:, 1, 0:1], ALU.add).then_inc(ve_done, 1)
                    pool.wait_ge(ve_done, n + 1)
                    nc.gpsimd.tensor_tensor(rs[:], ve[:], k["exponent"][:, 0:1], ALU.pow).then_inc(rs_done, 1)
                    pool.wait_ge(row_done, n + 1)
                    pool.sem_inc(row_seen, 1)
                    pool.indirect_dma_start(out.rearrange("b t f -> (b t) f"), bass.IndirectOffsetOnAxis(ap=token[:, s], axis=0),
                                            y[:, s], None, bounds_check=NTOK - 1, oob_is_err=False).then_inc(row_out[s], 16)

            pipeline(pool, SLOTS, 2, step)
            for s in range(2):
                pool.wait_ge(row_out[s], 16 * len(range(s, SLOTS, 2)))

        @block.vector
        def _(dve):
            dve.sem_inc(r_done, 1)

            def step(a, b):
                if a:
                    n, s, m = a
                    dve.wait_ge(x_in[s], m * 16 + 16)
                    if since(n, 2):
                        dve.wait_ge(row_out[s], m * 16)
                    nc.vector.tensor_copy(token[:, s], xt[:, s, D:D + 1].bitcast(U32)).then_inc(token_kept, 1)
                    dve.wait_ge(xT_done, n + 1)
                    if since(n, 1):
                        dve.wait_ge(h1_done, n * 2)
                    nc.vector.tensor_copy(xT[:], pX[:]).then_inc(xT_out, 1)
                if b:
                    n, s, m = b
                    at = weights(dve, n)
                    dve.wait_ge(h2_done, n + 1)
                    if since(n, 1):
                        dve.wait_ge(T2_done, n)
                    nc.vector.tensor_tensor(h2[:], ph2[:], wt[:, bass.ds(at + B2_AT, F2)], ALU.add).then_inc(h2_out, 1)
                if a:
                    n, s, m = a
                    at = weights(dve, n)
                    for q in range(2):
                        dve.wait_ge(h1_done, n * 2 + q + 1)
                        if since(n, 1):
                            dve.wait_ge(T1_done, n * 2 + q - 1)
                        nc.vector.tensor_tensor(h1[:, q], ph1[:, q], wt[:, bass.ds(at + (B1_AT + q * HALF), HALF)], ALU.add).then_inc(h1_out, 1)
                if b:
                    n, s, m = b
                    dve.wait_ge(y_done, n + 1)
                    dve.wait_ge(xb_done, n + 1)
                    nc.vector.tensor_tensor(r[:], py[:], xb[:, s], ALU.add).then_inc(r_done, 1)
                    dve.wait_ge(r_done, n + 2)
                    nc.vector.bn_stats(st6[:], r[:]).then_inc(st_done, 1)
                    dve.wait_ge(st_done, n + 1)
                    dve.sem_inc(st_seen, 1)
                    nc.vector.bn_aggr(mv[:], st6[:]).then_inc(mv_done, 1)
                    dve.wait_ge(rs_done, n + 1)
                    nc.vector.tensor_scalar(y[:, s], r[:], mv[:, 0:1], rs[:, 0:1], ALU.subtract, ALU.mult).then_inc(row_done, 1)

            pipeline(dve, SLOTS, 2, step)

        @block.scalar
        def _(act):
            def load(n, s):
                act.dma_start(xt[:, s], k["routed"][bass.ds(n * P, P), :]).then_inc(x_in[s], 16)

            load(0, 0)

            def step(a, b):
                if a:
                    n, s, m = a
                    if not (isinstance(n, int) and n == SLOTS - 1):
                        if since(n, 1):
                            act.wait_ge(xT_done, n)
                            act.wait_ge(xb_done, n)
                            act.wait_ge(token_kept, n)
                        load(n + 1, 1 - s)
                if b:
                    n, s, m = b
                    act.wait_ge(T2_done, n + 1)
                    if since(n, 1):
                        act.wait_ge(y_done, n)
                    nc.scalar.activation(g2[:], pT2[:], ACT.Gelu).then_inc(g2_done, 1)
                if a:
                    n, s, m = a
                    for q in range(2):
                        act.wait_ge(T1_done, n * 2 + q + 1)
                        if since(n, 1):
                            act.wait_ge(h2_done, n)
                        nc.scalar.activation(g1[:, q], pT1[:, q], ACT.Gelu).then_inc(g1_done, 1)

            pipeline(act, SLOTS, 2, step, after=1)

        @block.tensor
        def _(pe):
            def step(a, b):
                if a:
                    n, s, m = a
                    pe.wait_ge(x_in[s], m * 16 + 16)
                    if since(n, 1):
                        pe.wait_ge(xT_out, n)
                    for g in range(G):
                        ins = nc.tensor.transpose(pX[:, g], xt[:, s, g * P:(g + 1) * P], ident[:])
                    ins.then_inc(xT_done, 1)
                if b:
                    n, s, m = b
                    at_b = weights(pe, n)
                    if since(n, 1):
                        pe.wait_ge(h2_out, n)
                    for c in range(C1):
                        pe.wait_ge(g1_done, n * 2 + c // (C1 // 2) + 1)
                        ins = nc.tensor.matmul(ph2[:], g1[:, c // (C1 // 2), c % (C1 // 2)], wt[:, bass.ds(at_b + (W2_AT + c * F2), F2)],
                                               start=(c == 0), stop=(c == C1 - 1))
                    ins.then_inc(h2_done, 1)
                if a:
                    n, s, m = a
                    at_a = weights(pe, n)
                    pe.wait_ge(w_in, loads(pe, n))
                    pe.wait_ge(xT_out, n + 1)
                    for q in range(2):
                        if since(n, 1):
                            pe.wait_ge(h1_out, n * 2 + q - 1)
                        for g in range(G):
                            ins = nc.tensor.matmul(ph1[:, q], xT[:, g], wt[:, bass.ds(at_a + (W1_AT + g * F1 + q * HALF), HALF)],
                                                   start=(g == 0), stop=(g == G - 1))
                        ins.then_inc(h1_done, 1)
                if b:
                    n, s, m = b
                    pe.wait_ge(h2_out, n + 1)
                    if since(n, 1):
                        pe.wait_ge(g2_done, n)
                    for c in range(C2):
                        ins = nc.tensor.transpose(pT2[:, c], h2[:, c * P:(c + 1) * P], ident[:])
                    ins.then_inc(T2_done, 1)
                if a:
                    transposed(a, 0)
                if b:
                    n, s, m = b
                    pe.wait_ge(g2_done, n + 1)
                    if since(n, 1):
                        pe.wait_ge(r_done, n + 1)
                    for c in range(C2):
                        ins = nc.tensor.matmul(py[:], g2[:, c], wt[:, bass.ds(at_b + (W3_AT + c * D), D)], start=(c == 0), stop=(c == C2 - 1))
                    ins.then_inc(y_done, 1)
                if a:
                    transposed(a, 1)

            def transposed(a, q):
                n, s, m = a
                pe.wait_ge(h1_out, n * 2 + q + 1)
                if since(n, 1):
                    pe.wait_ge(g1_done, n * 2 + q - 1)
                for c in range(C1 // 2):
                    ins = nc.tensor.transpose(pT1[:, q, c], h1[:, q, c * P:(c + 1) * P], ident[:])
                ins.then_inc(T1_done, 1)

            pipeline(pe, SLOTS, 2, step)


INPUTS = ["x", "ctx_1024", "L0_attn_norm1_w", "L0_attn_norm2_w", "L0_attn_conv_w", "L0_attn_conv_b", "L0_attn_wq",
          "L0_attn_wk", "L0_attn_wv", "L0_attn_wb", "L0_attn_wa", "L0_attn_wo", "L0_attn_wg", "L0_attn_wu", "L0_attn_wd",
          "L0_xattn_Wq", "L0_xattn_bq", "L0_xattn_Wk", "L0_xattn_bk", "L0_xattn_Wv", "L0_xattn_bv", "L0_xattn_Wo",
          "L0_xattn_bo", "L0_ffn_Wr", "L0_ffn_br", "L0_ffn_W1", "L0_ffn_b1", "L0_ffn_W2", "L0_ffn_b2", "L0_ffn_W3",
          "L0_ffn_b3"]


def build(nc, w, out):
    k = {
        "qkv": nc.dram_tensor("qkv", (JB, 3, NB // 2, G, 2, P, TB), F32, kind="Internal").ap(),
        "gates": nc.dram_tensor("gates", (JB, 2, NB // 2, G, 2, H // G, TB), F32, kind="Internal").ap(),
        "o": nc.dram_tensor("o", (JB, NB // 2, G, 2, P, TB), F32, kind="Internal").ap(),
        "kE": nc.dram_tensor("kE", (NB, P, G * 2 * CTX), F32, kind="Internal").ap(),
        "vP": nc.dram_tensor("vP", (NB, CTX, H * 2 * HD), F32, kind="Internal").ap(),
        "x2": nc.dram_tensor("x2", (TILES, P, D), F32, kind="Internal").ap(),
        "routed": nc.dram_tensor("routed", ((SLOTS + 1) * P, XROW), F32, kind="Internal").ap(),
    }
    with ExitStack() as ctx:
        sb = lambda n, s, d=F32: ctx.enter_context(nc.sbuf_tensor(n, s, d))
        sem = lambda n: ctx.enter_context(nc.semaphore(n))
        k["ident"] = sb("ident", [P, P])
        k["exponent"] = sb("exponent", [P, 2])
        k["eps"] = sb("eps", [P, 2, 2])
        k["empty"] = sb("empty", [P, XROW])
        k["chosen"] = sb("chosen", [P, TILES, NE])
        with ExitStack() as scan:
            s = scan_state(nc, lambda n, shape: scan.enter_context(nc.sbuf_tensor(n, shape, F32)), sem)
            front_and_scan(nc, sem, w, k, s)
            scan_and_post(nc, sem, w, k, s)
        k["w_at"] = sb("w_at", [P, SLOTS], I32)
        k["w_loads"] = sb("w_loads", [P, SLOTS], I32)
        k["w_free"] = sb("w_free", [P, NE], I32)
        dispatch(nc, sem, w, k)
        experts(nc, sem, w, k, out)


def kernel(**inputs):
    import numpy as np
    import concourse.bacc as bacc
    from concourse.bass_utils import run_bass_kernel_spmd as run

    nc = bacc.Bacc("TRN2", target_bir_lowering=False, num_devices=1)
    arrays, w = {}, {}
    for name in INPUTS:
        arrays[f"in_{name}"] = np.ascontiguousarray(inputs[name])
        w[name] = nc.dram_tensor(f"in_{name}", arrays[f"in_{name}"].shape, F32, kind="ExternalInput").ap()
    out = nc.dram_tensor("out_0", (NB, T, D), F32, kind="ExternalOutput").ap()
    build(nc, w, out)
    return run(nc, [arrays], core_ids=[0]).results[0]["out_0"]
```

```python
import math
from contextlib import ExitStack
from functools import partial

import concourse.bass as bass
from concourse import mybir

F32 = mybir.dt.float32
I32 = mybir.dt.int32
U32 = mybir.dt.uint32
ALU = mybir.AluOpType
ACT = mybir.ActivationFunctionType
AX = mybir.AxisListType.X

P = 128
NB, T, D = 16, 256, 256
G = D // P
J = T // P
JB, TB = J, P
R, Q, V = 8, 4, 4
CHUNKS = TB // R
H, HD = 16, 16
KC = 4
INNER = int(D * 2.7)
IC = -(-INNER // P)
ILAST = INNER - (IC - 1) * P
CTX = 120
NE, F1, F2 = 8, 4 * D, 2 * D
NTOK = NB * T
TILES = NTOK // P
SLOTS = (NTOK + NE * (P - 1)) // P
REGION = NTOK + P
XROW = D + 4
WBUFS = 3
WSIZES = (G * F1, F1 // P * F2, F2 // P * D, F1, F2, D)
WPARTS = tuple(sum(WSIZES[:i]) for i in range(len(WSIZES)))
WROW = sum(WSIZES)
WDMAS = len(WSIZES) + 1
RMS_EPS, LN_EPS, GATE_BIAS = 1e-6, 1e-5, 4.0


def pipeline(eng, count, depth, body, base=0, after=0, between={}):
    first = depth - 1 + (0 if base >= 2 else 2)

    def at(step):
        items = [base + step - d if 0 <= step - d < count else None for d in range(depth)]
        body(*(None if n is None else (n, n % 2, n // 2) for n in items))

    def looped(i, c):
        c += base
        return i * 2 + c, c % 2, i + c // 2

    loops = (count - first - after) // 2
    for step in range(first):
        at(step)
    with eng.Fori(0, loops) as i:
        for u in range(2):
            body(*(looped(i, first + u - d) for d in range(depth)))
    for step in range(first + 2 * loops, count + depth - 1):
        at(step)
        between.get(step, lambda: None)()


def since(n, k):
    return not isinstance(n, int) or n >= k


def shaped(flat, dims):
    names = "abcdef"[:len(dims)]
    return flat.rearrange(f"p ({' '.join(names)}) -> p {' '.join(names)}", **dict(zip(names, dims)))


def column(vec):
    return vec.rearrange("(g p) -> p g", p=P)


def row(vec, parts=P):
    return vec.rearrange("(o n) -> o n", o=1).to_broadcast([parts, vec.shape[0]])


def scan_state(arena, sem):
    s = {n: shaped(arena(math.prod(dims)), dims) for n, dims in (
        ("q", (2, TB, HD)), ("k", (2, TB, HD)),
        ("vo", (2, HD, TB)),
        ("gate", (JB, 2, 2, TB)),
        ("nab", (JB, 2, TB)),
        ("S", (2, R, HD, HD)),
        ("kn", (2, R, HD)),
        ("sk", (2, V, HD, HD + 1)),
        ("w", (2, HD)), ("outer", (2, HD, HD)), ("so", (2, Q, HD, HD)))}
    for n in ("kn_done", "v_done", "sk_done", "w_done", "outer_done", "S_done"):
        s[n] = sem("s_" + n)
    for n in ("S_read", "o_fold", "o_done", "o_out"):
        s[n] = [sem(f"s_{n}{h}") for h in range(2)]
    return s


def next_keys(nc, s, jb, t, u, n):
    nc.vector.tensor_tensor(s["kn"][:, :, u:u + n], s["k"][:, :, bass.ds(t, n)],
                            s["nab"][:, jb, :, bass.ds(t, n)].rearrange("p h (t o) -> p h t o", o=1).to_broadcast([P, 2, n, HD]),
                            ALU.mult).then_inc(s["kn_done"], 1)


def next_values(nc, s, jb, vo, t, u, n):
    nc.vector.tensor_tensor(s["sk"][:, :, u:u + n, :, HD], vo[:, :, :, bass.ds(t, n)].rearrange("p h d t -> p h t d"),
                            s["gate"][:, jb, :, 0, bass.ds(t, n)].rearrange("p h (t o) -> p h t o", o=1).to_broadcast([P, 2, n, HD]),
                            ALU.mult).then_inc(s["v_done"], 1)


def scan_start(nc, s, jb, vo):
    next_keys(nc, s, jb, 0, 0, R)
    next_values(nc, s, jb, vo, 0, 0, V)


def scan_step(nc, dve, s, jb, vo, c, u, last=False):
    g = c + jb * CHUNKS
    t = c * R + u
    n = lambda h: g * (2 * R) + (2 * u + h + 1)
    first = isinstance(c, int) and c == 0
    keys = jb * (2 * CHUNKS - 1) + c * 2
    values = jb * (4 * CHUNKS - 1) + c * 4
    before, now = s["S"][:, :, (u - 1) % R], s["S"][:, :, u]
    for h in range(2):
        dve.wait_ge(s["S_done"], n(h))
        if h == 0 and u % 4 == 0:
            dve.wait_ge(s["kn_done"], keys + (1 if u or first else 0))
        nc.vector.tensor_tensor(s["sk"][:, h, u % V, :, 0:HD], before[:, h], s["kn"][:, h, u:u + 1].to_broadcast([P, HD, HD]),
                                ALU.mult).then_inc(s["sk_done"], 1)
    for h in range(2):
        dve.wait_ge(s["sk_done"], n(h))
        if h == 0 and u % 2 == 0:
            dve.wait_ge(s["v_done"], values + (max(u // 2, 1) if first else u // 2))
        nc.vector.tensor_reduce(s["w"][:, h], s["sk"][:, h, u % V], AX, ALU.add).then_inc(s["w_done"], 1)
    for h in range(2):
        dve.wait_ge(s["w_done"], n(h))
        nc.vector.tensor_tensor(s["outer"][:, h], s["w"][:, h].rearrange("p (v o) -> p v o", o=1).to_broadcast([P, HD, HD]),
                                s["k"][:, h, bass.ds(t, 1)].to_broadcast([P, HD, HD]), ALU.mult).then_inc(s["outer_done"], 1)
    if u % 2 and not (last and u > V):
        next_values(nc, s, jb, vo, t + (V - 1), (u - 1) % V, 2)
    if u % 4 == 3 and not last:
        next_keys(nc, s, jb, t + (R - 3), u - 3, 4)
    for h in range(2):
        dve.wait_ge(s["outer_done"], n(h))
        if u % Q == 0:
            dve.wait_ge(s["S_read"][h], g * (R // Q) + (u // Q + 1))
        nc.vector.scalar_tensor_tensor(now[:, h], before[:, h], s["gate"][:, jb, h, 1, bass.ds(t, 1)], s["outer"][:, h],
                                       ALU.mult, ALU.add).then_inc(s["S_done"], 1)


def scan_chunk(nc, dve, s, jb, vo, c, last=False):
    for u in range(R):
        scan_step(nc, dve, s, jb, vo, c, u, last)


def read_out(nc, pool, s, jb, vo, c, z, h):
    g = c + jb * CHUNKS
    done = g * (R // Q) + z
    now = bass.ds(c * R + z * Q, Q)
    pool.wait_ge(s["S_done"], g * (2 * R) + (2 + 2 * (z * Q + Q - 1) + h + 1))
    pool.wait_ge(s["o_done"][h], done + 1)
    x = s["so"][:, h]
    nc.gpsimd.tensor_tensor(x, s["S"][:, h, z * Q:(z + 1) * Q],
                            s["q"][:, h, now].rearrange("p t (o d) -> p t o d", o=1).to_broadcast([P, Q, HD, HD]),
                            ALU.mult).then_inc(s["S_read"][h], 1)
    pool.wait_ge(s["S_read"][h], done + 3)
    for f, half in enumerate((8, 4, 2)):
        nc.gpsimd.tensor_tensor(x[:, :, :, 0:half], x[:, :, :, 0:half], x[:, :, :, half:2 * half], ALU.add).then_inc(s["o_fold"][h], 1)
        pool.wait_ge(s["o_fold"][h], done * 3 + (f + 1))
    nc.gpsimd.tensor_tensor(vo[:, h, :, now].rearrange("p v t -> p t v"), x[:, :, :, 0], x[:, :, :, 1],
                            ALU.add).then_inc(s["o_done"][h], 1)


def store_o(sp, s, k, jb, vo, h):
    sp.wait_ge(s["o_done"][h], 1 + (jb + 1) * (TB // Q))
    sp.dma_start(k["o"][jb, h * (NB // 4):(h + 1) * (NB // 4)].rearrange("m g q (h d) t -> (m g q h) d t", d=HD), vo[:, h]).then_inc(s["o_out"][h], 16)


def front_and_scan(nc, sem, w, k, s, arena):
    ident = k["ident"]
    with ExitStack() as ctx:
        sb = lambda n, shape, d=F32: ctx.enter_context(nc.sbuf_tensor("f_" + n, shape, d))
        ps = lambda n, shape: ctx.enter_context(nc.psum_tensor("f_" + n, shape, F32))
        wqkv = sb("wqkv", [P, 3, G, D])
        wba = sb("wba", [P, G, 48])
        n1 = sb("n1", [P, G])
        cw, cb = sb("cw", [P, G, KC]), sb("cb", [P, G])
        xt = sb("xt", [P, 2, 2, D])
        ss, ms, rstd = (sb(n, [P, 2, 2]) for n in ("ss", "ms", "rstd"))
        xn = sb("xn", [P, 2, 2, D])
        xT = sb("xT", [P, 2, G, 2, TB + KC - 1])
        tail = sb("tail", [P, NB // 2, G, 2, KC - 1])
        acc = sb("acc", [P, G, 2, TB])
        wkv = sb("wkv", [P, 4 * D])
        taps = wkv[:].rearrange("p (c g f) -> p c g f", c=KC, g=G)
        xc = sb("xc", [P, 2, G, 2, TB])
        st = sb("st", [P, 3, G, 2 * TB])
        bst = sb("bst", [48, 2, TB])
        raw_q, raw_k, vo = (sb(n, [P, 2, HD, TB]) for n in ("raw_q", "raw_k", "vo"))
        values = [vo, s["vo"]]
        squares = shaped(arena(HD * TB), (HD, TB))
        lens, roots, rn = shaped(arena(4 * TB), (2, 2, TB)), sb("roots", [P, 2, 2, TB]), sb("rn", [P, 2, 2, TB])
        alpha_bias, len_eps = sb("alpha_bias", [P, 1]), sb("len_eps", [P, 1])
        wk, wv = (wkv[:, i * G * D:(i + 1) * G * D].rearrange("p (g n) -> p g n", g=G) for i in range(2))
        bk, bkp = sb("bk", [P, G]), sb("bkp", [P, G, 2])
        bv, ones = sb("bv", [1, D]), sb("ones", [1, CTX])
        number, bit, parity = sb("number", [P, 1], I32), sb("bit", [P, 1], I32), sb("parity", [P, 2])
        ct, cT = sb("ct", [CTX, 2, D]), sb("cT", [P, 2, G, CTX])
        kE = shaped(arena(2 * G * 2 * CTX), (2, G, 2, CTX))
        vP = sb("vP", [CTX, 2, H // 2, 2, 2 * HD])
        pT = ps("pT", [P, G, 2, TB])
        pp = ps("pp", [P, 4, G, 2 * TB])
        pa = ps("pa", [P, G, 2 * TB])
        pc = ps("pc", [P, G, CTX])
        pk = pa[:, :, 0:CTX]
        pv = ps("pv", [P, D])
        small_in, w_in, zeroed, set_up, n1_scaled, kv_in, taps_done, parity_done, bkp_done, halo_done = (
            sem("f_" + n) for n in ("small_in", "w_in", "zeroed", "set_up", "n1_scaled", "kv_in", "taps_done", "parity_done", "bkp_done", "halo_done"))
        x_in, ct_in, kv_out = ([sem(f"f_{n}{i}") for i in range(2)] for n in ("x_in", "ct_in", "kv_out"))
        out = [sem(f"f_out_{n}") for n in "qkv"]
        gates_out = [sem(f"f_gates_out{jb}") for jb in range(JB)]
        (ss_done, ms_done, rstd_done, xn_done, T_done, tail_done, xT_done, conv_done, xc_done, proj_done, evac_done) = (
            sem("f_" + n) for n in ("ss_done", "ms_done", "rstd_done", "xn_done", "T_done", "tail_done", "xT_done", "conv_done",
                                    "xc_done", "proj_done", "evac_done"))
        raw_in = {n: [sem(f"f_raw_in_{n}{h}") for h in range(2)] for n in "kqv"}
        gate_in = [sem(f"f_gate_in{h}") for h in range(2)]
        gate_done, nab_done, sq_done, fold_done, root_done, rn_done, norm_done = (
            sem("f_" + n) for n in ("gate_done", "nab_done", "sq_done", "fold_done", "root_done", "rn_done",
                                    "norm_done"))
        cT_done, cT_out, k_done, v_done, kE_done, vP_done = (
            sem("f_" + n) for n in ("cT_done", "cT_out", "k_done", "v_done", "kE_done", "vP_done"))
        M = NB // 2
        NSMALL, NW = 4, 5
        SETUPS = 12
        TAPS = KC * G
        block = ctx.enter_context(nc.Block())

        def store_gates(eng, jb, n):
            eng.wait_ge(evac_done, n * 4 + 4)
            for i in range(2):
                for g in range(G):
                    eng.dma_start(k["gates"][jb, i, bass.ds(n - jb * M, 1), g].rearrange("m q h t -> h (m q) t"),
                                  bst[32 * i + g * H // G:32 * i + (g + 1) * H // G]).then_inc(gates_out[jb], 16)

        @block.sync
        def _(sp):
            def load_rows(jb):
                def load(a):
                    n, s, m = a
                    if since(n, 2):
                        sp.wait_ge(xn_done, (n - 1) * 2)
                    sp.dma_start(xt[:, s], w["x"].rearrange("(m q) (j p) f -> j m p q f", q=2, p=P)[jb, bass.ds(n - jb * M, 1)]
                                 .rearrange("m p q f -> p (m q) f")).then_inc(x_in[s], 16)
                    if isinstance(n, int) and n == 1:
                        load_weights()

                pipeline(sp, M, 1, load, base=jb * M)

            def load_weights():
                for i, name in enumerate(("L0_attn_wq", "L0_attn_wk", "L0_attn_wv")):
                    sp.dma_start(wqkv[:, i], w[name].rearrange("(g p) n -> p g n", p=P)).then_inc(w_in, 16)
                sp.wait_ge(set_up, 1)
                with nc.allow_non_contiguous_dma(reason="small vectors"):
                    sp.dma_start(wba[:, :, 0:H], w["L0_attn_wb"].rearrange("(g p) n -> p g n", p=P)).then_inc(w_in, 16)
                    sp.dma_start(wba[:, :, 32:32 + H], w["L0_attn_wa"].rearrange("(g p) n -> p g n", p=P)).then_inc(w_in, 16)
                    sp.wait_ge(small_in, 16 * NSMALL)
                    sp.dma_start(bk[:], column(w["L0_xattn_bk"])).then_inc(small_in, 16)
                    sp.dma_start(bv[:], row(w["L0_xattn_bv"], 1)).then_inc(small_in, 16)

            def load_raw(jb, h):
                pairs = M * jb + M // 2 * (h + 1)
                half = lambda x: x[h * (M // 2):(h + 1) * (M // 2)]
                if jb:
                    sp.wait_ge(norm_done, 4 * jb)
                for i, name, dst in ((1, "k", raw_k), (0, "q", raw_q), (3, None, None), (2, "v", values[jb])):
                    if i == 3:
                        sp.wait_ge(gates_out[jb], 64 * (pairs - M * jb))
                        for x in range(2):
                            sp.dma_start(s["gate"][:, jb, h, x], half(k["gates"][jb, x]).rearrange("m g q h t -> (m g q h) t")).then_inc(gate_in[h], 16)
                    else:
                        sp.wait_ge(out[i], 16 * pairs)
                        sp.dma_start(dst[:, h], half(k["qkv"][jb, i]).rearrange("m g q (h d) t -> (m g q h) d t", d=HD)).then_inc(raw_in[name][h], 16)

            load_rows(0)
            for h in range(2):
                load_raw(0, h)
            load_rows(1)
            sp.wait_ge(conv_done, 2 * M * TAPS)
            for t, name in ((wk, "Wk"), (wv, "Wv")):
                sp.dma_start(t, w["L0_xattn_" + name].rearrange("(g p) n -> p g n", p=P)).then_inc(kv_in, 16)

            def contexts(a, b, c):
                if a:
                    n, slot, m = a
                    if since(n, 2):
                        sp.wait_ge(cT_done, n - 1)
                    sp.dma_start(ct[:, slot], w["ctx_1024"][bass.ds(n, 1)].rearrange("o c f -> c (o f)")).then_inc(ct_in[slot], 16)
                if c:
                    n, slot, m = c
                    sp.wait_ge(kE_done, (n + 1) * 2 * G)
                    sp.dma_start(k["kE"][bass.ds(n, 1)].rearrange("o p x -> p (o x)"), kE[:, slot].rearrange("p g a c -> p (g a c)")).then_inc(kv_out[slot], 16)
                    sp.wait_ge(vP_done, (n + 1) * 2)
                    sp.dma_start(k["vP"][bass.ds(n, 1)].rearrange("o p x -> p (o x)"), vP[:, slot].rearrange("c h a d -> c (h a d)")).then_inc(kv_out[slot], 16)

            pipeline(sp, NB, 3, contexts)
            for h in range(2):
                load_raw(1, h)
            for i in range(2):
                sp.wait_ge(kv_out[i], 32 * (NB // 2))
            for h in range(2):
                store_o(sp, s, k, 0, values[0], h)

        @block.gpsimd
        def _(pool):
            nc.gpsimd.memset(wba[:], 0.0).then_inc(set_up, 1)
            nc.gpsimd.memset(ident[:], 0.0).then_inc(zeroed, 1)
            nc.gpsimd.memset(k["exponent"][:], -0.5).then_inc(set_up, 1)
            nc.gpsimd.memset(k["eps"][:, 0], D * RMS_EPS).then_inc(set_up, 1)
            nc.gpsimd.memset(k["eps"][:, 1], LN_EPS).then_inc(set_up, 1)
            nc.gpsimd.memset(xT[:], 0.0).then_inc(set_up, 1)
            nc.gpsimd.memset(alpha_bias[:], GATE_BIAS).then_inc(set_up, 1)
            nc.gpsimd.memset(len_eps[:], RMS_EPS).then_inc(set_up, 1)
            nc.gpsimd.memset(ones[:], 1.0).then_inc(set_up, 1)
            nc.gpsimd.memset(vP[:], 0.0).then_inc(set_up, 1)
            nc.gpsimd.iota(number[:], [[0, 1]], base=0, channel_multiplier=1).then_inc(set_up, 1)
            nc.gpsimd.memset(s["S"][:, :, R - 1], 0.0).then_inc(set_up, 1)
            pool.wait_ge(zeroed, 1)
            nc.gpsimd.affine_select(out=ident[:], in_=ident[:], compare_op=ALU.not_equal, fill=1.0, base=0,
                                    pattern=[[-1, P]], channel_multiplier=1).then_inc(set_up, 1)
            pool.wait_ge(set_up, SETUPS)

            def inverse_rms(a):
                if a:
                    n, slot, m = a
                    pool.wait_ge(ss_done, (n + 1) * 2)
                    nc.gpsimd.tensor_tensor(ms[:, slot], ss[:, slot], k["eps"][:, 0], ALU.add).then_inc(ms_done, 1)
                    pool.wait_ge(ms_done, n + 1)
                    nc.gpsimd.tensor_tensor(rstd[:, slot], ms[:, slot], k["exponent"][:], ALU.pow).then_inc(rstd_done, 1)

            def first_block(a, b, c, d):
                inverse_rms(a)
                if d:
                    store_gates(pool, 0, d[0])

            pipeline(pool, M, 4, first_block)
            for h in range(2):
                pool.sem_inc(s["S_read"][h], 2)
                pool.sem_inc(s["o_done"][h], 1)
            pool.wait_ge(norm_done, 4)

            def outputs(c):
                for z in range(R // Q):
                    for h in range(2):
                        read_out(nc, pool, s, 0, values[0], c, z, h)

            for a in range(2):
                inverse_rms((M + a, a, M // 2))
                outputs(a)
            with pool.Fori(0, M // 2 - 1) as i:
                for u in range(2):
                    inverse_rms((i * 2 + (M + 2 + u), u, i + (M // 2 + 1)))
                    outputs(i * 2 + (2 + u))
            with pool.Fori(M, CHUNKS) as c:
                outputs(c)

        @block.vector
        def _(dve):
            dve.wait_ge(set_up, SETUPS)
            nc.vector.tensor_scalar(bit[:], number[:], HD.bit_length() - 1, 1, ALU.logical_shift_right, ALU.bitwise_and).then_inc(parity_done, 1)
            dve.wait_ge(parity_done, 1)
            nc.vector.tensor_copy(parity[:, 1:2], bit[:]).then_inc(parity_done, 1)
            dve.wait_ge(parity_done, 2)
            nc.vector.tensor_scalar(parity[:, 0:1], parity[:, 1:2], -1.0, 1.0, ALU.mult, ALU.add).then_inc(parity_done, 1)
            dve.wait_ge(small_in, 16 * NSMALL)
            nc.vector.tensor_scalar(n1[:], n1[:], float(D) ** 0.5, None, ALU.mult).then_inc(n1_scaled, 1)

            def step(a, b):
                if b:
                    n, slot, m = b
                    dve.wait_ge(xT_done, (n + 1) * G)
                    if since(n, 1):
                        dve.wait_ge(xc_done, n)
                    for c in range(KC):
                        for g in range(G):
                            src = xT[:, slot, g, :, c:c + TB]
                            if c == 0:
                                ins = nc.vector.tensor_scalar(acc[:, g], src, cw[:, g, 0:1], cb[:, g:g + 1], ALU.mult, ALU.add)
                            else:
                                dve.wait_ge(conv_done, n * TAPS + ((c - 1) * G + g + 1))
                                ins = nc.vector.scalar_tensor_tensor(acc[:, g], src, cw[:, g, c:c + 1], acc[:, g], ALU.mult, ALU.add)
                            ins.then_inc(conv_done, 1)
                if a:
                    n, slot, m = a
                    dve.wait_ge(rstd_done, n + 1)
                    if since(n, 2):
                        dve.wait_ge(T_done, n - 1)
                    for q in range(2):
                        nc.vector.tensor_scalar(xn[:, slot, q], xt[:, slot, q], rstd[:, slot, q:q + 1], None, ALU.mult).then_inc(xn_done, 1)

            def lengths(jb, h):
                p = jb * 2 + h

                def gates():
                    dve.wait_ge(gate_done, 2 * (p + 1))
                    beta, alpha = (s["gate"][:, jb, h, i] for i in range(2))
                    nc.vector.scalar_tensor_tensor(s["nab"][:, jb, h], beta, -1.0, alpha, ALU.mult, ALU.mult).then_inc(nab_done, 1)

                def sums(i):
                    folds = (p * 2 + i) * 4
                    dve.wait_ge(sq_done, p * 2 + i + 1)
                    for half in (8, 4, 2, 1):
                        if half < 8:
                            dve.wait_ge(fold_done, folds)
                        dst = squares[:, 0:half] if half > 1 else lens[:, h, i:i + 1]
                        nc.vector.tensor_tensor(dst, squares[:, 0:half], squares[:, half:2 * half], ALU.add).then_inc(fold_done, 1)
                        folds += 1

                def inverse():
                    dve.wait_ge(root_done, p + 1)
                    if jb:
                        dve.wait_ge(norm_done, 4)
                    nc.vector.reciprocal(rn[:, h], roots[:, h]).then_inc(rn_done, 1)

                return partial(sums, 0), partial(sums, 1), inverse, gates

            def normalise(jb, h, i):
                dst, src, name = ((s["k"], raw_k, "k"), (s["q"], raw_q, "q"))[i]
                dve.wait_ge(raw_in[name][h], 16 * (jb + 1))
                dve.wait_ge(rn_done, jb * 2 + h + 1)
                nc.vector.tensor_tensor(dst[:, h], src[:, h].rearrange("p d t -> p t d"),
                                        rn[:, h, i].rearrange("p (t o) -> p t o", o=1).to_broadcast([P, TB, HD]), ALU.mult).then_inc(norm_done, 1)

            keys, queries, inverse, gates = lengths(0, 0)
            pipeline(dve, M, 2, step, between={M - 1: keys, M: queries})
            dve.wait_ge(small_in, 16 * (NSMALL + 2))
            dve.wait_ge(parity_done, 3)
            for g in range(G):
                nc.vector.tensor_scalar(bkp[:, g], parity[:], bk[:, g:g + 1], None, ALU.mult).then_inc(bkp_done, 1)
            inverse()
            for i in range(2):
                normalise(0, 0, i)
            gates()
            keys, queries, inverse, gates = lengths(0, 1)
            keys()
            queries()
            inverse()
            for i in range(2):
                normalise(0, 1, i)
            gates()
            dve.sem_inc(s["S_done"], 2)
            for h in range(2):
                dve.wait_ge(raw_in["v"][h], 16)
            dve.wait_ge(nab_done, 2)
            dve.wait_ge(norm_done, 4)
            scan_start(nc, s, 0, values[0])
            scan_chunk(nc, dve, s, 0, values[0], 0)
            with dve.Fori(1, CHUNKS - 2) as c:
                scan_chunk(nc, dve, s, 0, values[0], c)
            for h in range(2):
                parts = list(lengths(1, h))
                for u in range(R):
                    scan_step(nc, dve, s, 0, values[0], CHUNKS - 2 + h, u, last=h == 1)
                    if u % 2:
                        parts.pop(0)()
            dve.wait_ge(s["S_done"], 2 + 2 * TB)
            for h in range(2):
                normalise(1, h, 0)
            for h in range(2):
                dve.wait_ge(s["S_read"][h], 2 + TB // Q)
                normalise(1, h, 1)
            for h in range(2):
                dve.wait_ge(raw_in["v"][h], 32)
            dve.wait_ge(nab_done, 4)
            dve.wait_ge(norm_done, 8)
            scan_start(nc, s, 1, values[1])

        @block.scalar
        def _(act):
            with nc.allow_non_contiguous_dma(reason="small vectors"):
                act.dma_start(n1[:], column(w["L0_attn_norm1_w"])).then_inc(small_in, 16)
                act.dma_start(cb[:], column(w["L0_attn_conv_b"])).then_inc(small_in, 16)
                for g in range(G):
                    act.dma_start(cw[:, g], w["L0_attn_conv_w"][g * P:(g + 1) * P, :]).then_inc(small_in, 16)
            act.wait_ge(n1_scaled, 1)
            act.wait_ge(set_up, SETUPS)

            def step(jb, a, b, c):
                if a:
                    n, slot, m = a
                    act.wait_ge(x_in[slot], m * 16 + 16)
                    if since(n, 2):
                        act.wait_ge(T_done, n - 1)
                    for q in range(2):
                        nc.scalar.activation(xn[:, slot, q], xt[:, slot, q], ACT.Square, accum_out=ss[:, slot, q:q + 1]).then_inc(ss_done, 1)
                if c:
                    projected(jb, c, 0)
                if a and jb:
                    n, slot, m = a
                    act.wait_ge(rstd_done, n + 1)
                    for q in range(2):
                        nc.scalar.activation(xn[:, slot, q], xt[:, slot, q], ACT.Copy, scale=rstd[:, slot, q:q + 1]).then_inc(xn_done, 1)
                if b:
                    n, slot, m = b
                    act.wait_ge(conv_done, (n + 1) * TAPS)
                    if since(n, 2):
                        act.wait_ge(proj_done, (n - 1) * 4)
                    if jb:
                        for g in range(G):
                            nc.scalar.activation(xc[:, slot, g].rearrange("p q t -> p (q t)"), pa[:, g], ACT.Silu, bias=cb[:, g:g + 1]).then_inc(xc_done, 1)
                    else:
                        nc.scalar.activation(xc[:, slot], acc[:], ACT.Silu).then_inc(xc_done, 1)
                if c:
                    projected(jb, c, 1)
                if a:
                    n, slot, m = a
                    act.wait_ge(T_done, n + 1)
                    if since(n, 2):
                        act.wait_ge(conv_done, (n - 1) * TAPS)
                    pair = bass.ds(n - jb * M, 1)
                    if jb:
                        nc.scalar.activation(xT[:, slot, :, :, 0:KC - 1], tail[:, pair].rearrange("p m g q t -> p (m g) q t"), ACT.Copy).then_inc(halo_done, 1)
                    for g in range(G):
                        nc.scalar.activation(xT[:, slot, g, :, KC - 1:], pT[:, g], ACT.Copy, scale=n1[:, g:g + 1]).then_inc(xT_done, 1)
                        if not jb:
                            nc.scalar.activation(tail[:, pair, g].rearrange("p m q t -> p (m q) t"), pT[:, g, :, TB - KC + 1:], ACT.Copy,
                                                 scale=n1[:, g:g + 1]).then_inc(tail_done, 1)
                if c:
                    projected(jb, c, 2)
                    gates(jb, c)

            def projected(jb, c, i):
                n, slot, m = c
                act.wait_ge(proj_done, n * 4 + (i + 1))
                if since(n, 1):
                    act.wait_ge(out[i], n * 16)
                nc.scalar.activation(st[:, i], pp[:, i], ACT.Copy).then_inc(evac_done, 1)
                act.wait_ge(evac_done, n * 4 + (i + 1))
                act.dma_start(k["qkv"][jb, i, bass.ds(n - jb * M, 1)].rearrange("m g q p t -> p (m g q) t"),
                              st[:, i].rearrange("p g (q t) -> p (g q) t", q=2)).then_inc(out[i], 16)

            def gates(jb, c):
                n, slot, m = c
                act.wait_ge(proj_done, n * 4 + 4)
                if isinstance(n, int) and n == M:
                    act.wait_ge(gates_out[0], n * 64)
                elif since(n, 1):
                    act.wait_ge(gates_out[jb], (n - jb * M) * 64)
                nc.scalar.activation(bst[:].rearrange("p q t -> p (q t)"), pp[0:48, 3, 0], ACT.Copy).then_inc(evac_done, 1)
                if jb:
                    store_gates(act, jb, n)

            def lengths(jb, h):
                p = jb * 2 + h

                def gates():
                    act.wait_ge(gate_in[h], 32 * (jb + 1))
                    beta, alpha = (s["gate"][:, jb, h, i] for i in range(2))
                    nc.scalar.activation(beta, beta, ACT.Sigmoid).then_inc(gate_done, 1)
                    nc.scalar.activation(alpha, alpha, ACT.Sigmoid, bias=alpha_bias[:, 0:1]).then_inc(gate_done, 1)

                def square(i):
                    name, src = (("k", raw_k), ("q", raw_q))[i]
                    act.wait_ge(raw_in[name][h], 16 * (jb + 1))
                    if p or i:
                        act.wait_ge(fold_done, (p * 2 + i) * 4)
                    nc.scalar.activation(squares[:], src[:, h], ACT.Square).then_inc(sq_done, 1)

                def root():
                    act.wait_ge(fold_done, (p + 1) * 8)
                    nc.scalar.activation(roots[:, h], lens[:, h], ACT.Sqrt, bias=len_eps[:, 0:1]).then_inc(root_done, 1)

                return partial(square, 0), partial(square, 1), root, gates

            keys, queries, root, set_gates = lengths(0, 0)
            pipeline(act, M, 3, partial(step, 0), after=2, between={M - 2: keys, M - 1: queries, M: root})
            for part in (set_gates, *lengths(0, 1)):
                part()
            for c in range(KC):
                for g in range(G):
                    nc.scalar.activation(taps[:, c, g], ident[:], ACT.Copy, scale=cw[:, g, c:c + 1]).then_inc(taps_done, 1)
            pipeline(act, M, 3, partial(step, 1), base=M)
            act.wait_ge(bkp_done, G)

            def keys_values(a, b):
                if a:
                    n, slot, m = a
                    act.wait_ge(cT_done, n + 1)
                    if since(n, 2):
                        act.wait_ge(v_done, n - 1)
                    nc.scalar.activation(cT[:, slot], pc[:], ACT.Copy).then_inc(cT_out, 1)
                if b:
                    n, slot, m = b
                    act.wait_ge(k_done, n + 1)
                    if since(n, 2):
                        act.wait_ge(kv_out[slot], m * 32)
                    for g in range(G):
                        for p in range(2):
                            nc.scalar.activation(kE[:, slot, g, p], pk[:, g], ACT.Identity, bias=bkp[:, g, p:p + 1],
                                                 scale=parity[:, p:p + 1]).then_inc(kE_done, 1)
                    act.wait_ge(v_done, n + 1)
                    for p in range(2):
                        nc.scalar.activation(vP[:, slot, :, p, p * HD:(p + 1) * HD],
                                             pv[0:CTX].rearrange("c (h p d) -> c h p d", p=2, d=HD)[:, :, p], ACT.Copy).then_inc(vP_done, 1)

            pipeline(act, NB, 2, keys_values)
            for h in range(2):
                for part in lengths(1, h):
                    part()

        @block.tensor
        def _(pe):
            pe.wait_ge(set_up, SETUPS)

            def step(jb, a, b, c_):
                if c_:
                    projections(c_, (0, 1), jb)
                if a:
                    n, slot, m = a
                    pe.wait_ge(xn_done, (n + 1) * 2)
                    if since(n, 1):
                        pe.wait_ge(xT_done, n * G)
                        if not jb:
                            pe.wait_ge(tail_done, n * G)
                    for q in range(2):
                        for g in range(G):
                            ins = nc.tensor.transpose(pT[:, g, q], xn[:, slot, q, g * P:(g + 1) * P], ident[:])
                    ins.then_inc(T_done, 1)
                if b and jb:
                    n, slot, m = b
                    pe.wait_ge(xT_done, (n + 1) * G)
                    if isinstance(n, int) and n == M:
                        pe.wait_ge(taps_done, TAPS)
                    if isinstance(n, int) and n == M:
                        pe.wait_ge(conv_done, M * TAPS)
                    else:
                        pe.wait_ge(xc_done, M + (n - M) * G)
                    for g in range(G):
                        for c in range(KC):
                            nc.tensor.matmul(pa[:, g], taps[:, c, g], xT[:, slot, g, :, c:c + TB], start=(c == 0),
                                             stop=(c == KC - 1)).then_inc(conv_done, 1)
                if c_:
                    projections(c_, (2, 3), jb)

            def projections(x, which, jb):
                n, slot, m = x
                if isinstance(n, int) and n == 0:
                    pe.wait_ge(w_in, 16 * NW)
                pe.wait_ge(xc_done, M + (n - M + 1) * G if jb else n + 1)
                x = lambda g: xc[:, slot, g].rearrange("p q t -> p (q t)")
                for i in which:
                    if since(n, 1):
                        pe.wait_ge(evac_done, n * 4 + (i - 3))
                    if i < 3:
                        for go in range(G):
                            for g in range(G):
                                ins = nc.tensor.matmul(pp[:, i, go], wqkv[:, i, g, go * P:(go + 1) * P], x(g),
                                                       start=(g == 0), stop=(g == G - 1))
                    else:
                        for g in range(G):
                            ins = nc.tensor.matmul(pp[0:48, i, 0], wba[:, g], x(g), start=(g == 0), stop=(g == G - 1))
                    ins.then_inc(proj_done, 1)

            pipeline(pe, M, 3, partial(step, 0))
            pe.wait_ge(tail_done, M * G)
            pipeline(pe, M, 3, partial(step, 1), base=M)
            pe.wait_ge(kv_in, 32)
            pe.wait_ge(small_in, 16 * (NSMALL + 2))
            pe.wait_ge(xc_done, M + M * G)

            def keys_values(a, b):
                if a:
                    n, slot, m = a
                    pe.wait_ge(ct_in[slot], m * 16 + 16)
                    if since(n, 1):
                        pe.wait_ge(cT_out, n)
                    for g in range(G):
                        ins = nc.tensor.transpose(pc[:, g], ct[:, slot, g * P:(g + 1) * P], ident[0:CTX, 0:CTX])
                    ins.then_inc(cT_done, 1)
                if b:
                    n, slot, m = b
                    pe.wait_ge(cT_out, n + 1)
                    if since(n, 1):
                        pe.wait_ge(kE_done, n * (2 * G))
                    for go in range(G):
                        for g in range(G):
                            ins = nc.tensor.matmul(pk[:, go], wk[:, g, go * P:(go + 1) * P], cT[:, slot, g], start=(g == 0), stop=(g == G - 1))
                    ins.then_inc(k_done, 1)
                    if since(n, 1):
                        pe.wait_ge(vP_done, n * 2)
                    for g in range(G):
                        nc.tensor.matmul(pv[0:CTX], cT[:, slot, g], wv[:, g], start=(g == 0), stop=False)
                    nc.tensor.matmul(pv[0:CTX], ones[:], bv[:], start=False, stop=True).then_inc(v_done, 1)

            pipeline(pe, NB, 2, keys_values)


def scan_and_post(nc, sem, w, k, s, arena):
    ident, before, ones, total = k["ident"], k["before"], k["ones"], k["total"]
    SCALE = HD ** -0.5
    M, STAGES = NB // 2, "abfcde"
    DEPTH = len(STAGES)
    HALVES, HG = 4, H // 2
    PLAN = (1, 1, 1, 2, 2, 2, 2, 2, 1, 1, 1)
    AGAIN = M + 3
    with ExitStack() as ctx:
        sb = lambda n, shape, d=F32: ctx.enter_context(nc.sbuf_tensor("p_" + n, shape, d))
        ps = lambda n, shape: ctx.enter_context(nc.psum_tensor("p_" + n, shape, F32))
        w_mix, wg, wu, wd = sb("w_mix", [P, G, D]), sb("wg", [P, G, INNER]), sb("wu", [P, G, INNER]), sb("wd", [P, IC, D])
        wq, wo, wr = sb("wq", [P, G, D]), sb("wo", [P, G, D]), sb("wr", [P, G, NE])
        n2, bq = sb("n2", [P, G]), sb("bq", [P, G])
        bo, br = sb("bo", [P, D]), sb("br", [P, NE])
        rank = sb("rank", [P, 2, NE])
        oT, xt, h, hn, r, x1 = (sb(n, [P, 2, D]) for n in ("oT", "xt", "h", "hn", "r", "x1"))
        xh, kept = sb("xh", [P, 2, D]), sb("kept", [P, 2, D])
        hT, x1T, qT, aT, x2T = (sb(n, [P, G, 2 * P]) for n in ("hT", "x1T", "qT", "aT", "x2T"))
        ss, ms, rstd = (sb(n, [P, 2]) for n in ("ss", "ms", "rstd"))
        gate, prod = sb("gate", [P, IC, 2 * P]), sb("prod", [P, IC, 2 * P])
        st6, mv, ve, rs = sb("st6", [P, 2, 6]), sb("mv", [P, 2, 2]), sb("ve", [P, 2]), sb("rs", [P, 2])
        kE, vP = sb("kE", [P, 2, G, 2, CTX]), sb("vP", [CTX, 2, H // 2, 2, 2 * HD])
        pr = shaped(arena(2 * H * CTX), (2, H, CTX))
        mx, sm, rc = (sb(n, [P, 2, H]) for n in ("mx", "sm", "rc"))
        prT = sb("prT", [CTX, H, 2 * P])
        xb, r2 = (sb(n, [P, 2, D]) for n in ("xb", "r2"))
        x2 = sb("x2", [P, 2, XROW])
        st62, mv2, ve2, rs2 = sb("st62", [P, 2, 6]), sb("mv2", [P, 2, 2]), sb("ve2", [P, 2]), sb("rs2", [P, 2])
        scaled_mean, shift = sb("scaled_mean", [P, 2, 2]), sb("shift", [P, 2, 2])
        lg, best, chosen, place = (sb(n, [P, 2, NE]) for n in ("lg", "best", "chosen", "place"))
        lmax, first, pos, pos_i = sb("lmax", [P, 2]), sb("first", [P, 2]), sb("pos", [P, 2]), sb("pos_i", [P, 2], U32)
        pm = ps("pm", [P, 2, D])
        pT = ps("pT", [P, G, 2 * P])
        py = ps("py", [P, 2, D])
        pX = ps("pX", [P, 2, 2, 512])
        pq = ps("pq", [P, G, 2 * P])
        gu = lambda i: pX[:, i // 2 % 2, i % 2].rearrange("p (u t) -> p u t", u=2)
        pP = lambda j: pX[0:CTX, j // 2 % 2, j % 2].rearrange("p (x t) -> p x t", t=P)
        scores = lambda x: pX[:, x % 2, :, 0:4 * CTX].rearrange("p r (x c) -> p r x c", c=CTX)
        places = pT[:, 0, 0:2 * NE]
        w_in, set_up, scaled, o_in, x_in, k_in, v_in = (
            sem("p_" + n) for n in ("w_in", "set_up", "scaled", "o_in", "x_in", "k_in", "v_in"))
        (mix_done, h_done, ss_done, ms_done, rstd_done, hn_done, T_done, hT_done, xh_done, kept_done) = (
            sem("p_" + n) for n in ("mix_done", "h_done", "ss_done", "ms_done", "rstd_done", "hn_done", "T_done", "hT_done", "xh_done",
                                    "kept_done"))
        (gu_done, gate_done, prod_done, down_done, r_done, st_done, mv_done, ve_done, rs_done, x1_done) = (
            sem("p_" + n) for n in ("gu_done", "gate_done", "prod_done", "down_done", "r_done", "st_done", "mv_done",
                                    "ve_done", "rs_done", "x1_done"))
        (x1T_done, x1T_out, xb_done, q_done, q_out, score_done, max_done, exp_done, rec_done, norm_done) = (
            sem("p_" + n) for n in ("x1T_done", "x1T_out", "xb_done", "q_done", "q_out", "score_done", "max_done", "exp_done",
                                    "rec_done", "norm_done"))
        (PT_done, PT_out, pv_done, pv_out, att_done, r2_done, st2_done, mv2_done, ve2_done, rs2_done, x2_done, x2T_done,
         x2T_out, logit_done) = (
            sem("p_" + n) for n in ("PT_done", "PT_out", "pv_done", "pv_out", "att_done", "r2_done", "st2_done", 
                                    "mv2_done", "ve2_done", "rs2_done", "x2_done", "x2T_done", "x2T_out", "logit_done"))
        lg_done, choice, count_done, position, pos_out, number_done, row_out = (
            sem("p_" + n) for n in ("lg_done", "choice", "count_done", "position", "pos_out", "number_done", "row_out"))
        MAX, BEST, TIED, FIRST, CHOSEN, COUNTED = range(1, 7)
        PLACED, SUMMED = 1, 3
        chose = lambda e, what=0: 1 + e * COUNTED + what
        placed = lambda e, what=0: 1 + e * SUMMED + what
        NW = 6 + 6
        width = lambda i: P if i < IC - 1 else ILAST
        block = ctx.enter_context(nc.Block())

        def at(jb, step):
            if not isinstance(step, int):
                return STAGES, *(step - (d + jb * (AGAIN - M)) for d in range(DEPTH))
            since_start = lambda d: (step - d, step - d - AGAIN)
            return ("".join(x for d, x in enumerate(STAGES) if any(0 <= n < M for n in since_start(d))),
                    *(sum(min(max(n, 0), M) for n in since_start(d)) for d in range(DEPTH)))

        def late(jb, n):
            return n >= M if isinstance(n, int) else jb

        def steps(eng, body):
            first = 0
            for jb, start in enumerate((0, AGAIN)):
                for step in range(first, start + DEPTH - 1):
                    body(None, step)
                with eng.Fori(start + DEPTH - 1, start + M) as step:
                    body(jb, step)
                first = start + M
            for step in range(first, first + DEPTH - 1):
                body(None, step)

        def chunks(jb, step):
            if not isinstance(step, int):
                return [] if jb else [(step - (DEPTH - 1)) * 2 + (sum(PLAN[:DEPTH - 1]) + i) for i in range(2)]
            return [sum(PLAN[:step]) + i for i in range(PLAN[step] if step < len(PLAN) else 0)]

        assert sum(PLAN) == CHUNKS

        def stored(eng):
            for h in range(2):
                eng.wait_ge(s["o_out"][h], 16)

        @block.sync
        def _(sp):
            stored(sp)
            with nc.allow_non_contiguous_dma(reason="small vectors"):
                sp.dma_start(w_mix[:], w["L0_attn_wo"].rearrange("(g p) n -> p g n", p=P)).then_inc(w_in, 16)
                sp.dma_start(n2[:], column(w["L0_attn_norm2_w"])).then_inc(w_in, 16)
                sp.dma_start(bq[:], column(w["L0_xattn_bq"])).then_inc(w_in, 16)
                sp.dma_start(wg[:], w["L0_attn_wg"].rearrange("(g p) n -> p g n", p=P)).then_inc(w_in, 16)
                sp.dma_start(wu[:], w["L0_attn_wu"].rearrange("(g p) n -> p g n", p=P)).then_inc(w_in, 16)
                sp.dma_start(wd[:, 0:IC - 1], w["L0_attn_wd"][0:(IC - 1) * P, :].rearrange("(c p) n -> p c n", p=P)).then_inc(w_in, 16)
                sp.dma_start(wd[0:ILAST, IC - 1], w["L0_attn_wd"][(IC - 1) * P:INNER, :]).then_inc(w_in, 16)
                sp.dma_start(wq[:], w["L0_xattn_Wq"].rearrange("(g p) n -> p g n", p=P)).then_inc(w_in, 16)
                sp.dma_start(wo[:], w["L0_xattn_Wo"].rearrange("(g p) n -> p g n", p=P)).then_inc(w_in, 16)
                sp.dma_start(wr[:], w["L0_ffn_Wr"].rearrange("(g p) n -> p g n", p=P)).then_inc(w_in, 16)
                sp.dma_start(bo[:], row(w["L0_xattn_bo"])).then_inc(w_in, 16)
                sp.dma_start(br[:], row(w["L0_ffn_br"])).then_inc(w_in, 16)
            sp.wait_ge(set_up, 3)
            sp.dma_start(k["routed"][NE * REGION:NE * REGION + P, :], k["empty"][:]).then_inc(k["empty_out"], 16)

            def load(jb, step):
                on, a, b, f, c, d, e = at(jb, step)
                if "d" in on:
                    if since(d, 1):
                        sp.wait_ge(pv_done, d)
                    sp.dma_start(vP[:].rearrange("c q h a d -> c q (h a d)"),
                                 k["vP"].rearrange("(m q) c x -> m c q x", q=2)[bass.ds(d - M * late(jb, d), 1)].rearrange("m c q x -> c (m q) x")).then_inc(v_in, 16)
                if "a" in on:
                    for h in range(2):
                        if isinstance(a, int) and a == M + h:
                            store_o(sp, s, k, 1, s["vo"], h)
                        if isinstance(a, int) and a == M + h * (M // 2):
                            sp.wait_ge(s["o_out"][h], 32)
                    if since(a, 1):
                        sp.wait_ge(mix_done, a)
                    sp.dma_start(oT[:].rearrange("p g (q t) -> p (g q) t", q=2),
                                 k["o"][late(jb, a), bass.ds(a - M * late(jb, a), 1)].rearrange("m g q p t -> p (m g q) t")).then_inc(o_in, 16)
                if "c" in on:
                    if since(c, 1):
                        sp.wait_ge(score_done, c * HALVES)
                    sp.dma_start(kE[:].rearrange("p q g a c -> p q (g a c)"),
                                 k["kE"].rearrange("(m q) p x -> m p q x", q=2)[bass.ds(c - M * late(jb, c), 1)].rearrange("m p q x -> p (m q) x")).then_inc(k_in, 16)
                if "a" in on:
                    if since(a, 1):
                        sp.wait_ge(xh_done, a)
                    sp.dma_start(xt[:], w["x"].rearrange("(m q) (j p) f -> j m p q f", q=2, p=P)[late(jb, a), bass.ds(a - M * late(jb, a), 1)]
                                 .rearrange("m p q f -> p (m q) f")).then_inc(x_in, 16)

            def load_all(jb, step):
                load(jb, step)
                for e in range(WBUFS - 1):
                    if isinstance(step, int) and step == AGAIN + M + 2 * e:
                        load_expert(sp, w, k, e)

            steps(sp, load_all)
            sp.wait_ge(k["w_in"], 16 * WDMAS * (WBUFS - 1))

        @block.gpsimd
        def _(pool):
            stored(pool)
            nc.gpsimd.memset(k["empty"][:], 0.0).then_inc(set_up, 1)
            nc.gpsimd.memset(x2[:], 0.0).then_inc(set_up, 1)
            pool.wait_ge(set_up, 2)
            nc.gpsimd.memset(k["empty"][:, D:D + 1], float(NTOK)).then_inc(set_up, 1)
            nc.gpsimd.iota(x2[:, :, D:D + 1], [[T, 2], [0, 1]], base=-2 * T, channel_multiplier=1,
                           allow_small_or_imprecise_dtypes=True).then_inc(set_up, 1)
            nc.gpsimd.iota(rank[:], [[0, 2], [-1, NE]], base=NE, channel_multiplier=0,
                           allow_small_or_imprecise_dtypes=True).then_inc(set_up, 1)
            nc.gpsimd.memset(ones[:], 1.0).then_inc(set_up, 1)
            nc.gpsimd.memset(before[:], 1.0).then_inc(set_up, 1)
            nc.gpsimd.iota(total[:, 0], [[REGION // P, NE]], base=0, channel_multiplier=0,
                           allow_small_or_imprecise_dtypes=True).then_inc(set_up, 1)
            pool.wait_ge(set_up, 8)
            nc.gpsimd.affine_select(out=before[:], in_=before[:], compare_op=ALU.is_gt, fill=0.0, base=0,
                                    pattern=[[1, P]], channel_multiplier=-1).then_inc(set_up, 1)

            def send(e):
                pool.wait_ge(pos_out, e + 1)
                pool.wait_ge(number_done, e + 1)
                pool.wait_ge(x2_done, (e + 1) * 2)
                pool.sem_inc(k["carry"], 1)
                for q in range(2):
                    pool.indirect_dma_start(k["routed"], bass.IndirectOffsetOnAxis(ap=pos_i[:, q:q + 1], axis=0), x2[:, q], None).then_inc(row_out, 16)

            def biased(c):
                pool.wait_ge(x1_done, (c + 1) * 2)
                if since(c, 1):
                    pool.wait_ge(r2_done, c)
                nc.gpsimd.tensor_tensor(xb[:], x1[:], bo[:].rearrange("p (o f) -> p o f", o=1).to_broadcast([P, 2, D]), ALU.add).then_inc(xb_done, 1)

            def inverse_rms(a):
                pool.wait_ge(ss_done, (a + 1) * 2)
                nc.gpsimd.tensor_tensor(ms[:], ss[:], k["eps"][:, 0], ALU.add).then_inc(ms_done, 1)
                pool.wait_ge(ms_done, a + 1)
                if since(a, 1):
                    pool.wait_ge(hn_done, a * 2)
                nc.gpsimd.tensor_tensor(rstd[:], ms[:], k["exponent"][:], ALU.pow).then_inc(rstd_done, 1)

            def inverse_std(n, which, mv, mv_done, ve, ve_done, rs, rs_done, norm_done, norms):
                pool.wait_ge(mv_done, (n + 1) * 2)
                nc.gpsimd.tensor_tensor(ve[:], mv[:, :, 1], k["eps"][:, 1], ALU.add).then_inc(ve_done, 1)
                pool.wait_ge(ve_done, n + 1)
                if since(n, 1):
                    pool.wait_ge(norm_done, n * norms)
                nc.gpsimd.tensor_tensor(rs[:], ve[:], k["exponent"][:], ALU.pow).then_inc(rs_done, 1)
                pool.wait_ge(rs_done, n * 3 + 1)
                nc.gpsimd.tensor_tensor(scaled_mean[:, which], mv[:, :, 0], rs[:], ALU.mult).then_inc(rs_done, 1)
                pool.wait_ge(rs_done, n * 3 + 2)
                nc.gpsimd.tensor_tensor(shift[:, which], k["empty"][:, 0:2], scaled_mean[:, which], ALU.subtract).then_inc(rs_done, 1)

            def gated(b):
                for i in range(IC):
                    c = width(i)
                    pool.wait_ge(gate_done, (b * IC + (i + 1)) * 2)
                    nc.gpsimd.tensor_tensor(prod[0:c, i], prod[0:c, i], gate[0:c, i], ALU.mult).then_inc(prod_done, 1)

            def doubled(a):
                pool.wait_ge(h_done, a + 1)
                if since(a, 1):
                    pool.wait_ge(kept_done, a)
                nc.gpsimd.tensor_tensor(xh[:], xt[:], h[:], ALU.add).then_inc(xh_done, 1)

            def step(jb, step):
                on, a, b, f, c, d, e = at(jb, step)
                parts = [(x, z, h) for x in chunks(jb, step) for z in range(R // Q) for h in range(2)]
                full = len(parts) > 4

                def outputs(first, last):
                    for x, z, h in parts[first:last]:
                        read_out(nc, pool, s, 1, s["vo"], x, z, h)

                if full:
                    outputs(0, 2)
                if "e" in on:
                    send(e)
                if full:
                    outputs(2, 3)
                if "f" in on:
                    inverse_std(f, 0, mv, mv_done, ve, ve_done, rs, rs_done, x1_done, 2)
                if "c" in on:
                    biased(c)
                outputs(3 if full else 0, 4 if full else 1)
                if "d" in on:
                    inverse_std(d, 1, mv2, mv2_done, ve2, ve2_done, rs2, rs2_done, x2_done, 2)
                if "a" in on:
                    inverse_rms(a)
                    doubled(a)
                outputs(4 if full else 1, len(parts) - 2)
                if "b" in on:
                    gated(b)
                outputs(len(parts) - 2, len(parts))

            steps(pool, step)
            for x in k["upto"]:
                nc.gpsimd.memset(x[:], 0.0).then_inc(set_up, 1)
            for n, pattern in (("row_start", [[REGION, NE]]), ("full", [[0, NE], [P, TILES]]), ("tile_no", [[1, SLOTS], [0, NE]]),
                               ("tile_row", [[P, SLOTS], [0, NE]])):
                nc.gpsimd.iota(k[n][:], pattern, base=0, channel_multiplier=0, allow_small_or_imprecise_dtypes=True).then_inc(set_up, 1)
            pool.wait_ge(set_up, 9 + 6)
            pool.wait_ge(row_out, 32 * M * JB)
            pool.wait_ge(k["empty_out"], 16)

        @block.vector
        def _(dve):
            for x in (choice, position):
                dve.sem_inc(x, 1)

            def residual(a):
                dve.wait_ge(mix_done, a + 1)
                dve.wait_ge(x_in, a * 16 + 16)
                if since(a, 1):
                    dve.wait_ge(hn_done, a * 2)
                    dve.wait_ge(xh_done, a)
                nc.vector.tensor_tensor(h[:], pm[:], xt[:], ALU.add).then_inc(h_done, 1)

            def statistics(n, r, r_done, st6, st_done, mv, mv_done, rs_done):
                dve.wait_ge(r_done, n + 1)
                for q in range(2):
                    nc.vector.bn_stats(st6[:, q], r[:, q]).then_inc(st_done, 1)
                dve.wait_ge(st_done, (n + 1) * 2)
                if since(n, 1):
                    dve.wait_ge(rs_done, n * 3)
                dve.sem_inc(k["carry"], 1)
                for q in range(2):
                    nc.vector.bn_aggr(mv[:, q], st6[:, q]).then_inc(mv_done, 1)

            def mlp_out(f):
                dve.wait_ge(down_done, (f + 1) * 2)
                dve.wait_ge(kept_done, f + 1)
                if since(f, 1):
                    dve.wait_ge(x1_done, f * 2)
                nc.vector.tensor_tensor(r[:], py[:], kept[:], ALU.add).then_inc(r_done, 1)

            def maximum(c, x):
                dve.wait_ge(score_done, c * HALVES + (x + 1))
                if since(c, 1):
                    dve.wait_ge(exp_done, c * HALVES)
                nc.vector.tensor_reduce(mx[:, x // 2, x % 2 * HG:(x % 2 + 1) * HG].rearrange("p (r x) -> p r x", r=2), scores(x), AX, ALU.max,
                                        negate=True).then_inc(max_done, 1)

            def inverse_sums(n, q):
                dve.wait_ge(exp_done, n * HALVES + 2 * (q + 1))
                if since(n, 1):
                    dve.wait_ge(norm_done, n * 2 + q - 1)
                nc.vector.reciprocal(rc[:, q], sm[:, q]).then_inc(rec_done, 1)

            def normalise(n, q):
                dve.wait_ge(rec_done, n * 2 + (q + 1))
                nc.vector.tensor_tensor(pr[:, q], pr[:, q], rc[:, q].rearrange("p (h o) -> p h o", o=1).to_broadcast([P, H, CTX]),
                                        ALU.mult).then_inc(norm_done, 1)

            def attended(d):
                dve.wait_ge(att_done, d + 1)
                dve.wait_ge(xb_done, d + 1)
                if since(d, 1):
                    dve.wait_ge(x2_done, d * 2)
                nc.vector.tensor_tensor(r2[:], pm[:], xb[:], ALU.add).then_inc(r2_done, 1)

            def number(d):
                if isinstance(d, int) and d == 0:
                    dve.wait_ge(set_up, 9)
                if since(d, 1):
                    dve.wait_ge(row_out, d * 32)
                further = 2 * T + (P - NTOK if isinstance(d, int) and d == M else 0)
                nc.vector.tensor_scalar(x2[:, :, D:D + 1], x2[:, :, D:D + 1], float(further), None, ALU.add).then_inc(number_done, 1)

            def logits(e):
                dve.wait_ge(logit_done, e + 1)
                dve.wait_ge(choice, chose(e))
                nc.vector.tensor_tensor(lg[:], pq[:, :, 0:NE], br[:].rearrange("p (o e) -> p o e", o=1).to_broadcast([P, 2, NE]), ALU.add).then_inc(lg_done, 1)
                dve.wait_ge(lg_done, e + 1)
                nc.vector.tensor_reduce(lmax[:], lg[:], AX, ALU.max).then_inc(choice, 1)
                dve.wait_ge(choice, chose(e, MAX))
                nc.vector.tensor_tensor(best[:], lg[:], lmax[:].rearrange("p (j o) -> p j o", o=1).to_broadcast([P, 2, NE]), ALU.is_ge).then_inc(choice, 1)

            def choose(e):
                dve.wait_ge(choice, chose(e, BEST))
                nc.vector.tensor_tensor(best[:], best[:], rank[:], ALU.mult).then_inc(choice, 1)
                dve.wait_ge(choice, chose(e, TIED))
                nc.vector.tensor_reduce(first[:], best[:], AX, ALU.max).then_inc(choice, 1)
                dve.wait_ge(choice, chose(e, FIRST))
                dve.wait_ge(position, placed(e))
                nc.vector.tensor_tensor(chosen[:], best[:], first[:].rearrange("p (j o) -> p j o", o=1).to_broadcast([P, 2, NE]),
                                        ALU.is_equal).then_inc(choice, 1)
                dve.wait_ge(choice, chose(e, CHOSEN))
                nc.vector.tensor_tensor(total[:, 1], total[:, 0], chosen[:, 0], ALU.add).then_inc(choice, 1)

            def positions(e):
                dve.wait_ge(count_done, e + 1)
                nc.vector.tensor_tensor(place[:], places.rearrange("p (q e) -> p q e", q=2), chosen[:], ALU.mult).then_inc(position, 1)
                nc.vector.tensor_tensor(total[:, 0], total[:, 1], chosen[:, 1], ALU.add).then_inc(position, 1)
                dve.wait_ge(position, placed(e, PLACED))
                nc.vector.tensor_reduce(pos[:], place[:], AX, ALU.add).then_inc(position, 1)
                dve.wait_ge(position, placed(e, SUMMED))
                if since(e, 1):
                    dve.wait_ge(row_out, e * 32)
                nc.vector.tensor_copy(pos_i[:], pos[:]).then_inc(pos_out, 1)

            def step(jb, step):
                on, a, b, f, c, d, e = at(jb, step)
                turns = [(x, u) for x in chunks(jb, step) for u in range(R)]

                def scan(i):
                    if len(turns) < 2 * R:
                        if i % 2 or not turns:
                            return
                        i //= 2
                    x, u = turns[i]
                    scan_step(nc, dve, s, 1, s["vo"], x, u, last=isinstance(x, int) and x == CHUNKS - 1)

                if "d" in on and late(jb, d):
                    normalise(d, 1)
                scan(0)
                if "e" in on:
                    logits(e)
                scan(1)
                if "e" in on:
                    choose(e)
                scan(2)
                scan(3)
                if "e" in on:
                    positions(e)
                if "c" in on:
                    maximum(c, 0)
                scan(4)
                if "c" in on:
                    maximum(c, 1)
                scan(5)
                scan(6)
                if "c" in on:
                    maximum(c, 2)
                scan(7)
                if "c" in on:
                    inverse_sums(c, 0)
                    if late(jb, c):
                        normalise(c, 0)
                if "f" in on:
                    mlp_out(f)
                scan(8)
                if "d" in on:
                    attended(d)
                if "f" in on:
                    statistics(f, r, r_done, st6, st_done, mv, mv_done, rs_done)
                scan(9)
                if "c" in on:
                    maximum(c, 3)
                scan(10)
                if "a" in on:
                    residual(a)
                if "d" in on:
                    statistics(d, r2, r2_done, st62, st2_done, mv2, mv2_done, rs2_done)
                scan(11)
                scan(12)
                if "d" in on:
                    number(d)
                scan(13)
                if "c" in on:
                    inverse_sums(c, 1)
                scan(14)
                scan(15)

            steps(dve, step)

        @block.scalar
        def _(act):
            act.wait_ge(w_in, 16 * NW)
            nc.scalar.activation(n2[:], n2[:], ACT.Copy, scale=float(D) ** 0.5).then_inc(scaled, 1)
            nc.scalar.activation(bq[:], bq[:], ACT.Copy, scale=SCALE).then_inc(scaled, 1)
            act.wait_ge(scaled, 2)

            def probabilities(d, some):
                for j in some:
                    act.wait_ge(PT_done, d * 8 + (j + 1))
                    if since(d, 1):
                        act.wait_ge(pv_done, d)
                    nc.scalar.activation(prT[:, j % 4 * 4:j % 4 * 4 + 4, j // 4 * P:(j // 4 + 1) * P], pP(j), ACT.Copy).then_inc(PT_out, 1)

            def exponential(c, x):
                act.wait_ge(max_done, c * HALVES + (x + 1))
                if since(c, 1):
                    act.wait_ge(PT_done, c * 8)
                    act.wait_ge(rec_done, c * 2)
                for y in range(HG):
                    head = x % 2 * HG + y
                    ins = nc.scalar.activation(pr[:, x // 2, head], scores(x)[:, y // 4, y % 4], ACT.Exp, bias=mx[:, x // 2, head:head + 1],
                                               accum_out=sm[:, x // 2, head:head + 1])
                ins.then_inc(exp_done, 1)

            def normalise(n, q):
                act.wait_ge(rec_done, n * 2 + (q + 1))
                for head in range(H):
                    ins = nc.scalar.activation(pr[:, q, head], pr[:, q, head], ACT.Copy, scale=rc[:, q, head:head + 1])
                ins.then_inc(norm_done, 1)

            def gate_out(b, i):
                c = width(i)
                act.wait_ge(gu_done, b * IC + (i + 1))
                if i == 0 and since(b, 1):
                    act.wait_ge(down_done, b * 2)
                nc.scalar.activation(gate[0:c, i], gu(i)[0:c, 0], ACT.Silu).then_inc(gate_done, 1)
                nc.scalar.activation(prod[0:c, i], gu(i)[0:c, 1], ACT.Copy).then_inc(gate_done, 1)

            def copied(n, done, out, used, dst, src):
                act.wait_ge(done, n + 1)
                if since(n, 1):
                    act.wait_ge(used[0], n * used[1])
                nc.scalar.activation(dst, src, ACT.Copy).then_inc(out, 1)

            def first_norm(f):
                act.wait_ge(rs_done, (f + 1) * 3)
                if since(f, 1):
                    act.wait_ge(x1T_done, f)
                    act.wait_ge(xb_done, f)
                for q in range(2):
                    nc.scalar.activation(x1[:, q], r[:, q], ACT.Identity, bias=shift[:, 0, q:q + 1], scale=rs[:, q:q + 1]).then_inc(x1_done, 1)

            def second_norm(d):
                act.wait_ge(rs2_done, (d + 1) * 3)
                if since(d, 1):
                    act.wait_ge(x2T_done, d)
                    act.wait_ge(row_out, d * 32)
                if isinstance(d, int) and d == 0:
                    act.wait_ge(set_up, 9)
                for q in range(2):
                    nc.scalar.activation(x2[:, q, 0:D], r2[:, q], ACT.Identity, bias=shift[:, 1, q:q + 1], scale=rs2[:, q:q + 1]).then_inc(x2_done, 1)

            def squares(a):
                act.wait_ge(h_done, a + 1)
                if since(a, 1):
                    act.wait_ge(T_done, a)
                for q in range(2):
                    nc.scalar.activation(hn[:, q], h[:, q], ACT.Square, accum_out=ss[:, q:q + 1]).then_inc(ss_done, 1)

            def normed(a):
                act.wait_ge(rstd_done, a + 1)
                for q in range(2):
                    nc.scalar.activation(hn[:, q], h[:, q], ACT.Copy, scale=rstd[:, q:q + 1]).then_inc(hn_done, 1)

            def step(jb, step):
                on, a, b, f, c, d, e = at(jb, step)
                if "c" in on:
                    copied(c, x1T_done, x1T_out, (q_done, 1), x1T[:], pT[:])
                if "d" in on:
                    probabilities(d, (0, 1))
                if "c" in on:
                    act.wait_ge(q_done, c + 1)
                    if since(c, 1):
                        act.wait_ge(score_done, c * HALVES)
                    for g in range(G):
                        nc.scalar.activation(qT[:, g], pq[:, g], ACT.Identity, bias=bq[:, g:g + 1], scale=SCALE).then_inc(q_out, 1)
                if "d" in on:
                    probabilities(d, range(2, 8))
                if "c" in on:
                    exponential(c, 0)
                    exponential(c, 1)
                if "d" in on:
                    copied(d, pv_done, pv_out, (att_done, 1), aT[:], pq[:])
                if "c" in on:
                    exponential(c, 2)
                if "b" in on:
                    act.wait_ge(xh_done, b + 1)
                    if "f" in on or since(f, 1):
                        act.wait_ge(r_done, f + 1 if "f" in on else f)
                    nc.scalar.activation(kept[:], xh[:], ACT.Copy).then_inc(kept_done, 1)
                if "c" in on:
                    if not late(jb, c):
                        normalise(c, 0)
                    exponential(c, 3)
                if "a" in on:
                    squares(a)
                if "b" in on:
                    gate_out(b, 0)
                    gate_out(b, 1)
                if "d" in on:
                    second_norm(d)
                if "a" in on:
                    normed(a)
                if "b" in on:
                    gate_out(b, 2)
                    gate_out(b, 3)
                if "d" in on:
                    copied(d, x2T_done, x2T_out, (logit_done, 1), x2T[:], pT[:])
                if "f" in on:
                    first_norm(f)
                if "b" in on:
                    gate_out(b, 4)
                    gate_out(b, 5)
                if "a" in on:
                    act.wait_ge(T_done, a + 1)
                    if "b" in on or since(b, 1):
                        act.wait_ge(gu_done, (b + 1 if "b" in on else b) * IC)
                    for g in range(G):
                        nc.scalar.activation(hT[:, g], pm[:, g], ACT.Copy, scale=n2[:, g:g + 1]).then_inc(hT_done, 1)
                if "c" in on and not late(jb, c):
                    normalise(c, 1)

            steps(act, step)

        @block.tensor
        def _(pe):
            pe.wait_ge(w_in, 16 * NW)
            pe.wait_ge(set_up, 9)

            def transposed(dst, src, done):
                for q in range(2):
                    for g in range(G):
                        ins = nc.tensor.transpose(dst[:, g, q * P:(q + 1) * P], src[:, q, g * P:(g + 1) * P], ident[:])
                ins.then_inc(done, 1)

            def by_rows(dst, rows, wt, done):
                for q in range(2):
                    for g in range(G):
                        ins = nc.tensor.matmul(dst[:, q], rows[:, g, q * P:(q + 1) * P], wt[:, g], start=(g == 0), stop=(g == G - 1))
                ins.then_inc(done, 1)

            def gate_up(b, i):
                c = width(i)
                if i == 0:
                    pe.wait_ge(hT_done, (b + 1) * G)
                if i == 4:
                    pe.wait_ge(gate_done, (b * IC + 2) * 2)
                for which, wt in enumerate((wg, wu)):
                    for g in range(G):
                        ins = nc.tensor.matmul(gu(i)[0:c, which], wt[:, g, i * P:i * P + c], hT[:, g], start=(g == 0), stop=(g == G - 1))
                ins.then_inc(gu_done, 1)

            def down(f, q):
                if q == 0:
                    pe.wait_ge(prod_done, (f + 1) * IC)
                    if since(f, 1):
                        pe.wait_ge(r_done, f)
                for i in range(IC):
                    c = width(i)
                    ins = nc.tensor.matmul(py[:, q], prod[0:c, i, q * P:(q + 1) * P], wd[0:c, i], start=(i == 0), stop=(i == IC - 1))
                ins.then_inc(down_done, 1)

            def queries(c):
                pe.wait_ge(x1T_out, c + 1)
                for go in range(G):
                    for g in range(G):
                        ins = nc.tensor.matmul(pq[:, go], wq[:, g, go * P:(go + 1) * P], x1T[:, g], start=(g == 0), stop=(g == G - 1))
                ins.then_inc(q_done, 1)

            def score(c, x):
                q = x // 2
                if x == 0:
                    pe.wait_ge(q_out, (c + 1) * G)
                    pe.wait_ge(k_in, c * 16 + 16)
                if x >= 2:
                    pe.wait_ge(exp_done, c * HALVES + (x - 1))
                for g in range(G):
                    for i in range(2):
                        group = x % 2 * 2 + i
                        rows = slice(32 * group, 32 * group + 32)
                        ins = nc.tensor.matmul(pX[:, x % 2, i, g * 2 * CTX:(g + 1) * 2 * CTX], qT[rows, g, q * P:(q + 1) * P],
                                               kE[rows, q, g].rearrange("p a c -> p (a c)"), start=True, stop=True)
                ins.then_inc(score_done, 1)

            def probabilities(d, some):
                for j in some:
                    q, x = j // 4, j % 4
                    if x == 0:
                        pe.wait_ge(norm_done, d * 2 + (q + 1))
                    if j >= 4:
                        pe.wait_ge(PT_out, d * 8 + (j - 3))
                    for y in range(4):
                        ins = nc.tensor.transpose(pP(j)[:, y], pr[:, q, x * 4 + y], ident[:])
                    ins.then_inc(PT_done, 1)

            def values(d):
                pe.wait_ge(PT_out, (d + 1) * 8)
                pe.wait_ge(v_in, d * 16 + 16)
                for q in range(2):
                    for group in range(4):
                        for g in range(G):
                            for p in range(2):
                                ins = nc.tensor.matmul(pq[32 * group:32 * group + 32, g, q * P:(q + 1) * P], vP[:, q, g * 4 + group, p],
                                                       prT[:, group * 4 + g * 2 + p, q * P:(q + 1) * P], start=(p == 0), stop=(p == 1))
                ins.then_inc(pv_done, 1)

            def count(e):
                pe.wait_ge(choice, chose(e, COUNTED))
                nc.tensor.matmul(places, before[:], chosen[:].rearrange("p q e -> p (q e)"), start=True, stop=False)
                nc.tensor.matmul(places, ones[:], total[:].rearrange("p q e -> p (q e)"), start=False, stop=True).then_inc(count_done, 1)

            def routed(d):
                pe.wait_ge(x2T_out, d + 1)
                for q in range(2):
                    for g in range(G):
                        ins = nc.tensor.matmul(pq[:, q, 0:NE], x2T[:, g, q * P:(q + 1) * P], wr[:, g], start=(g == 0), stop=(g == G - 1))
                ins.then_inc(logit_done, 1)

            def step(jb, step):
                on, a, b, f, c, d, e = at(jb, step)
                if "c" in on:
                    pe.wait_ge(x1_done, (c + 1) * 2)
                    if since(c, 1):
                        pe.wait_ge(x1T_out, c)
                    if since(d, 1):
                        pe.wait_ge(x2T_out, d)
                    pe.wait_ge(position, placed(e))
                    transposed(pT, x1, x1T_done)
                if "c" in on or "d" in on or "b" in on:
                    if since(b, 1):
                        pe.wait_ge(gate_done, b * (2 * IC))
                    if since(c, 1):
                        pe.wait_ge(exp_done, c * HALVES)
                    if since(d, 1):
                        pe.wait_ge(PT_out, d * 8)
                if "d" in on:
                    probabilities(d, (0, 1))
                if since(d, 1) and ("c" in on or "d" in on):
                    pe.wait_ge(lg_done, d)
                if "c" in on:
                    queries(c)
                if "d" in on:
                    probabilities(d, range(2, 6))
                if "e" in on and "d" in on:
                    if "c" in on:
                        pe.wait_ge(x1T_out, c + 1)
                    pe.wait_ge(x2T_out, e + 1)
                    count(e)
                if "d" in on:
                    probabilities(d, range(6, 8))
                if "c" in on:
                    if "d" in on:
                        pe.wait_ge(PT_out, d * 8 + 6)
                    score(c, 0)
                    if "d" in on:
                        pe.wait_ge(PT_out, d * 8 + 8)
                    score(c, 1)
                if "f" in on:
                    down(f, 0)
                if "d" in on:
                    values(d)
                if "c" in on:
                    score(c, 2)
                if "f" in on:
                    down(f, 1)
                if since(a, 1) and ("d" in on or "a" in on):
                    pe.wait_ge(hT_done, a * G)
                if "d" in on:
                    pe.wait_ge(pv_out, d + 1)
                    by_rows(pm, aT, wo, att_done)
                if "c" in on:
                    score(c, 3)
                if "a" in on:
                    pe.wait_ge(o_in, a * 16 + 16)
                    if "d" in on or since(d, 1):
                        pe.wait_ge(r2_done, d + 1 if "d" in on else d)
                    by_rows(pm, oT, w_mix, mix_done)
                if "e" in on and "d" not in on:
                    pe.wait_ge(x2T_out, e + 1)
                    count(e)
                if "b" in on:
                    for some in ((0, 1), (2, 3)):
                        if "c" in on:
                            pe.wait_ge(exp_done, c * HALVES + (some[0] // 2 + 3))
                        elif "d" in on:
                            pe.wait_ge(PT_out, d * 8 + 8)
                        for i in some:
                            gate_up(b, i)
                if "d" in on:
                    pe.wait_ge(x2_done, (d + 1) * 2)
                    pe.wait_ge(x1T_out, c + 1 if "c" in on else c)
                    pe.wait_ge(position, placed(e, PLACED) if "e" in on else placed(e))
                    transposed(pT, x2, x2T_done)
                if "a" in on:
                    pe.wait_ge(hn_done, (a + 1) * 2)
                    transposed(pm, hn, T_done)
                if "b" in on:
                    gate_up(b, 4)
                    gate_up(b, 5)
                if "d" in on:
                    routed(d)

            steps(pe, step)


def load_expert(sp, w, k, e):
    wt, w_in = k["wt"], k["w_in"]
    C1, C2 = F1 // P, F2 // P
    at = lambda part, first, n: wt[:, e % WBUFS * WROW + WPARTS[part] + first:e % WBUFS * WROW + WPARTS[part] + first + n]
    rows = lambda name, first, n: w["L0_ffn_" + name][e, first * P:(first + n) * P].rearrange("(c p) n -> p c n", p=P)
    pieces = [(at(0, 0, G * F1), rows("W1", 0, G), G)]
    pieces += [(at(1, c * F2, C1 // 2 * F2), rows("W2", c, C1 // 2), C1 // 2) for c in (0, C1 // 2)]
    pieces += [(at(2, 0, C2 * D), rows("W3", 0, C2), C2)]
    pieces += [(at(3 + i, 0, n), row(w["L0_ffn_" + name][e]), None) for i, (name, n) in enumerate((("b1", F1), ("b2", F2), ("b3", D)))]
    assert len(pieces) == WDMAS
    for i, (dst, src, c) in enumerate(pieces):
        if e * WDMAS + i:
            sp.wait_ge(w_in, 16 * (e * WDMAS + i))
        sp.dma_start(dst if c is None else dst.rearrange("p (c n) -> p c n", c=c), src).then_inc(w_in, 16)


def dispatch(nc, sem, w, k):
    total, ones = k["total"], k["ones"]
    row_start, full, upto, tile_no, tile_row = (k[n] for n in ("row_start", "full", "upto", "tile_no", "tile_row"))
    EMPTY = NE * REGION
    with ExitStack() as ctx:
        sb = lambda n, s, d=F32: ctx.enter_context(nc.sbuf_tensor("d_" + n, s, d))
        sums = ctx.enter_context(nc.psum_tensor("d_sums", [P, NE], F32))
        row_end = sb("row_end", [P, NE], I32)
        tokens = sb("tokens", [P, NE])
        needs = sb("needs", [P, NE, TILES])
        used = sb("used", [P, NE])
        start, first_row = sb("start", [P, NE]), sb("first_row", [P, NE])
        begun, passed = sb("begun", [P, SLOTS, NE]), sb("passed", [P, SLOTS, NE])
        at = sb("at", [P, SLOTS])
        expert = sb("expert", [P, SLOTS])
        turn = sb("turn", [P, 2, SLOTS])
        counted, ends, tables = (sem("d_" + n) for n in ("counted", "ends", "tables"))
        block = ctx.enter_context(nc.Block())

        def close(eng, some):
            eng.wait_ge(ends, 2)
            for e in some:
                after = eng.value_load(row_end[0:1, e:e + 1], min_val=0, max_val=NE * REGION - P)
                eng.dma_start(k["routed"][bass.ds(after, P), :], k["empty"][:]).then_inc(k["empty_out"], 16)

        @block.sync
        def _(sp):
            close(sp, range(0, NE // 2))
            sp.wait_ge(k["empty_out"], 16 * (1 + NE))

        @block.scalar
        def _(act):
            close(act, range(NE // 2, NE))

        @block.tensor
        def _(pe):
            nc.tensor.matmul(sums[:], ones[:], total[:, 0], start=True, stop=True).then_inc(counted, 1)

        @block.vector
        def _(dve):
            over = lambda x: x.rearrange("p (o e) -> p o e", o=1).to_broadcast([P, SLOTS, NE])
            dve.wait_ge(counted, 1)
            nc.vector.tensor_copy(row_end[:], sums[:]).then_inc(ends, 1)
            nc.vector.tensor_tensor(tokens[:], sums[:], row_start[:], ALU.subtract).then_inc(ends, 1)
            dve.wait_ge(ends, 2)
            nc.vector.tensor_tensor(needs[:], tokens[:].rearrange("p (e o) -> p e o", o=1).to_broadcast([P, NE, TILES]), full[:],
                                    ALU.is_gt).then_inc(tables, 1)
            dve.wait_ge(tables, 1)
            nc.vector.tensor_reduce(used[:], needs[:], AX, ALU.add).then_inc(tables, 1)
            dve.wait_ge(tables, 2)
            nc.vector.tensor_copy(upto[0][:, NE:], used[:]).then_inc(tables, 1)
            m, d = 3, 1
            while d < NE:
                dve.wait_ge(tables, m)
                src, dst = upto[(m - 3) % 2], upto[(m - 2) % 2]
                nc.vector.tensor_tensor(dst[:, NE:], src[:, NE:], src[:, NE - d:2 * NE - d], ALU.add).then_inc(tables, 1)
                m, d = m + 1, 2 * d
            end = upto[(m - 3) % 2][:, NE:]
            dve.wait_ge(tables, m)
            nc.vector.tensor_tensor(start[:], end, used[:], ALU.subtract).then_inc(tables, 1)
            nc.vector.tensor_tensor(passed[:], tile_no[:], over(end), ALU.is_ge).then_inc(tables, 1)
            dve.wait_ge(tables, m + 2)
            nc.vector.tensor_tensor(begun[:], tile_no[:], over(start[:]), ALU.is_ge).then_inc(tables, 1)
            nc.vector.tensor_scalar(first_row[:], start[:], float(P), float(EMPTY), ALU.mult, ALU.add).then_inc(tables, 1)
            nc.vector.tensor_reduce(expert[:], passed[:], AX, ALU.add).then_inc(tables, 1)
            dve.wait_ge(tables, m + 5)
            nc.vector.tensor_tensor(first_row[:], row_start[:], first_row[:], ALU.subtract).then_inc(tables, 1)
            nc.vector.tensor_tensor(begun[:], begun[:], passed[:], ALU.subtract).then_inc(tables, 1)
            nc.vector.tensor_scalar(expert[:], expert[:], NE - 1.0, None, ALU.min).then_inc(tables, 1)
            dve.wait_ge(tables, m + 8)
            nc.vector.tensor_tensor(tile_row[:], tile_row[:], over(first_row[:]), ALU.add).then_inc(tables, 1)
            for i in range(2):
                nc.vector.tensor_scalar(turn[:, i], expert[:], (i + 1.0) * WBUFS, -float(WBUFS), ALU.is_ge, ALU.mult).then_inc(tables, 1)
            dve.wait_ge(tables, m + 11)
            nc.vector.tensor_tensor(tile_row[:], tile_row[:], begun[:], ALU.mult).then_inc(tables, 1)
            nc.vector.tensor_tensor(turn[:, 0], turn[:, 0], turn[:, 1], ALU.add).then_inc(tables, 1)
            dve.wait_ge(tables, m + 13)
            nc.vector.tensor_reduce(at[:], tile_row[:], AX, ALU.add).then_inc(tables, 1)
            nc.vector.tensor_tensor(turn[:, 0], turn[:, 0], expert[:], ALU.add).then_inc(tables, 1)
            dve.wait_ge(tables, m + 15)
            nc.vector.tensor_scalar(k["x_at"][:], at[:], float(EMPTY), None, ALU.add).then_inc(tables, 1)
            nc.vector.tensor_scalar(k["w_at"][:], turn[:, 0], float(WROW), None, ALU.mult).then_inc(tables, 1)
            nc.vector.tensor_scalar(k["w_loads"][:], expert[:], 16.0 * WDMAS, 16.0 * WDMAS, ALU.mult, ALU.add).then_inc(tables, 1)
            nc.vector.tensor_scalar(k["w_free"][:], end, 1.0, None, ALU.add).then_inc(tables, 1)
            dve.wait_ge(tables, m + 19)


def experts(nc, sem, w, k, out):
    ident, wt, w_in = k["ident"], k["wt"], k["w_in"]
    C1, C2, HALF = F1 // P, F2 // P, F1 // 2
    W1_AT, W2_AT, W3_AT, B1_AT, B2_AT, B3_AT = WPARTS
    with ExitStack() as ctx:
        sb = lambda n, s, d=F32: ctx.enter_context(nc.sbuf_tensor("e_" + n, s, d))
        ps = lambda n, s: ctx.enter_context(nc.psum_tensor("e_" + n, s, F32))
        xt = sb("xt", [P, 2, XROW])
        token = sb("token", [P, 2, 1], U32)
        xb = sb("xb", [P, 2, D])
        xT = sb("xT", [P, G, P])
        h1 = sb("h1", [P, 2, HALF])
        g1 = sb("g1", [P, 2, C1 // 2, P])
        h2 = sb("h2", [P, F2])
        g2 = sb("g2", [P, C2, P])
        r = sb("r", [P, D])
        st6 = sb("st6", [P, 6])
        mv = sb("mv", [P, 2])
        ve, rs = sb("ve", [P, 1]), sb("rs", [P, 1])
        y = sb("y", [P, 2, D])
        pX = ps("pX", [P, G, P])
        ph1 = ps("ph1", [P, 2, HALF])
        pT1 = ps("pT1", [P, 2, C1 // 2, P])
        ph2 = ps("ph2", [P, F2])
        pT2 = ps("pT2", [P, C2, P])
        py = ps("py", [P, D])
        names = ("xT_done", "xT_out", "token_kept", "xb_done", "h1_done", "h1_out", "T1_done", "g1_done", "h2_done",
                 "h2_out", "T2_done", "g2_done", "y_done", "r_done", "st_done", "mv_done", "ve_done", "rs_done", "row_done")
        (xT_done, xT_out, token_kept, xb_done, h1_done, h1_out, T1_done, g1_done, h2_done, h2_out, T2_done, g2_done,
         y_done, r_done, st_done, mv_done, ve_done, rs_done, row_done) = (sem("e_" + n) for n in names)
        x_in, row_out = ([sem(f"e_{n}{s}") for s in range(2)] for n in ("x_in", "row_out"))
        block = ctx.enter_context(nc.Block())

        def entry(eng, table, n, top):
            return eng.value_load(k[table][0:1, bass.ds(n, 1)], min_val=0, max_val=top)

        def weights(eng, n):
            return entry(eng, "w_at", n, (WBUFS - 1) * WROW)

        def loads(eng, n):
            return entry(eng, "w_loads", n, 16 * WDMAS * NE)

        @block.sync
        def _(sp):
            for s in range(2):
                sp.wait_ge(x_in[s], 16)
            for e in range(WBUFS - 1, NE):
                if e >= WBUFS:
                    sp.wait_ge(r_done, entry(sp, "w_free", e - WBUFS, SLOTS + 1))
                load_expert(sp, w, k, e)
            sp.wait_ge(w_in, 16 * WDMAS * NE)

        @block.gpsimd
        def _(pool):
            def step(a, b):
                if a:
                    n, s, m = a
                    at = weights(pool, n)
                    pool.wait_ge(w_in, loads(pool, n))
                    pool.wait_ge(x_in[s], m * 16 + 16)
                    if since(n, 2):
                        pool.wait_ge(r_done, n)
                    pool.sem_inc(k["carry"], 1)
                    nc.gpsimd.tensor_tensor(xb[:, s], xt[:, s, 0:D], wt[:, bass.ds(at + B3_AT, D)], ALU.add).then_inc(xb_done, 1)
                if b:
                    n, s, m = b
                    pool.wait_ge(mv_done, n + 1)
                    nc.gpsimd.tensor_tensor(ve[:], mv[:, 1:2], k["eps"][:, 1, 0:1], ALU.add).then_inc(ve_done, 1)
                    pool.wait_ge(ve_done, n + 1)
                    nc.gpsimd.tensor_tensor(rs[:], ve[:], k["exponent"][:, 0:1], ALU.pow).then_inc(rs_done, 1)
                    pool.wait_ge(row_done, n + 1)
                    pool.sem_inc(k["carry"], 1)
                    pool.indirect_dma_start(out.rearrange("b t f -> (b t) f"), bass.IndirectOffsetOnAxis(ap=token[:, s], axis=0),
                                            y[:, s], None, bounds_check=NTOK - 1, oob_is_err=False).then_inc(row_out[s], 16)

            pipeline(pool, SLOTS, 2, step)
            for s in range(2):
                pool.wait_ge(row_out[s], 16 * len(range(s, SLOTS, 2)))

        @block.vector
        def _(dve):
            dve.sem_inc(r_done, 1)

            def step(a, b):
                if a:
                    n, s, m = a
                    dve.wait_ge(x_in[s], m * 16 + 16)
                    if since(n, 2):
                        dve.wait_ge(row_out[s], m * 16)
                    nc.vector.tensor_copy(token[:, s], xt[:, s, D:D + 1]).then_inc(token_kept, 1)
                    dve.wait_ge(xT_done, n + 1)
                    if since(n, 1):
                        dve.wait_ge(h1_done, n * 2)
                    nc.vector.tensor_copy(xT[:], pX[:]).then_inc(xT_out, 1)
                if b:
                    n, s, m = b
                    at = weights(dve, n)
                    dve.wait_ge(h2_done, n + 1)
                    if since(n, 1):
                        dve.wait_ge(T2_done, n)
                    nc.vector.tensor_tensor(h2[:], ph2[:], wt[:, bass.ds(at + B2_AT, F2)], ALU.add).then_inc(h2_out, 1)
                if a:
                    n, s, m = a
                    at = weights(dve, n)
                    for q in range(2):
                        dve.wait_ge(h1_done, n * 2 + q + 1)
                        if since(n, 1):
                            dve.wait_ge(T1_done, n * 2 + q - 1)
                        nc.vector.tensor_tensor(h1[:, q], ph1[:, q], wt[:, bass.ds(at + (B1_AT + q * HALF), HALF)], ALU.add).then_inc(h1_out, 1)
                if b:
                    n, s, m = b
                    dve.wait_ge(y_done, n + 1)
                    dve.wait_ge(xb_done, n + 1)
                    nc.vector.tensor_tensor(r[:], py[:], xb[:, s], ALU.add).then_inc(r_done, 1)
                    dve.wait_ge(r_done, n + 2)
                    nc.vector.bn_stats(st6[:], r[:]).then_inc(st_done, 1)
                    dve.wait_ge(st_done, n + 1)
                    dve.sem_inc(k["carry"], 1)
                    nc.vector.bn_aggr(mv[:], st6[:]).then_inc(mv_done, 1)
                    dve.wait_ge(rs_done, n + 1)
                    nc.vector.tensor_scalar(y[:, s], r[:], mv[:, 0:1], rs[:, 0:1], ALU.subtract, ALU.mult).then_inc(row_done, 1)

            pipeline(dve, SLOTS, 2, step)

        @block.scalar
        def _(act):
            def load(n, s):
                at = entry(act, "x_at", n, NE * REGION)
                act.dma_start(xt[:, s], k["routed"][bass.ds(at, P), :]).then_inc(x_in[s], 16)

            for n in range(2):
                load(n, n)

            def step(a, b):
                if b:
                    n, s, m = b
                    act.wait_ge(T2_done, n + 1)
                    if since(n, 1):
                        act.wait_ge(y_done, n)
                    nc.scalar.activation(g2[:], pT2[:], ACT.Gelu).then_inc(g2_done, 1)
                if a:
                    n, s, m = a
                    for q in range(2):
                        act.wait_ge(T1_done, n * 2 + q + 1)
                        if since(n, 1):
                            act.wait_ge(h2_done, n)
                        nc.scalar.activation(g1[:, q], pT1[:, q], ACT.Gelu).then_inc(g1_done, 1)
                    if not (isinstance(n, int) and n >= SLOTS - 2):
                        act.wait_ge(xT_done, n + 1)
                        act.wait_ge(xb_done, n + 1)
                        act.wait_ge(token_kept, n + 1)
                        load(n + 2, s)

            pipeline(act, SLOTS, 2, step, after=2)

        @block.tensor
        def _(pe):
            def step(a, b):
                if a:
                    n, s, m = a
                    pe.wait_ge(x_in[s], m * 16 + 16)
                    if since(n, 1):
                        pe.wait_ge(xT_out, n)
                    for g in range(G):
                        ins = nc.tensor.transpose(pX[:, g], xt[:, s, g * P:(g + 1) * P], ident[:])
                    ins.then_inc(xT_done, 1)
                if b:
                    n, s, m = b
                    at_b = weights(pe, n)
                    if since(n, 1):
                        pe.wait_ge(h2_out, n)
                    for c in range(C1):
                        pe.wait_ge(g1_done, n * 2 + c // (C1 // 2) + 1)
                        ins = nc.tensor.matmul(ph2[:], g1[:, c // (C1 // 2), c % (C1 // 2)], wt[:, bass.ds(at_b + (W2_AT + c * F2), F2)],
                                               start=(c == 0), stop=(c == C1 - 1))
                    ins.then_inc(h2_done, 1)
                if a:
                    n, s, m = a
                    at_a = weights(pe, n)
                    pe.wait_ge(w_in, loads(pe, n))
                    pe.wait_ge(xT_out, n + 1)
                    first_layer(n, at_a, 0)
                if b:
                    n, s, m = b
                    pe.wait_ge(h2_out, n + 1)
                    if since(n, 1):
                        pe.wait_ge(g2_done, n)
                    for c in range(C2):
                        ins = nc.tensor.transpose(pT2[:, c], h2[:, c * P:(c + 1) * P], ident[:])
                    ins.then_inc(T2_done, 1)
                if a:
                    n, s, m = a
                    first_layer(n, at_a, 1)
                if a:
                    transposed(a, 0)
                if b:
                    n, s, m = b
                    pe.wait_ge(g2_done, n + 1)
                    if since(n, 1):
                        pe.wait_ge(r_done, n + 1)
                    for c in range(C2):
                        ins = nc.tensor.matmul(py[:], g2[:, c], wt[:, bass.ds(at_b + (W3_AT + c * D), D)], start=(c == 0), stop=(c == C2 - 1))
                    ins.then_inc(y_done, 1)
                if a:
                    transposed(a, 1)

            def first_layer(n, at, q):
                if since(n, 1):
                    pe.wait_ge(h1_out, n * 2 + q - 1)
                for g in range(G):
                    ins = nc.tensor.matmul(ph1[:, q], xT[:, g], wt[:, bass.ds(at + (W1_AT + g * F1 + q * HALF), HALF)],
                                           start=(g == 0), stop=(g == G - 1))
                ins.then_inc(h1_done, 1)

            def transposed(a, q):
                n, s, m = a
                pe.wait_ge(h1_out, n * 2 + q + 1)
                if since(n, 1):
                    pe.wait_ge(g1_done, n * 2 + q - 1)
                for c in range(C1 // 2):
                    ins = nc.tensor.transpose(pT1[:, q, c], h1[:, q, c * P:(c + 1) * P], ident[:])
                ins.then_inc(T1_done, 1)

            pipeline(pe, SLOTS, 2, step)


INPUTS = ["x", "ctx_1024", "L0_attn_norm1_w", "L0_attn_norm2_w", "L0_attn_conv_w", "L0_attn_conv_b", "L0_attn_wq",
          "L0_attn_wk", "L0_attn_wv", "L0_attn_wb", "L0_attn_wa", "L0_attn_wo", "L0_attn_wg", "L0_attn_wu", "L0_attn_wd",
          "L0_xattn_Wq", "L0_xattn_bq", "L0_xattn_Wk", "L0_xattn_bk", "L0_xattn_Wv", "L0_xattn_bv", "L0_xattn_Wo",
          "L0_xattn_bo", "L0_ffn_Wr", "L0_ffn_br", "L0_ffn_W1", "L0_ffn_b1", "L0_ffn_W2", "L0_ffn_b2", "L0_ffn_W3",
          "L0_ffn_b3"]


def build(nc, w, out):
    k = {
        "qkv": nc.dram_tensor("qkv", (JB, 3, NB // 2, G, 2, P, TB), F32, kind="Internal").ap(),
        "gates": nc.dram_tensor("gates", (JB, 2, NB // 2, G, 2, H // G, TB), F32, kind="Internal").ap(),
        "o": nc.dram_tensor("o", (JB, NB // 2, G, 2, P, TB), F32, kind="Internal").ap(),
        "kE": nc.dram_tensor("kE", (NB, P, G * 2 * CTX), F32, kind="Internal").ap(),
        "vP": nc.dram_tensor("vP", (NB, CTX, H * 2 * HD), F32, kind="Internal").ap(),
        "routed": nc.dram_tensor("routed", (NE * REGION + P, XROW), F32, kind="Internal").ap(),
    }
    with ExitStack() as ctx:
        sb = lambda n, s, d=F32: ctx.enter_context(nc.sbuf_tensor(n, s, d))
        sem = lambda n: ctx.enter_context(nc.semaphore(n))
        k["ident"] = sb("ident", [P, P])
        k["exponent"] = sb("exponent", [P, 2])
        k["eps"] = sb("eps", [P, 2, 2])
        k["empty"] = sb("empty", [P, XROW])
        k["before"] = sb("before", [P, P])
        k["ones"] = sb("ones", [P, P])
        k["total"] = sb("total", [P, 2, NE])
        k["wt"] = sb("wt", [P, WBUFS * WROW])
        k["w_in"], k["empty_out"] = sem("w_in"), sem("empty_out")
        k["carry"] = sem("carry")
        taken = [0]

        def arena(n):
            taken[0] += n
            return k["wt"][:, taken[0] - n:taken[0]]

        s = scan_state(arena, sem)
        assert taken[0] >= (WBUFS - 1) * WROW
        scan_end = taken[0]
        front_and_scan(nc, sem, w, k, s, arena)
        taken[0] = scan_end
        k["row_start"] = sb("row_start", [P, NE])
        k["full"] = sb("full", [P, NE, TILES])
        k["upto"] = [sb(f"upto{i}", [P, NE + NE]) for i in range(2)]
        k["tile_no"], k["tile_row"] = sb("tile_no", [P, SLOTS, NE]), sb("tile_row", [P, SLOTS, NE])
        scan_and_post(nc, sem, w, k, s, arena)
        for n, width in (("x_at", SLOTS), ("w_at", SLOTS), ("w_loads", SLOTS), ("w_free", NE)):
            k[n] = sb(n, [P, width], I32)
        dispatch(nc, sem, w, k)
        experts(nc, sem, w, k, out)


def kernel(**inputs):
    import numpy as np
    import concourse.bacc as bacc
    from concourse.bass_utils import run_bass_kernel_spmd as run

    nc = bacc.Bacc("TRN2", target_bir_lowering=False, num_devices=1)
    arrays, w = {}, {}
    for name in INPUTS:
        arrays[f"in_{name}"] = np.ascontiguousarray(inputs[name])
        w[name] = nc.dram_tensor(f"in_{name}", arrays[f"in_{name}"].shape, F32, kind="ExternalInput").ap()
    out = nc.dram_tensor("out_0", (NB, T, D), F32, kind="ExternalOutput").ap()
    build(nc, w, out)
    return run(nc, [arrays], core_ids=[0]).results[0]["out_0"]
```
